# Optimizing a Trainium2 kernel written in Bass

```python
import numpy as np
import jax
import jax.numpy as jnp

def _softmax(x, axis=-1):
    return jax.nn.softmax(x, axis=axis)

def _gelu(x):
    return jax.nn.gelu(x, approximate=True)

def _silu(x):
    return jax.nn.silu(x)

def _sigmoid(x):
    return jax.nn.sigmoid(x)

def _layernorm(x, axis=-1, eps=1e-05):
    m = jnp.mean(x, axis=axis, keepdims=True)
    v = jnp.var(x, axis=axis, keepdims=True)
    return (x - m) / jnp.sqrt(v + eps)

def _scatter_add(tgt, idx, src, axis=0):
    return tgt.at[idx].add(src)

def _segment_sum(src, seg, n):
    return jax.ops.segment_sum(src, seg, n)
kernel_name = 'mk_hybrid_d1_jaxref_r8_17b80a'

def setup_inputs(seed: int=0):
    np.random.seed(seed)
    _w = jnp.asarray

    def _L0_attn_a_setup():
        import jax, jax.numpy as jnp
        import numpy as np
        D_MODEL, D_STATE, D_CONV, EXPAND = (128, 16, 4, 2)
        D_INNER = D_MODEL * EXPAND
        BATCH, SEQ = (2, 256)

        def _layernorm(x, w, b, eps=1e-05):
            mu = jnp.mean(x, axis=-1, keepdims=True)
            var = jnp.var(x, axis=-1, keepdims=True)
            return (x - mu) * jax.lax.rsqrt(var + eps) * w + b

        def _causal_depthwise_conv(x, w, b):
            K = w.shape[1]
            xp = jnp.pad(x, ((0, 0), (K - 1, 0), (0, 0)))
            L = x.shape[1]
            out = b
            for k in range(K):
                out = out + xp[:, k:k + L, :] * w[:, k]
            return out
        key = jax.random.key(seed)
        ks = jax.random.split(key, 10)
        s = lambda d: 1.0 / np.sqrt(d)
        return {'x': jax.random.normal(ks[0], (BATCH, SEQ, D_MODEL), jnp.float32), 'norm_w': jnp.ones((D_MODEL,), jnp.float32), 'norm_b': jnp.zeros((D_MODEL,), jnp.float32), 'W_in': jax.random.normal(ks[1], (2 * D_INNER, D_MODEL), jnp.float32) * s(D_MODEL), 'conv_w': jax.random.normal(ks[2], (D_INNER, D_CONV), jnp.float32) * s(D_CONV), 'conv_b': jnp.zeros((D_INNER,), jnp.float32), 'W_dt': jax.random.normal(ks[3], (D_INNER, D_INNER), jnp.float32) * s(D_INNER), 'b_dt': jnp.zeros((D_INNER,), jnp.float32), 'W_B': jax.random.normal(ks[4], (D_STATE, D_INNER), jnp.float32) * s(D_INNER), 'W_C': jax.random.normal(ks[5], (D_STATE, D_INNER), jnp.float32) * s(D_INNER), 'D': jnp.ones((D_INNER,), jnp.float32), 'A_log': jnp.broadcast_to(jnp.log(jnp.arange(1, D_STATE + 1, dtype=jnp.float32)), (D_INNER, D_STATE)), 'W_out': jax.random.normal(ks[6], (D_MODEL, D_INNER), jnp.float32) * s(D_INNER)}
    _L0_attn_a_in = _L0_attn_a_setup()

    def _L0_attn_b_setup():
        import jax, jax.numpy as jnp
        import numpy as np
        import math
        N_HEAD = 16
        ROPE_BASE = 10000.0

        def _rope_as_in_source(x):
            B, H, T, hd = x.shape
            theta = 1.0 / ROPE_BASE ** (jnp.arange(0, hd, 2, dtype=jnp.float32) / hd)
            ang = jnp.arange(H, dtype=jnp.float32)[:, None] * theta[None, :]
            cos = jnp.cos(ang)[None, :, None, :]
            sin = jnp.sin(ang)[None, :, None, :]
            xr = x.reshape(B, H, T, hd // 2, 2)
            out = jnp.stack([xr[..., 0] * cos - xr[..., 1] * sin, xr[..., 1] * cos + xr[..., 0] * sin], axis=-1)
            return out.reshape(B, H, T, hd)
        key = jax.random.key(seed)
        ks = jax.random.split(key, 5)
        B, T, C = (2, 256, 128)
        s = 0.02
        return {'x': jax.random.normal(ks[0], (B, T, C), dtype=jnp.float32), 'W_attn': jax.random.normal(ks[1], (C, 3 * C), dtype=jnp.float32) * s, 'b_attn': jnp.zeros((3 * C,), dtype=jnp.float32), 'W_proj': jax.random.normal(ks[2], (C, C), dtype=jnp.float32) * s, 'b_proj': jnp.zeros((C,), dtype=jnp.float32)}
    _L0_attn_b_in = _L0_attn_b_setup()

    def _L0_ffn_setup():
        import jax, jax.numpy as jnp
        import numpy as np
        B, T, C = (2, 64, 128)
        I = 512
        E = 8
        K = 2
        key = jax.random.key(seed)
        ks = jax.random.split(key, 8)
        s = 0.02
        return {'x': jax.random.normal(ks[0], (B, T, C), jnp.float32), 'Wr1': jax.random.normal(ks[1], (C, C // 4), jnp.float32) * s, 'br1': jnp.zeros((C // 4,), jnp.float32), 'Wr2': jax.random.normal(ks[2], (C // 4, E), jnp.float32) * s, 'br2': jnp.zeros((E,), jnp.float32), 'Ws1': jax.random.normal(ks[3], (C, I), jnp.float32) * s, 'bs1': jnp.zeros((I,), jnp.float32), 'Ws2': jax.random.normal(ks[4], (I, C), jnp.float32) * s, 'bs2': jnp.zeros((C,), jnp.float32), 'We1': jax.random.normal(ks[5], (E, C, I), jnp.float32) * s, 'be1': jnp.zeros((E, I), jnp.float32), 'We2': jax.random.normal(ks[6], (E, I, C), jnp.float32) * s, 'be2': jnp.zeros((E, C), jnp.float32)}
    _L0_ffn_in = _L0_ffn_setup()
    _d = {'L0_attn_a_x': _L0_attn_a_in['x'], 'L0_attn_a_norm_w': _L0_attn_a_in['norm_w'], 'L0_attn_a_norm_b': _L0_attn_a_in['norm_b'], 'L0_attn_a_W_in': _L0_attn_a_in['W_in'], 'L0_attn_a_conv_w': _L0_attn_a_in['conv_w'], 'L0_attn_a_conv_b': _L0_attn_a_in['conv_b'], 'L0_attn_a_W_dt': _L0_attn_a_in['W_dt'], 'L0_attn_a_b_dt': _L0_attn_a_in['b_dt'], 'L0_attn_a_W_B': _L0_attn_a_in['W_B'], 'L0_attn_a_W_C': _L0_attn_a_in['W_C'], 'L0_attn_a_D': _L0_attn_a_in['D'], 'L0_attn_a_A_log': _L0_attn_a_in['A_log'], 'L0_attn_a_W_out': _L0_attn_a_in['W_out'], 'L0_attn_b_W_attn': _L0_attn_b_in['W_attn'], 'L0_attn_b_b_attn': _L0_attn_b_in['b_attn'], 'L0_attn_b_W_proj': _L0_attn_b_in['W_proj'], 'L0_attn_b_b_proj': _L0_attn_b_in['b_proj'], 'L0_ffn_Wr1': _L0_ffn_in['Wr1'], 'L0_ffn_br1': _L0_ffn_in['br1'], 'L0_ffn_Wr2': _L0_ffn_in['Wr2'], 'L0_ffn_br2': _L0_ffn_in['br2'], 'L0_ffn_Ws1': _L0_ffn_in['Ws1'], 'L0_ffn_bs1': _L0_ffn_in['bs1'], 'L0_ffn_Ws2': _L0_ffn_in['Ws2'], 'L0_ffn_bs2': _L0_ffn_in['bs2'], 'L0_ffn_We1': _L0_ffn_in['We1'], 'L0_ffn_be1': _L0_ffn_in['be1'], 'L0_ffn_We2': _L0_ffn_in['We2'], 'L0_ffn_be2': _L0_ffn_in['be2']}
    _x0 = _d['L0_attn_a_x']
    _d['L0_attn_a_x'] = jax.random.normal(jax.random.fold_in(jax.random.key(seed), 1), (8, 256, 128), dtype=_x0.dtype)
    del _x0
    return _d

def reference(L0_attn_a_x, L0_attn_a_norm_w, L0_attn_a_norm_b, L0_attn_a_W_in, L0_attn_a_conv_w, L0_attn_a_conv_b, L0_attn_a_W_dt, L0_attn_a_b_dt, L0_attn_a_W_B, L0_attn_a_W_C, L0_attn_a_D, L0_attn_a_A_log, L0_attn_a_W_out, L0_attn_b_W_attn, L0_attn_b_b_attn, L0_attn_b_W_proj, L0_attn_b_b_proj, L0_ffn_Wr1, L0_ffn_br1, L0_ffn_Wr2, L0_ffn_br2, L0_ffn_Ws1, L0_ffn_bs1, L0_ffn_Ws2, L0_ffn_bs2, L0_ffn_We1, L0_ffn_be1, L0_ffn_We2, L0_ffn_be2):

    def _L0_attn_a_ref(x, norm_w, norm_b, W_in, conv_w, conv_b, W_dt, b_dt, W_B, W_C, D, A_log, W_out):
        import jax, jax.numpy as jnp
        import numpy as np
        D_MODEL, D_STATE, D_CONV, EXPAND = (128, 16, 4, 2)
        D_INNER = D_MODEL * EXPAND
        BATCH, SEQ = (2, 256)

        def _layernorm(x, w, b, eps=1e-05):
            mu = jnp.mean(x, axis=-1, keepdims=True)
            var = jnp.var(x, axis=-1, keepdims=True)
            return (x - mu) * jax.lax.rsqrt(var + eps) * w + b

        def _causal_depthwise_conv(x, w, b):
            K = w.shape[1]
            xp = jnp.pad(x, ((0, 0), (K - 1, 0), (0, 0)))
            L = x.shape[1]
            out = b
            for k in range(K):
                out = out + xp[:, k:k + L, :] * w[:, k]
            return out
        residual = x
        xn = _layernorm(x, norm_w, norm_b)
        xz = jnp.einsum('bld,ed->ble', xn, W_in)
        x_part, z = jnp.split(xz, 2, axis=-1)
        x_conv = jax.nn.silu(_causal_depthwise_conv(x_part, conv_w, conv_b))
        dt = jax.nn.softplus(jnp.einsum('bld,ed->ble', x_conv, W_dt) + b_dt)
        Bm = jnp.einsum('bld,nd->bln', x_conv, W_B)
        Cm = jnp.einsum('bld,nd->bln', x_conv, W_C)
        A = -jnp.exp(A_log)

        def step(h, inp):
            dt_t, B_t, C_t, xc_t = inp
            h = h * jnp.exp(A[None] * dt_t[:, :, None]) + xc_t[:, :, None] * B_t[:, None, :] * dt_t[:, :, None]
            y_t = jnp.sum(h * C_t[:, None, :], axis=-1)
            return (h, y_t)
        h0 = jnp.zeros((x.shape[0], A.shape[0], A.shape[1]), x_conv.dtype)
        xs = (jnp.swapaxes(dt, 0, 1), jnp.swapaxes(Bm, 0, 1), jnp.swapaxes(Cm, 0, 1), jnp.swapaxes(x_conv, 0, 1))
        _, y = jax.lax.scan(step, h0, xs)
        y = jnp.swapaxes(y, 0, 1)
        y = y + x_conv * D
        y = y * jax.nn.silu(z)
        return residual + jnp.einsum('ble,de->bld', y, W_out)

    def _L0_attn_b_ref(x, W_attn, b_attn, W_proj, b_proj):
        import jax, jax.numpy as jnp
        import numpy as np
        import math
        N_HEAD = 16
        ROPE_BASE = 10000.0

        def _rope_as_in_source(x):
            B, H, T, hd = x.shape
            theta = 1.0 / ROPE_BASE ** (jnp.arange(0, hd, 2, dtype=jnp.float32) / hd)
            ang = jnp.arange(H, dtype=jnp.float32)[:, None] * theta[None, :]
            cos = jnp.cos(ang)[None, :, None, :]
            sin = jnp.sin(ang)[None, :, None, :]
            xr = x.reshape(B, H, T, hd // 2, 2)
            out = jnp.stack([xr[..., 0] * cos - xr[..., 1] * sin, xr[..., 1] * cos + xr[..., 0] * sin], axis=-1)
            return out.reshape(B, H, T, hd)
        B, T, C = x.shape
        H = N_HEAD
        hd = C // H
        qkv = x @ W_attn + b_attn
        q, k, v = jnp.split(qkv, 3, axis=2)
        q = q.reshape(B, T, H, hd).transpose(0, 2, 1, 3)
        k = k.reshape(B, T, H, hd).transpose(0, 2, 1, 3)
        v = v.reshape(B, T, H, hd).transpose(0, 2, 1, 3)
        q = _rope_as_in_source(q)
        k = _rope_as_in_source(k)
        att = jnp.einsum('bhqd,bhkd->bhqk', q, k) * (1.0 / math.sqrt(hd))
        causal = jnp.tril(jnp.ones((T, T), dtype=bool))
        att = jnp.where(causal[None, None, :, :], att, -jnp.inf)
        att = jax.nn.softmax(att, axis=-1)
        y = jnp.einsum('bhqk,bhkd->bhqd', att, v)
        y = y.transpose(0, 2, 1, 3).reshape(B, T, C)
        return y @ W_proj + b_proj

    def _L0_ffn_ref(x, Wr1, br1, Wr2, br2, Ws1, bs1, Ws2, bs2, We1, be1, We2, be2):
        import jax, jax.numpy as jnp
        import numpy as np
        B, T, C = (2, 64, 128)
        I = 512
        E = 8
        K = 2
        Bb, Tt, Cc = x.shape
        xf = x.reshape(-1, Cc)
        logits = jax.nn.relu(xf @ Wr1 + br1) @ Wr2 + br2
        gates = jax.nn.softmax(logits, axis=-1)
        tg, ti = jax.lax.top_k(gates, K)
        tg = jax.nn.softmax(tg / K, axis=-1)
        out = jax.nn.silu(xf @ Ws1 + bs1) @ Ws2 + bs2
        for e in range(E):
            h = jax.nn.silu(xf @ We1[e] + be1[e]) @ We2[e] + be2[e]
            w = jnp.sum(tg * (ti == e), axis=-1)
            out = out + w[:, None] * h
        return out.reshape(Bb, Tt, Cc)
    x = L0_attn_a_x
    x = x + _L0_attn_a_ref(_layernorm(x, axis=-1), L0_attn_a_norm_w, L0_attn_a_norm_b, L0_attn_a_W_in, L0_attn_a_conv_w, L0_attn_a_conv_b, L0_attn_a_W_dt, L0_attn_a_b_dt, L0_attn_a_W_B, L0_attn_a_W_C, L0_attn_a_D, L0_attn_a_A_log, L0_attn_a_W_out)
    x = x + _L0_ffn_ref(_layernorm(x, axis=-1), L0_ffn_Wr1, L0_ffn_br1, L0_ffn_Wr2, L0_ffn_br2, L0_ffn_Ws1, L0_ffn_bs1, L0_ffn_Ws2, L0_ffn_bs2, L0_ffn_We1, L0_ffn_be1, L0_ffn_We2, L0_ffn_be2)
    x = x + _L0_attn_b_ref(_layernorm(x, axis=-1), L0_attn_b_W_attn, L0_attn_b_b_attn, L0_attn_b_W_proj, L0_attn_b_b_proj)
    x = x + _L0_ffn_ref(_layernorm(x, axis=-1), L0_ffn_Wr1, L0_ffn_br1, L0_ffn_Wr2, L0_ffn_br2, L0_ffn_Ws1, L0_ffn_bs1, L0_ffn_Ws2, L0_ffn_bs2, L0_ffn_We1, L0_ffn_be1, L0_ffn_We2, L0_ffn_be2)
    return x

_drawn_inputs = setup_inputs


def setup_inputs(seed=0):
    import zlib

    import numpy as np

    out = dict(_drawn_inputs(seed))
    spreads = {'L0_attn_a_norm_w': (1.0, 0.2),
     'L0_attn_a_norm_b': (0.0, 0.1),
     'L0_attn_a_conv_b': (0.0, 0.1),
     'L0_attn_a_b_dt': (0.0, 0.385),
     'L0_attn_a_D': (1.0, 0.2),
     'L0_attn_b_b_attn': (0.0, 0.8),
     'L0_attn_b_b_proj': (0.0, 0.1),
     'L0_ffn_br1': (0.0, 0.453),
     'L0_ffn_br2': (0.0, 0.1),
     'L0_ffn_bs1': (0.0, 0.374),
     'L0_ffn_bs2': (0.0, 0.1),
     'L0_ffn_be1': (0.0, 0.561),
     'L0_ffn_be2': (0.0, 0.1)}
    factors = {'L0_attn_b_W_attn': 8.0, 'L0_attn_b_W_proj': 4.904}
    for name, (base, spread) in spreads.items():
        noise = np.random.default_rng([zlib.crc32(name.encode()), seed]).standard_normal(out[name].shape)
        drawn = base * np.exp(spread * noise) if base else spread * noise
        out[name] = jnp.asarray(drawn.astype(out[name].dtype))
    for name, factor in factors.items():
        out[name] = (out[name] * factor).astype(out[name].dtype)
    return out
```

```python
from contextlib import ExitStack
import math

import concourse.bass as bass
from concourse import mybir

P = 128
F32 = mybir.dt.float32
BF16 = mybir.dt.bfloat16
U32 = mybir.dt.uint32
ALU = mybir.AluOpType
ACT = mybir.ActivationFunctionType
AX_X = mybir.AxisListType.X


def hybrid_block_kernel(nc, t, out):
    B, S, C = t["L0_attn_a_x"].shape
    T = B * S
    NT = T // P
    NCH, CT = 4, NT // 4
    CW = CT * P
    BPC = CW // S
    DI, NS = t["L0_attn_a_A_log"].shape
    KC = t["L0_attn_a_conv_w"].shape[1]
    NE, _, FI = t["L0_ffn_We1"].shape
    NI = FI // P
    RH = t["L0_ffn_Wr1"].shape[1]
    NH, HD = 16, C // 16
    NG, GH = 4, 4
    QT = S // P
    EPS = 1e-5
    NX = NE + 1
    assert C == P and DI == 2 * P and BPC == 2 and QT == 2 and NG * GH == NH

    with ExitStack() as ctx:
        def sb(name, shape, dt=F32):
            return ctx.enter_context(nc.sbuf_tensor(name, shape, dt))

        def sem(name):
            return ctx.enter_context(nc.semaphore(name))

        bank = [ctx.enter_context(nc.psum_tensor(f"bank{i}", [P, 512], F32)) for i in range(8)]

        X = sb("X", [P, NT, C])
        D = sb("D", [P, NT, C])
        U = sb("U", [P, NT, C])
        SQ = sb("SQ", [P, NT * C])
        xT = SQ
        arena = sb("arena", [P, 4 * 2 * T])
        ident = sb("ident", [P, P])
        identb = sb("identb", [P, P], BF16)
        sel = sb("sel", [P, 2 * NS], BF16)
        cmask = sb("cmask", [P, 512], BF16)
        iota = sb("iota", [P, NE])
        rope = sb("rope", [P, 2, 2 * NH, HD // 2])
        stage = sb("stage", [P, 2, CT, C])
        xnT = sb("xnT", [P, 2, CW])

        st_sum = sb("st_sum", [P, NT])
        st_mean = sb("st_mean", [P, NT])
        st_sd = sb("st_sd", [P, NT])
        st_r = sb("st_r", [P, NT])

        def part(k):
            return arena[:, k * 2 * T:(k + 1) * 2 * T].rearrange("p (h t) -> p h t", h=2)
        xc, zs, dt_, dtx = part(0), part(1), part(2), part(3)
        w_nat = sb("w_nat", [P, 4 * C + 2 * DI + DI + DI])
        win_n = w_nat[:, 0:512].rearrange("p (e d) -> p e d", e=4)
        wdt_n = w_nat[:, 512:1024].rearrange("p (e d) -> p e d", e=2)
        wbc_n = w_nat[:, 1024:1280]
        wout_n = w_nat[:, 1280:1536]
        winT = sb("winT", [P, 4, P])
        wdtT = sb("wdtT", [P, 2, 2, P])
        wboT = sb("wboT", [P, 4, P])
        nw = sb("nw", [P, 1])
        nb = sb("nb", [P, 1])
        cw = sb("cw", [P, 2, KC])
        cb = sb("cb", [P, 2])
        bdt = sb("bdt", [P, 2])
        Dv = sb("Dv", [P, 2])
        Am = sb("Am", [P, 2, NS])
        xpad = sb("xpad", [P, 2, 2, BPC, S + KC - 1])
        conv = sb("conv", [P, 2, 2, CW])
        BCs = sb("BCs", [P, T], BF16)
        bcr = sb("bcr", [P, 2, CW])
        bcm = sb("bcm", [P, 2, CW], BF16)
        NR = 4
        decay = sb("decay", [P, NR, BPC, S])
        xpad_f = xpad[:].rearrange("p s h b t -> p (s h b t)")
        inp = xpad_f[:, 0:NR * CW].rearrange("p (s t) -> p s t", s=NR)
        hst = conv[:].rearrange("p s h t -> p (s h) t")
        Csb = bcr
        ybuf = sb("ybuf", [P, 2, CW])

        w1 = sb("w1", [P, NX, FI])
        w2 = sb("w2", [P, NX, NI, C])
        b1n = sb("b1n", [NX * NI, P])
        b1T = sb("b1T", [P, NX * NI])
        b2r = sb("b2r", [NX, C])
        wr1 = sb("wr1", [P, RH])
        wr2 = sb("wr2", [RH, NE])
        br1 = sb("br1", [RH, 1])
        br2 = sb("br2", [P, NE])
        r1 = ybuf[0:RH, :, :]
        gate = sb("gate", [P, NT, NE])
        gex = sb("gex", [P, NT, NE])
        gmx = sb("gmx", [P, NT])
        gsum = sb("gsum", [P, NT])
        top8 = sb("top8", [P, NT, 8])
        idx8 = sb("idx8", [P, NT, 8], U32)
        idxf = sb("idxf", [P, NT, 2])
        wk = sb("wk", [P, 4, NT])
        pick = sb("pick", [P, 2, NT, NE])
        wts = sb("wts", [P, NT, NX])
        wst = sb("wst", [P, 2, CT, NX])
        wtT = w_nat[0:NX, 0:2 * CW].rearrange("p (s t) -> p s t", s=2)
        acc = bcr[:].rearrange("p s (n c) -> p s n c", c=C)
        hT = arena[:, 8192:12288].rearrange("p (s i t) -> p s i t", s=2, i=NI)

        wat = sb("wat", [P, 3 * C])
        ra = arena[:, 8192:8320].rearrange("p (h i) -> p h i", h=2 * NH)
        rb = arena[:, 8320:8448].rearrange("p (h i) -> p h i", h=2 * NH)
        wqk = sb("wqk", [P, 2 * NH, 32])
        bat = sb("bat", [1, 2 * C])
        bra = arena[0:1, 8448:8576].rearrange("p (h i) -> p h i", h=2 * NH)
        brb = arena[0:1, 8576:8704].rearrange("p (h i) -> p h i", h=2 * NH)
        sel_f = arena[:, 9728:9728 + 2 * NS]
        cmask_f = arena[:, 9760:9760 + P]
        bqk_r = arena[0:1, 8704:9728].rearrange("p (h d) -> p h d", d=32)
        one1 = sb("one1", [1, 1])
        bqk = sb("bqk", [P, 2 * NG])
        bv = sb("bv", [P, C])
        bpj = sb("bpj", [P, C])
        wpj = sb("wpj", [P, C])
        qblk = arena[:, 0:8192].rearrange("p (s g j t) -> p s g j t", s=2, g=NG, j=GH)
        PR = arena[:, 8192:8192 + 3072].rearrange("p (s n) -> p s n", s=2)
        PT = arena[:, 11264:11264 + 3072].rearrange("p (s n) -> p s n", s=2)
        kT = arena[:, 14336:16384].rearrange("p (s g t) -> p s g t", s=2, g=NG)
        va = U[:].rearrange("p n c -> p (n c)").rearrange("p (s q h d) -> p s q h d", s=2, q=QT, h=NH)
        ngm = sb("ngm", [P, 2, QT, GH])
        conv_f = conv[:].rearrange("p s h t -> p (s h t)")
        oT = conv_f[:, 0:2 * S].rearrange("p (s t) -> p s t", s=2)
        rden = sb("rden", [P, 2, QT, GH])
        yat = conv_f[:, 2 * S:4 * S].rearrange("p (s q h d) -> p s q h d", s=2, q=QT, h=NH)
        yT = conv_f[:, 4 * S:6 * S].rearrange("p (s t) -> p s t", s=2)

        ld_x = sem("ld_x")
        ld_a = sem("ld_a")
        ld_f = sem("ld_f")
        ld_b = sem("ld_b")
        n_ld = {"x": 0, "a": 0, "f": 0, "b": 0}
        st_zero = sem("st_zero")
        st_wbc = sem("st_wbc")
        st_tr = sem("st_tr")
        st_cp = sem("st_cp")
        st_const = sem("st_const")
        st_A = sem("st_A")
        st_rope = sem("st_rope")
        st_bq = sem("st_bq")
        st_bqc = sem("st_bqc")
        st_qz = sem("st_qz")
        s_out = sem("s_out")

        def chunk(c, n=CT):
            return bass.ds(c * n, n)

        def cols(c, n=CW):
            return bass.ds(c * n, n)

        def bcast(ap, n):
            return ap.unsqueeze(ap.ndim).broadcast_to(list(ap.shape) + [n])

        act_steps = sem("act_steps")

        def apart(a):
            a.sem_inc(act_steps, 1)

        LN = {k: {q: sem(f"{k}_{q}") for q in ("m", "c", "q", "v", "s", "r")} for k in ("ln0", "ln1", "lnf0", "lnb", "lnf1")}

        def ln_vector(v, k, src, dst):
            s = LN[k]
            nc.vector.tensor_reduce(st_sum[:], src, AX_X, ALU.add).then_inc(s["m"], 1)
            v.wait_ge(s["m"], 1)
            nc.vector.tensor_scalar(st_mean[:], st_sum[:], 1.0 / C, None, ALU.mult).then_inc(s["m"], 1)
            v.wait_ge(s["m"], 2)
            nc.vector.tensor_tensor(dst, src, bcast(st_mean[:], C), ALU.subtract).then_inc(s["c"], 1)
            v.wait_ge(s["q"], 1)
            nc.vector.tensor_reduce(st_sum[:], SQ[:].rearrange("p (n c) -> p n c", c=C), AX_X,
                                    ALU.add).then_inc(s["v"], 1)
            v.wait_ge(s["s"], 1)
            nc.vector.reciprocal(st_r[:], st_sd[:]).then_inc(s["r"], 1)
            v.wait_ge(s["r"], 1)

        def ln_scalar(a, k, src):
            s = LN[k]
            a.wait_ge(s["c"], 1)
            nc.scalar.activation(SQ[:], src[:].rearrange("p n c -> p (n c)"), ACT.Square).then_inc(s["q"], 1)
            a.wait_ge(s["v"], 1)
            nc.scalar.activation(st_sd[:], st_sum[:], ACT.Sqrt, bias=eps_t[:, 0:1], scale=1.0 / C).then_inc(s["s"], 1)

        eps_t = sb("eps_t", [P, 1])
        one_t = sb("one_t", [P, 1])

        m1_st, m1_tr, m1_xn, m1_xz, m1_xe, m1_ze, m1_cd, m1_cv, m1_xc = (
            sem("m1_" + q) for q in ("st", "tr", "xn", "xz", "xe", "ze", "cd", "cv", "xc"))
        m2_mm, m2_ab, m2_ex, m2_re, m2_hi, m2_r, m2_md, m2_st, m2_ln = (
            sem("m2_" + q) for q in ("mm", "ab", "ex", "re", "hi", "r", "md", "st", "ln"))
        m3_dt, m3_dx, m3_a, m3_bb, m3_cb, m3_cs, m3_b, m3_sc, m3_hc, m3_ns, m3_ya, m3_y, m3_o, m3_x = (
            sem("m3_" + q) for q in ("dt", "dx", "a", "bb", "cb", "cs", "b", "sc", "hc", "ns", "ya", "y", "o", "x"))
        FS = [{q: sem(f"f{k}_{q}") for q in ("st", "tr", "xt", "r1", "r1s", "lg", "g", "ga", "ws", "wt", "wc",
                                             "bp", "l1", "h", "l2", "acc", "x")} for k in range(2)]
        AS = {q: sem(f"a_{q}") for q in ("st", "tr", "ln", "q", "k", "v", "ve", "s", "m", "se", "t", "te", "o", "oe",
                                         "ot", "rd", "y", "yt", "ye", "p", "x", "xb")}


        def ffn_scalar(a, k, ln):
            f = FS[k]
            ln_scalar(a, ln, D)
            with a.Fori(0, NCH // 2) as i:
                for s in range(2):
                    c = 2 * i + s
                    a.wait_ge(f["tr"], c + 1 + 2)
                    apart(a)
                    nc.scalar.activation(xT[:, cols(c)], bank[6 + s][:], ACT.Copy).then_inc(f["xt"], 1)
                    a.wait_ge(f["r1"], c + 1)
                    nc.scalar.activation(r1[:, s, :], bank[4 + s][0:RH, :], ACT.Relu,
                                         bias=br1[:, 0:1]).then_inc(f["r1s"], 1)
            a.wait_ge(f["g"], GATE_EXP)
            nc.scalar.activation(gex[:], gex[:], ACT.Exp).then_inc(f["ga"], 1)
            a.wait_ge(f["g"], GATE_DIFF)
            nc.scalar.activation(wk[:, 1, :], wk[:, 0, :], ACT.Exp, scale=1.0 / 2).then_inc(f["ga"], 1)
            with a.Fori(0, NCH // 2) as i:
                for s in range(2):
                    c = 2 * i + s
                    for e in range(NX):
                        a.wait_ge(f["l2"], c * NX + e + 1)
                        for b in range(NI):
                            a.wait_ge(f["l1"], c * NX * NI + e * NI + b + 1)
                            nc.scalar.activation(hT[:, (s + e) % 2, b, :], bank[b][:], ACT.Silu,
                                                 bias=b1T[:, e * NI + b:e * NI + b + 1]).then_inc(f["h"], 1)

        GATE_EXP, GATE_DIFF = 3, 4 + 2 + 2 * NT + 1

        def ffn_vector(v, k, ln):
            f = FS[k]
            ln_vector(v, ln, X[:], D[:])
            with v.Fori(0, NCH // 2) as i:
                for s in range(2):
                    c = 2 * i + s
                    v.wait_ge(f["tr"], c + 1)
                    nc.vector.tensor_tensor(stage[:, s, :, :], D[:, chunk(c), :], bcast(st_r[:, chunk(c)], C),
                                            ALU.mult).then_inc(f["st"], 1)
            g = [0]

            def then(ins):
                ins.then_inc(f["g"], 1)
                g[0] += 1
                v.wait_ge(f["g"], g[0])

            logits = bank[2][:, 0:NT * NE].rearrange("p (n e) -> p n e", e=NE)
            v.wait_ge(f["lg"], NCH)
            then(nc.vector.tensor_tensor(gate[:], logits, br2[:].unsqueeze(1).broadcast_to([P, NT, NE]), ALU.add))
            then(nc.vector.tensor_reduce(gmx[:], gate[:], AX_X, ALU.max))
            then(nc.vector.tensor_tensor(gex[:], gate[:], bcast(gmx[:], NE), ALU.subtract))
            assert g[0] == GATE_EXP
            v.wait_ge(f["ga"], 1)
            then(nc.vector.tensor_reduce(gsum[:], gex[:], AX_X, ALU.add))
            then(nc.vector.reciprocal(gmx[:], gsum[:]))
            then(nc.vector.tensor_tensor(gate[:], gex[:], bcast(gmx[:], NE), ALU.mult))
            for n in range(NT):
                nc.vector.max(top8[:, n, :], gate[:, n, :]).then_inc(f["g"], 1)
            g[0] += NT
            for n in range(NT):
                v.wait_ge(f["g"], g[0] - NT + n + 1)
                nc.vector.max_index(idx8[:, n, :], top8[:, n, :], gate[:, n, :]).then_inc(f["g"], 1)
            g[0] += NT
            then(nc.vector.tensor_tensor(wk[:, 0, :], top8[:, :, 1], top8[:, :, 0], ALU.subtract))
            assert g[0] == GATE_DIFF
            then(nc.vector.tensor_copy(idxf[:], idx8[:, :, 0:2]))
            v.wait_ge(f["ga"], 2)
            then(nc.vector.tensor_scalar(wk[:, 2, :], wk[:, 1, :], 1.0, None, ALU.add))
            then(nc.vector.reciprocal(wk[:, 3, :], wk[:, 2, :]))
            then(nc.vector.tensor_tensor(wk[:, 2, :], wk[:, 3, :], wk[:, 1, :], ALU.mult))
            for q in range(2):
                then(nc.vector.tensor_tensor(pick[:, q, :, :], iota[:].unsqueeze(1).broadcast_to([P, NT, NE]),
                                             bcast(idxf[:, :, q], NE), ALU.is_equal))
                then(nc.vector.tensor_tensor(pick[:, q, :, :], pick[:, q, :, :], bcast(wk[:, 3 - q, :], NE), ALU.mult))
            then(nc.vector.tensor_tensor(wts[:, :, 0:NE], pick[:, 0, :, :], pick[:, 1, :, :], ALU.add))

            with v.Fori(0, NCH // 2) as i:
                for s in range(2):
                    c = 2 * i + s
                    nc.vector.tensor_copy(wst[:, s, :, :], wts[:, chunk(c), :]).then_inc(f["ws"], 1)
                    for e in range(NX):
                        b = 4 + (s + e) % 2
                        v.wait_ge(f["l2"], c * NX + e + 1 + 2)
                        if e == 0:
                            nc.vector.tensor_tensor(acc[:, s, :, :], bank[b][:].rearrange("p (n c) -> p n c", c=C),
                                                    X[:, chunk(c), :], ALU.add).then_inc(f["acc"], 1)
                            continue
                        v.wait_ge(f["acc"], c * NX + e + 2)
                        for n in range(CT):
                            last = nc.vector.scalar_tensor_tensor(
                                out=acc[:, s, n, :], in0=bank[b][:, n * C:(n + 1) * C],
                                scalar=wst[:, s, n, e - 1:e], in1=acc[:, s, n, :], op0=ALU.mult, op1=ALU.add)
                        last.then_inc(f["acc"], 1)
                    v.wait_ge(f["wt"], c + 1)
                    nc.vector.tensor_copy(wtT[:, s, :], bank[7][0:NX, :]).then_inc(f["wc"], 1)
                    v.wait_ge(f["bp"], c + 1)
                    v.wait_ge(f["acc"], c * NX + NX + 2)
                    nc.vector.tensor_tensor(X[:, chunk(c), :], acc[:, s, :, :],
                                            bank[6][:].rearrange("p (n c) -> p n c", c=C), ALU.add).then_inc(f["x"], 1)

        def ffn_tensor(pe, k):
            f = FS[k]
            with pe.Fori(0, NCH // 2) as i:
                for s in range(2):
                    c = 2 * i + s
                    pe.wait_ge(f["st"], c + 1)
                    pe.wait_ge(f["xt"], c + 1)
                    for n in range(CT):
                        last = nc.tensor.transpose(bank[6 + s][:, n * P:(n + 1) * P], stage[:, s, n, :], ident[:])
                    last.then_inc(f["tr"], 1)
                    pe.wait_ge(f["xt"], c + 1 + 2)
                    nc.tensor.matmul(bank[4 + s][0:RH, :], wr1[:], xT[:, cols(c)], start=True, stop=True)\
                        .then_inc(f["r1"], 1)
                    pe.wait_ge(f["r1s"], c + 1)
                    for n in range(CT):
                        last = nc.tensor.matmul(bank[2][:, bass.ds(c * (CT * NE) + n * NE, NE)],
                                                r1[:, s, n * P:(n + 1) * P], wr2[:], start=True, stop=True)
                    last.then_inc(f["lg"], 1)

            def layer1(c, s, e):
                for b in range(NI):
                    pe.wait_ge(f["h"], c * NX * NI + e * NI + b + 1)
                    nc.tensor.matmul(bank[b][:], w1[:, e, b * P:(b + 1) * P], xT[:, cols(c)],
                                     start=True, stop=True).then_inc(f["l1"], 1)

            def layer2(c, s, e):
                pe.wait_ge(f["h"], c * NX * NI + e * NI + NI + NI)
                pe.wait_ge(f["acc"], c * NX + e + 1)
                for n in range(CT):
                    for b in range(NI):
                        last = nc.tensor.matmul(bank[4 + (s + e) % 2][:, n * C:(n + 1) * C],
                                                hT[:, (s + e) % 2, b, n * P:(n + 1) * P], w2[:, e, b, :],
                                                start=(b == 0), stop=(b == NI - 1))
                last.then_inc(f["l2"], 1)

            pe.wait_ge(f["g"], GATE_EXP)
            with pe.Fori(0, NCH // 2) as i:
                for s in range(2):
                    c = 2 * i + s
                    layer1(c, s, 0)
                    for e in range(1, NX):
                        layer1(c, s, e)
                        layer2(c, s, e - 1)
                    layer2(c, s, NX - 1)
                    pe.wait_ge(f["ws"], c + 1)
                    pe.wait_ge(f["wc"], c + 1)
                    for n in range(CT):
                        last = nc.tensor.transpose(bank[7][0:NX, n * P:(n + 1) * P], wst[:, s, n, :], ident[:])
                    last.then_inc(f["wt"], 1)
                    pe.wait_ge(f["wc"], c + 1 + 1)
                    pe.wait_ge(f["x"], c + 1)
                    for n in range(CT):
                        last = nc.tensor.matmul(bank[6][:, n * C:(n + 1) * C], wtT[:, s, n * P:(n + 1) * P], b2r[:],
                                                start=True, stop=True)
                    last.then_inc(f["bp"], 1)

        KU = QU = NG // 2
        SU, TU = KU + 3 * NG, QU + 3 * NG
        HQ = [(0, 0, GH), (1, 0, GH // 2), (1, GH // 2, GH // 2)]

        def s_bank(s, u):
            return bank[(SU * s + u) % 4]

        def t_bank(u):
            return bank[4 + u % 2]

        def probs(s, g, qt):
            kw = (qt + 1) * P
            return PR[:, g % 2, GH * P * qt:GH * P * qt + GH * kw].rearrange("p (j k) -> p j k", k=kw)

        def probsT(g, kt):
            qw = S - kt * P
            at = 0 if kt == 0 else GH * S
            return PT[:, g % 2, at:at + GH * qw].rearrange("p (j q) -> p j q", q=qw)

        def attention_scalar(a):
            f = AS
            ln_scalar(a, "lnb", D)

            def exps(b, s, g):
                a.wait_ge(f["t"], b * 3 * NG + 3 * g + 3)
                for r, (qt, j0, nj) in enumerate(HQ):
                    a.wait_ge(f["m"], b * 3 * NG + 3 * g + r + 1)
                    kw = (qt + 1) * P
                    for j in range(nj):
                        last = nc.scalar.activation(probs(s, g, qt)[:, j0 + j, :],
                                                    s_bank(s, KU + 3 * g + r)[:, j * kw:(j + 1) * kw], ACT.Exp,
                                                    bias=ngm[:, g % 2, qt, j0 + j:j0 + j + 1])
                    last.then_inc(f["se"], 1)

            def o_out(b, s, g):
                a.wait_ge(f["ot"], b * NG + g + 1)
                a.wait_ge(f["o"], b * NG + g + 1 + 2)
                nc.scalar.activation(oT[:, g % 2, :], bank[6][:, 0:S], ACT.Copy).then_inc(f["oe"], 1)

            with a.Fori(0, B // 2) as i:
                for s in range(2):
                    b = 2 * i + s
                    a.wait_ge(f["tr"], b + 1)
                    nc.scalar.activation(xnT[:, s, 0:S], bank[7][:, 0:S], ACT.Copy).then_inc(f["ln"], 1)
                    for u in range(KU):
                        a.wait_ge(f["k"], b * KU + u + 1)
                        for w in range(2):
                            g = 2 * u + w
                            last = nc.scalar.activation(kT[:, s, g, :], s_bank(s, u)[:, w * S:(w + 1) * S],
                                                        ACT.Identity, bias=bqk[:, NG + g:NG + g + 1])
                        last.then_inc(f["se"], 1)
                    exps(b, s, 0)
                    exps(b, s, 1)
                    exps(b, s, 2)
                    o_out(b, s, 0)
                    exps(b, s, 3)
                    for g in range(1, NG):
                        o_out(b, s, g)
                    a.wait_ge(f["yt"], b + 1)
                    nc.scalar.activation(yT[:, s, :], bank[7][:, 0:S], ACT.Copy).then_inc(f["ye"], 1)

        def attention_vector(v):
            f = AS
            ln_vector(v, "lnb", X[:], D[:])

            def maxima(b, s, g):
                v.wait_ge(f["se"], b * SU + 3 * g + 3)
                for r, (qt, j0, nj) in enumerate(HQ):
                    v.wait_ge(f["s"], b * 3 * NG + 3 * g + r + 1)
                    sc = s_bank(s, KU + 3 * g + r)[:].rearrange("p (j k) -> p j k", j=nj)
                    nc.vector.tensor_reduce(ngm[:, g % 2, qt, j0:j0 + nj], sc, AX_X, ALU.max,
                                            negate=True).then_inc(f["m"], 1)

            def pt_out(b, s, g):
                v.wait_ge(f["o"], b * NG + g + 1)
                for r, dst in enumerate((probsT(g, 0)[:, :, 0:P], probsT(g, 0)[:, :, P:S], probsT(g, 1))):
                    v.wait_ge(f["t"], b * 3 * NG + 3 * g + r + 1 + 6)
                    nc.vector.tensor_copy(dst, t_bank(QU + 3 * g + r)[:].rearrange("p (j q) -> p j q", q=P))\
                        .then_inc(f["te"], 1)

            def norm(b, s, g):
                v.wait_ge(f["ot"], b * NG + g + 1 + 2)
                o = bank[7][:, (g % 2) * S:(g % 2 + 1) * S].rearrange("p (qt j d) -> p qt j d", qt=QT, j=GH)
                nc.vector.reciprocal(rden[:, g % 2, :, :], o[:, :, :, HD]).then_inc(f["rd"], 1)
                v.wait_ge(f["rd"], b * NG + g + 1)
                nc.vector.tensor_tensor(yat[:, s, :, GH * g:GH * (g + 1), :], o[:, :, :, 0:HD],
                                        bcast(rden[:, g % 2, :, :], HD), ALU.mult).then_inc(f["y"], 1)

            with v.Fori(0, B // 2) as i:
                for s in range(2):
                    b = 2 * i + s
                    nc.vector.tensor_tensor(stage[:, s, 0:QT, :], D[:, chunk(b, QT), :], bcast(st_r[:, chunk(b, QT)], C),
                                            ALU.mult).then_inc(f["st"], 1)
                for s in range(2):
                    b = 2 * i + s
                    for u in range(QU):
                        v.wait_ge(f["q"], b * QU + u + 1)
                        for j in range(GH):
                            r = slice(32 * j, 32 * j + 32)
                            last = nc.vector.tensor_tensor(
                                qblk[r, s, 2 * u:2 * u + 2, j, :], t_bank(u)[r, :].rearrange("p (w t) -> p w t", w=2),
                                bcast(bqk[r, 2 * u:2 * u + 2], S), ALU.add)
                        last.then_inc(f["te"], 1)
                    v.wait_ge(f["v"], b + 1)
                    nc.vector.tensor_tensor(
                        va[:, s, :, :, 0:HD], bank[6][:, 0:S].rearrange("p (q h d) -> p q h d", q=QT, h=NH),
                        bv[:].rearrange("p (h d) -> p h d", h=NH).unsqueeze(1).broadcast_to([P, QT, NH, HD]),
                        ALU.add).then_inc(f["ve"], 1)
                    maxima(b, s, 0)
                    maxima(b, s, 1)
                    pt_out(b, s, 0)
                    maxima(b, s, 2)
                    pt_out(b, s, 1)
                    maxima(b, s, 3)
                    norm(b, s, 0)
                    pt_out(b, s, 2)
                    norm(b, s, 1)
                    pt_out(b, s, 3)
                    norm(b, s, 2)
                    norm(b, s, 3)
                    v.wait_ge(f["p"], b + 1)
                    xb = X[:, chunk(b, QT), :]
                    nc.vector.tensor_tensor(xb, bank[7][:, S:2 * S].rearrange("p (q c) -> p q c", q=QT), xb,
                                            ALU.add).then_inc(f["x"], 1)
                    v.wait_ge(f["x"], b + 1 + 1)
                    nc.vector.tensor_tensor(xb, xb, bpj[:].unsqueeze(1).broadcast_to([P, QT, C]),
                                            ALU.add).then_inc(f["xb"], 1)
            v.wait_ge(f["xb"], B)

        def attention_tensor(pe):
            f = AS

            def scores(b, s, g):
                for r, (qt, j0, nj) in enumerate(HQ):
                    u = KU + 3 * g + r
                    kw = (qt + 1) * P
                    pe.wait_ge(f["se"], b * SU + u + 1)
                    for j in range(nj):
                        nc.tensor.matmul(s_bank(s, u)[:, j * kw:(j + 1) * kw], qblk[:, s, g, j0 + j, qt * P:(qt + 1) * P],
                                         kT[:, s, g, 0:kw], start=(j == 0), stop=False)
                    diag = s_bank(s, u)[:].rearrange("p (j k) -> p j k", j=nj)[:, :, qt * P:(qt + 1) * P]
                    nc.tensor.matmul(diag, identb[:], cmask[:, 0:nj * P].rearrange("p (j k) -> p j k", j=nj),
                                     start=False, stop=True).then_inc(f["s"], 1)

            def transposes(b, s, g):
                for r, (qt, kt) in enumerate(((0, 0), (1, 0), (1, 1))):
                    if r < 2:
                        pe.wait_ge(f["se"], b * SU + KU + 3 * g + (1, 3)[r] + 4)
                    pe.wait_ge(f["te"], b * TU + QU + 3 * g + r + 1)
                    for j in range(GH):
                        last = nc.tensor.transpose(t_bank(QU + 3 * g + r)[:, j * P:(j + 1) * P],
                                                   probs(s, g, qt)[:, j, kt * P:(kt + 1) * P], ident[:])
                    last.then_inc(f["t"], 1)

            def pv(b, s, g):
                pe.wait_ge(f["te"], b * TU + QU + 3 * g + 3 + 2)
                if g == 0:
                    pe.wait_ge(f["ve"], b + 1)
                pe.wait_ge(f["oe"], b * NG + g + 1)
                for kt in range(QT):
                    for j in range(GH):
                        last = nc.tensor.matmul(bank[6][32 * j:32 * j + 32, kt * P:S], va[:, s, kt, GH * g + j, :],
                                                probsT(g, kt)[:, j, :], start=(kt == 0), stop=(kt == QT - 1),
                                                tile_position=(0, 32 * j), skip_group_check=True)
                last.then_inc(f["o"], 1)

            def o_transposes(b, s, g):
                pe.wait_ge(f["oe"], b * NG + g + 1 + 1)
                if g > 0:
                    pe.wait_ge(f["y"], b * NG + g)
                for qt in range(QT):
                    at = (g % 2) * S + qt * P
                    last = nc.tensor.transpose(bank[7][:, at:at + P], oT[:, g % 2, qt * P:(qt + 1) * P], ident[:])
                last.then_inc(f["ot"], 1)

            with pe.Fori(0, B // 2) as i:
                for s in range(2):
                    b = 2 * i + s
                    pe.wait_ge(f["st"], b + 1)
                    pe.wait_ge(f["x"], b + 1)
                    for q in range(QT):
                        last = nc.tensor.transpose(bank[7][:, q * P:(q + 1) * P], stage[:, s, q, :], ident[:])
                    last.then_inc(f["tr"], 1)
                    pe.wait_ge(f["ln"], b + 1)
                    for u in range(QU):
                        pe.wait_ge(f["te"], b * TU + u + 1)
                        for w in range(2):
                            last = nc.tensor.matmul(t_bank(u)[:, w * S:(w + 1) * S],
                                                    wqk[:, GH * (2 * u + w):GH * (2 * u + w + 1), :],
                                                    xnT[:, s, 0:S], start=True, stop=True)
                        last.then_inc(f["q"], 1)
                    for u in range(KU):
                        pe.wait_ge(f["se"], b * SU + u + 1)
                        for w in range(2):
                            h0 = NH + GH * (2 * u + w)
                            last = nc.tensor.matmul(s_bank(s, u)[:, w * S:(w + 1) * S], wqk[:, h0:h0 + GH, :],
                                                    xnT[:, s, 0:S], start=True, stop=True)
                        last.then_inc(f["k"], 1)
                    pe.wait_ge(f["oe"], b * NG + 1)
                    for q in range(QT):
                        last = nc.tensor.matmul(bank[6][:, q * P:(q + 1) * P], xnT[:, s, q * P:(q + 1) * P],
                                                wat[:, 2 * C:3 * C], start=True, stop=True)
                    last.then_inc(f["v"], 1)
                    pe.wait_ge(f["te"], b * TU + QU + 2)
                    pe.wait_ge(f["se"], b * SU + KU + 4)
                    scores(b, s, 0)
                    scores(b, s, 1)
                    transposes(b, s, 0)
                    scores(b, s, 2)
                    pv(b, s, 0)
                    transposes(b, s, 1)
                    scores(b, s, 3)
                    o_transposes(b, s, 0)
                    pv(b, s, 1)
                    transposes(b, s, 2)
                    o_transposes(b, s, 1)
                    pv(b, s, 2)
                    transposes(b, s, 3)
                    o_transposes(b, s, 2)
                    pv(b, s, 3)
                    o_transposes(b, s, 3)
                    pe.wait_ge(f["y"], b * NG + NG)
                    for q in range(QT):
                        last = nc.tensor.transpose(bank[7][:, q * P:(q + 1) * P],
                                                   yat[:, s, q, :, :].rearrange("p h d -> p (h d)"), ident[:])
                    last.then_inc(f["yt"], 1)
                    pe.wait_ge(f["ye"], b + 1)
                    for q in range(QT):
                        last = nc.tensor.matmul(bank[7][:, S + q * P:S + (q + 1) * P], yT[:, s, q * P:(q + 1) * P],
                                                wpj[:], start=True, stop=True)
                    last.then_inc(f["p"], 1)

        block = ctx.enter_context(nc.Block())

        @block.sync
        def _(sp):
            xv = t["L0_attn_a_x"].rearrange("b (q p) c -> p (b q) c", p=P)
            for c in range(NCH):
                sp.dma_start(X[:, c * CT:(c + 1) * CT, :], xv[:, c * CT:(c + 1) * CT, :]).then_inc(ld_x, 16)

            def load(key, s, dst, src, **how):
                sp.dma_start(dst, src, **how).then_inc(s, 16)
                n_ld[key] += 16

            def rows(v):
                return v.rearrange("(a n) -> a n", a=1)

            def column(dst, v, h=1):
                load("a", ld_a, dst, v.rearrange("(h p) -> p h", h=h), allow_slow_non_contiguous=True)

            load("a", ld_a, ident[:], t["c_ident"])
            load("a", ld_a, win_n, t["L0_attn_a_W_in"].rearrange("(e p) d -> p e d", p=P))
            column(nw[:], t["L0_attn_a_norm_w"])
            column(nb[:], t["L0_attn_a_norm_b"])
            load("a", ld_a, cw[:], t["L0_attn_a_conv_w"].rearrange("(h p) k -> p h k", h=2))
            column(cb[:], t["L0_attn_a_conv_b"], 2)
            load("a", ld_a, wdt_n, t["L0_attn_a_W_dt"].rearrange("(e p) d -> p e d", p=P))
            column(bdt[:], t["L0_attn_a_b_dt"], 2)
            column(Dv[:], t["L0_attn_a_D"], 2)
            load("a", ld_a, Am[:], t["L0_attn_a_A_log"].rearrange("(h p) n -> p h n", h=2))
            load("a", ld_a, wout_n, t["L0_attn_a_W_out"])
            load("a", ld_a, sel_f, t["c_sel"])
            sp.wait_ge(st_wbc, 1)
            for q in range(3):
                load("a", ld_a, wbc_n[32 * q:32 * q + NS, :], t["L0_attn_a_W_B"])
                load("a", ld_a, wbc_n[32 * q + NS:32 * q + 2 * NS, :], t["L0_attn_a_W_C"])

            load("f", ld_f, w1[:, 0, :], t["L0_ffn_Ws1"])
            load("f", ld_f, w1[:, 1:NX, :], t["L0_ffn_We1"].rearrange("e c i -> c e i"))
            load("f", ld_f, w2[:, 0, :, :], t["L0_ffn_Ws2"].rearrange("(i p) c -> p i c", p=P))
            for e in range(NE):
                load("f", ld_f, w2[:, 1 + e, :, :], t["L0_ffn_We2"][e].rearrange("(i p) c -> p i c", p=P))
            load("f", ld_f, b1n[0:NI, :], t["L0_ffn_bs1"].rearrange("(i p) -> i p", p=P))
            load("f", ld_f, b1n[NI:NX * NI, :], t["L0_ffn_be1"].rearrange("e (i p) -> (e i) p", p=P))
            load("f", ld_f, b2r[0:NE, :], t["L0_ffn_be2"])
            load("f", ld_f, b2r[NE:NX, :], rows(t["L0_ffn_bs2"]))
            load("f", ld_f, wr1[:], t["L0_ffn_Wr1"])
            load("f", ld_f, wr2[:], t["L0_ffn_Wr2"])
            load("f", ld_f, br1[:], t["L0_ffn_br1"].rearrange("(p a) -> p a", a=1))
            load("f", ld_f, br2[:], t["L0_ffn_br2"].partition_broadcast(P))
            load("f", ld_f, iota[:], t["c_iota"].partition_broadcast(P))

            load("b", ld_b, wat[:], t["L0_attn_b_W_attn"])
            load("b", ld_b, rope[:], t["c_rope"].partition_broadcast(P))
            load("b", ld_b, bat[:], rows(t["L0_attn_b_b_attn"])[:, 0:2 * C])
            load("b", ld_b, bv[:], t["L0_attn_b_b_attn"][2 * C:3 * C].partition_broadcast(P))
            load("b", ld_b, bpj[:], t["L0_attn_b_b_proj"].partition_broadcast(P))
            load("b", ld_b, wpj[:], t["L0_attn_b_W_proj"])
            load("b", ld_b, cmask_f, t["c_mask"])

            ov = out.rearrange("b (q p) c -> p (b q) c", p=P)
            for c in range(NCH):
                sp.wait_ge(FS[1]["x"], c + 1 + 1)
                sp.dma_start(ov[:, c * CT:(c + 1) * CT, :], X[:, c * CT:(c + 1) * CT, :]).then_inc(s_out, 16)
            sp.wait_ge(s_out, 16 * NCH)

        LOADED_A, LOADED_F, LOADED_B = n_ld["a"], n_ld["f"], n_ld["b"]

        @block.gpsimd
        def _(pool):
            pool.sem_inc(m3_hc, 4)
            nc.gpsimd.memset(wbc_n, 0.0).then_inc(st_wbc, 1)
            nc.gpsimd.memset(eps_t[:], EPS).then_inc(st_zero, 1)
            nc.gpsimd.memset(one_t[:], 1.0).then_inc(st_zero, 1)
            nc.gpsimd.memset(xpad[:], 0.0).then_inc(st_zero, 1)
            nc.gpsimd.memset(decay[:, :, :, 0:1], 0.0).then_inc(st_zero, 1)
            pool.wait_ge(st_wbc, 1)
            nc.gpsimd.memset(wqk[:], 0.0).then_inc(st_zero, 1)
            nc.gpsimd.memset(bqk_r, 0.0).then_inc(st_zero, 1)
            nc.gpsimd.memset(one1[:], 1.0).then_inc(st_zero, 1)
            nc.gpsimd.memset(wts[:, :, NE:NX], 1.0).then_inc(st_zero, 1)

            pool.wait_ge(ld_a, LOADED_A)
            nc.gpsimd.tensor_copy(identb[:], ident[:]).then_inc(st_const, 1)
            nc.gpsimd.tensor_copy(sel[:], sel_f).then_inc(st_const, 1)
            pool.wait_ge(ld_b, LOADED_B)
            nc.gpsimd.tensor_copy(cmask[:].rearrange("p (j k) -> p j k", k=P),
                                  cmask_f.unsqueeze(1).broadcast_to([P, 512 // P, P])).then_inc(st_const, 1)

            pool.wait_ge(ld_b, LOADED_B)
            n = 0
            for w, wa, wb, o in ((wat[:, 0:2 * C], ra, rb, wqk[:, :, 0:HD]),
                                 (bat[:], bra, brb, bqk_r[:, :, 0:HD])):
                p = w.shape[0]
                pair = w.rearrange("p (h i two) -> p h i two", h=2 * NH, two=2)
                turned = o.rearrange("p h (i two) -> p h i two", two=2)
                cos, sin = rope[0:p, 0, :, :], rope[0:p, 1, :, :]
                for first, second, op in ((0, 1, ALU.subtract), (1, 0, ALU.add)):
                    nc.gpsimd.tensor_tensor(wa, pair[:, :, :, first], cos, ALU.mult).then_inc(st_rope, 1)
                    nc.gpsimd.tensor_tensor(wb, pair[:, :, :, second], sin, ALU.mult).then_inc(st_rope, 1)
                    n += 2
                    pool.wait_ge(st_rope, n)
                    nc.gpsimd.tensor_tensor(turned[:, :, :, first], wa, wb, op).then_inc(st_rope, 1)
                    n += 1
                    pool.wait_ge(st_rope, n)

            with pool.Fori(0, NCH) as c:
                for n in range(NS):
                    pool.wait_ge(m3_cs, c * NS + n + 1 + 2)
                    for h in range(2):
                        k = 2 * n + h
                        pool.wait_ge(m3_sc, c * 2 * NS + k + 1 + NR)
                        nc.gpsimd.tensor_tensor(hst[:, k % NR, :], hst[:, k % NR, :], Csb[:, n % 2, :],
                                                ALU.mult).then_inc(m3_hc, 1)

            pool.wait_ge(m3_x, 2 * NCH)
            nc.gpsimd.memset(arena[:, 0:8192], 0.0).then_inc(st_qz, 1)
            nc.gpsimd.memset(va, 0.0).then_inc(st_qz, 1)
            pool.wait_ge(st_qz, 2)
            nc.gpsimd.memset(va[:, :, :, :, HD:HD + 1], 1.0).then_inc(st_qz, 1)

        @block.scalar
        def _(act):
            act.sem_inc(m1_xe, 4)
            act.sem_inc(m1_ze, 2)
            act.sem_inc(m1_xc, 4)
            act.sem_inc(m2_ab, 4)
            act.sem_inc(m2_hi, 2)
            act.sem_inc(m3_cs, 2)
            for k in range(2):
                act.sem_inc(FS[k]["xt"], 2)
                act.sem_inc(FS[k]["h"], NI)
            act.sem_inc(AS["se"], 4)
            act.sem_inc(AS["oe"], 1)
            act.wait_ge(st_zero, 8)
            ln_scalar(act, "ln0", U)
            ln_scalar(act, "ln1", D)
            act.wait_ge(ld_a, LOADED_A)

            with act.Fori(0, NCH // 2) as i:
                for s in range(2):
                    c = 2 * i + s
                    act.wait_ge(m1_tr, c + 1 + 2)
                    nc.scalar.activation(xnT[:, s, :], bank[6 + s][:], ACT.Identity, bias=nb[:, 0:1],
                                         scale=nw[:, 0:1]).then_inc(m1_xn, 1)
                    act.wait_ge(m1_cv, 2 * c + 2)
                    for h in range(2):
                        act.wait_ge(m1_xz, 4 * c + h + 1)
                        nc.scalar.activation(xpad[:, s, h, :, KC - 1:KC - 1 + S],
                                             bank[2 * s + h][:].rearrange("p (b t) -> p b t", b=BPC),
                                             ACT.Copy).then_inc(m1_xe, 1)
                    for h in range(2):
                        act.wait_ge(m1_xz, 4 * c + 2 + h + 1)
                        apart(act)
                        nc.scalar.activation(zs[:, h, cols(c)], bank[4 + h][:], ACT.Silu).then_inc(m1_ze, 1)
                for s in range(2):
                    c = 2 * i + s
                    for h in range(2):
                        act.wait_ge(m1_cv, 2 * c + h + 1 + 4)
                        apart(act)
                        nc.scalar.activation(xc[:, h, cols(c)], conv[:, s, h, :], ACT.Silu).then_inc(m1_xc, 1)

            nc.scalar.activation(Am[:], Am[:], ACT.Exp).then_inc(st_A, 1)

            with act.Fori(0, NCH // 2) as i:
                for s in range(2):
                    c = 2 * i + s
                    for h in range(2):
                        act.wait_ge(m2_mm, 3 * c + h + 1)
                        apart(act)
                        nc.scalar.activation(dt_[:, h, cols(c)], bank[2 * s + h][:], ACT.Abs,
                                             bias=bdt[:, h:h + 1]).then_inc(m2_ab, 1)
                    act.wait_ge(m2_mm, 3 * c + 3)
                    apart(act)
                    nc.scalar.activation(BCs[:, cols(c)], bank[4 + s][:], ACT.Copy).then_inc(m2_hi, 1)
                    for h in range(2):
                        act.wait_ge(m2_ab, 2 * c + h + 1 + 4)
                        apart(act)
                        nc.scalar.activation(dt_[:, h, cols(c)], dt_[:, h, cols(c)], ACT.Exp,
                                             scale=-1.0).then_inc(m2_ex, 1)
            act.wait_ge(m2_ex, 2 * NCH)
            for h in range(2):
                nc.scalar.activation(dt_[:, h, :], dt_[:, h, :], ACT.Ln, bias=one_t[:, 0:1]).then_inc(m2_ln, 1)

            with act.Fori(0, NCH) as c:
                act.wait_ge(st_A, 2)
                for n in range(NS):
                    act.wait_ge(m3_cb, c * NS + n + 1)
                    act.wait_ge(m3_hc, c * 2 * NS + 2 * n + 2)
                    nc.scalar.activation(Csb[:, n % 2, :], bank[2 + n % 2][:], ACT.Copy).then_inc(m3_cs, 1)
                    for h in range(2):
                        k = 2 * n + h
                        act.wait_ge(m3_dt, 2 * c + h + 1)
                        act.wait_ge(m3_sc, c * 2 * NS + k + 1)
                        apart(act)
                        nc.scalar.activation(decay[:, k % NR, :, 1:S],
                                             dt_[:, h, cols(c)].rearrange("p (b t) -> p b t", b=BPC)[:, :, 1:S],
                                             ACT.Exp, scale=Am[:, h, n:n + 1]).then_inc(m3_a, 1)

            ffn_scalar(act, 0, "lnf0")
            attention_scalar(act)
            ffn_scalar(act, 1, "lnf1")

        @block.vector
        def _(v):
            v.sem_inc(m1_cv, 4)
            v.sem_inc(m2_re, 4)
            v.sem_inc(m2_r, 2)
            v.sem_inc(m3_sc, NR)
            v.sem_inc(m3_b, 4)
            v.sem_inc(m3_ya, 2)
            for k in range(2):
                v.sem_inc(FS[k]["acc"], 2)
                v.sem_inc(FS[k]["wc"], 1)
                v.sem_inc(FS[k]["x"], 1)
            v.sem_inc(AS["te"], 2)
            v.sem_inc(AS["x"], 1)

            v.wait_ge(ld_x, 16 * NCH)
            ln_vector(v, "ln0", X[:], U[:])
            nc.vector.tensor_tensor(U[:], U[:], bcast(st_r[:], C), ALU.mult).then_inc(LN["ln0"]["r"], 1)
            v.wait_ge(LN["ln0"]["r"], 2)
            ln_vector(v, "ln1", U[:], D[:])

            for n, dst in enumerate((winT[:].rearrange("p a b -> p (a b)"), wdtT[:].rearrange("p a b c -> p (a b c)"),
                                     wboT[:].rearrange("p a b -> p (a b)"), b1T[:])):
                v.wait_ge(st_tr, n + 1)
                nc.vector.tensor_copy(dst, bank[n][:, 0:dst.shape[1]]).then_inc(st_cp, 1)
            v.wait_ge(st_bq, 1)
            nc.vector.tensor_copy(bqk[:], bank[4][:, 0:2 * NG]).then_inc(st_bqc, 1)
            v.wait_ge(ld_a, LOADED_A)

            with v.Fori(0, NCH // 2) as i:
                for s in range(2):
                    c = 2 * i + s
                    v.wait_ge(m1_tr, c + 1)
                    nc.vector.tensor_tensor(stage[:, s, :, :], D[:, chunk(c), :], bcast(st_r[:, chunk(c)], C),
                                            ALU.mult).then_inc(m1_st, 1)
                for s in range(2):
                    c = 2 * i + s
                    for k in range(KC):
                        for h in range(2):
                            src = xpad[:, s, h, :, k:k + S]
                            dst = conv[:, s, h, :].rearrange("p (b t) -> p b t", b=BPC)
                            if k == 0:
                                v.wait_ge(m1_xe, 2 * c + h + 1 + 4)
                                v.wait_ge(m1_xc, 2 * c + h + 1)
                                nc.vector.tensor_scalar(dst, src, cw[:, h, 0:1], cb[:, h:h + 1], ALU.mult,
                                                        ALU.add).then_inc(m1_cd, 1)
                                continue
                            v.wait_ge(m1_cd, c * (2 * KC - 2) + 2 * k + h - 1)
                            last = nc.vector.scalar_tensor_tensor(out=dst, in0=src, scalar=cw[:, h, k:k + 1], in1=dst,
                                                                  op0=ALU.mult, op1=ALU.add)
                            last.then_inc(m1_cd if k < KC - 1 else m1_cv, 1)

            v.wait_ge(st_A, 1)
            nc.vector.tensor_scalar(Am[:], Am[:], -1.0, None, ALU.mult).then_inc(st_A, 1)

            with v.Fori(0, NCH // 2) as i:
                for s in range(2):
                    c = 2 * i + s
                    for h in range(2):
                        v.wait_ge(m2_ab, 2 * c + h + 1 + 4)
                        nc.vector.tensor_scalar(dtx[:, h, cols(c)], bank[2 * s + h][:], bdt[:, h:h + 1], 0.0, ALU.add,
                                                ALU.max).then_inc(m2_re, 1)
                    v.wait_ge(m2_hi, c + 1 + 2)
                    nc.vector.tensor_tensor(bcr[:, s, :], bank[4 + s][:], BCs[:, cols(c)], ALU.subtract)\
                        .then_inc(m2_r, 1)
                    v.wait_ge(m2_r, c + 1 + 2)
                    nc.vector.tensor_copy(bcm[:, s, :], bcr[:, s, :]).then_inc(m2_md, 1)
                    v.wait_ge(m2_md, c + 1)
                    nc.vector.tensor_copy(BCs[32:64, cols(c)], bcm[32:64, s, :]).then_inc(m2_st, 1)
                    nc.vector.tensor_tensor(BCs[64:96, cols(c)], bcr[64:96, s, :], bcm[64:96, s, :],
                                            ALU.subtract).then_inc(m2_st, 1)

            with v.Fori(0, NCH) as c:
                for h in range(2):
                    v.wait_ge(m2_ln, h + 1)
                    nc.vector.tensor_tensor(dt_[:, h, cols(c)], dt_[:, h, cols(c)], dtx[:, h, cols(c)], ALU.add)\
                        .then_inc(m3_dt, 1)
                for h in range(2):
                    v.wait_ge(m3_dt, 2 * c + h + 1)
                    nc.vector.tensor_tensor(dtx[:, h, cols(c)], dt_[:, h, cols(c)], xc[:, h, cols(c)], ALU.mult)\
                        .then_inc(m3_dx, 1)

                def inputs(k):
                    n, h = k // 2, k % 2
                    if k < 2:
                        v.wait_ge(m3_dx, 2 * c + h + 1)
                    v.wait_ge(m3_sc, c * 2 * NS + k + 1)
                    v.wait_ge(m3_bb, c * NS + n + 1)
                    nc.vector.tensor_tensor(inp[:, k % NR, :], bank[n % 2][:], dtx[:, h, cols(c)], ALU.mult)\
                        .then_inc(m3_b, 1)

                inputs(0)
                for k in range(2 * NS):
                    if k + 1 < 2 * NS:
                        inputs(k + 1)
                    v.wait_ge(m3_a, c * 2 * NS + k + 1)
                    v.wait_ge(m3_ns, c * 2 * NS + k + 1)
                    v.wait_ge(m3_b, c * 2 * NS + k + 1 + 4)
                    nc.vector.tensor_tensor_scan(hst[:, k % NR, :], decay[:, k % NR, :, :].rearrange("p b t -> p (b t)"),
                                                 inp[:, k % NR, :], 0.0, ALU.mult, ALU.add).then_inc(m3_sc, 1)
                for h in range(2):
                    v.wait_ge(m3_ns, c * 2 * NS + 2 * NS - 1 + h + NR)
                    nc.vector.scalar_tensor_tensor(out=ybuf[:, h, :], in0=xc[:, h, cols(c)], scalar=Dv[:, h:h + 1],
                                                   in1=bank[4 + h][:], op0=ALU.mult, op1=ALU.add).then_inc(m3_ya, 1)
                for h in range(2):
                    v.wait_ge(m3_ya, 2 * c + h + 1 + 2)
                    nc.vector.tensor_tensor(ybuf[:, h, :], ybuf[:, h, :], zs[:, h, cols(c)], ALU.mult)\
                        .then_inc(m3_y, 1)
                v.wait_ge(m3_o, c + 1)
                nc.vector.tensor_tensor(U[:, chunk(c), :], bank[6][:].rearrange("p (n c) -> p n c", c=C),
                                        U[:, chunk(c), :], ALU.add).then_inc(m3_x, 1)
                v.wait_ge(m3_x, 2 * c + 1)
                nc.vector.tensor_tensor(X[:, chunk(c), :], X[:, chunk(c), :], U[:, chunk(c), :], ALU.add)\
                    .then_inc(m3_x, 1)
            v.wait_ge(m3_x, 2 * NCH)
            ffn_vector(v, 0, "lnf0")
            v.wait_ge(FS[0]["x"], NCH + 1)
            v.wait_ge(st_qz, 3)
            attention_vector(v)
            ffn_vector(v, 1, "lnf1")

        @block.tensor
        def _(pe):
            pe.sem_inc(m1_tr, 2)
            pe.sem_inc(m3_ns, NR)
            for k in range(2):
                pe.sem_inc(FS[k]["tr"], 2)
                pe.sem_inc(FS[k]["l2"], 2)
            pe.sem_inc(AS["t"], 6)
            pe.sem_inc(AS["o"], 2)
            pe.sem_inc(AS["ot"], 2)

            pe.wait_ge(ld_a, LOADED_A)
            for e in range(4):
                last = nc.tensor.transpose(bank[0][:, e * P:(e + 1) * P], win_n[:, e, :], ident[:])
            last.then_inc(st_tr, 1)
            for e in range(2):
                for d in range(2):
                    last = nc.tensor.transpose(bank[1][:, (2 * e + d) * P:(2 * e + d + 1) * P],
                                               wdt_n[:, e, d * P:(d + 1) * P], ident[:])
            last.then_inc(st_tr, 1)
            for d in range(2):
                nc.tensor.transpose(bank[2][:, d * P:(d + 1) * P], wbc_n[:, d * P:(d + 1) * P], ident[:])
            for d in range(2):
                last = nc.tensor.transpose(bank[2][:, (2 + d) * P:(3 + d) * P], wout_n[:, d * P:(d + 1) * P], ident[:])
            last.then_inc(st_tr, 1)
            pe.wait_ge(ld_f, LOADED_F)
            nc.tensor.transpose(bank[3][:, 0:NX * NI], b1n[:], ident[0:NX * NI, 0:NX * NI]).then_inc(st_tr, 1)
            pe.wait_ge(st_const, 3)
            pe.wait_ge(st_rope, 12)
            pe.wait_ge(st_zero, 8)
            for g in range(2 * NG):
                last = nc.tensor.matmul(bank[4][:, g:g + 1], bqk_r[:, GH * g:GH * (g + 1), :], one1[:],
                                        start=True, stop=True)
            last.then_inc(st_bq, 1)
            pe.wait_ge(st_cp, 4)
            pe.wait_ge(st_bqc, 1)

            with pe.Fori(0, NCH // 2) as i:
                for s in range(2):
                    c = 2 * i + s
                    pe.wait_ge(m1_st, c + 1)
                    for n in range(CT):
                        last = nc.tensor.transpose(bank[6 + s][:, n * P:(n + 1) * P], stage[:, s, n, :], ident[:])
                    last.then_inc(m1_tr, 1)
                for s in range(2):
                    c = 2 * i + s
                    pe.wait_ge(m1_xn, c + 1)
                    for e in range(4):
                        if e < 2:
                            dst = bank[2 * s + e]
                            pe.wait_ge(m1_xe, 2 * c + e + 1)
                        else:
                            dst = bank[4 + e - 2]
                            pe.wait_ge(m1_ze, 2 * c + e - 2 + 1)
                        nc.tensor.matmul(dst[:], winT[:, e, :], xnT[:, s, :], start=True, stop=True).then_inc(m1_xz, 1)

            pe.wait_ge(m1_xc, 2 * NCH + 4)
            with pe.Fori(0, NCH // 2) as i:
                for s in range(2):
                    c = 2 * i + s
                    for e in range(2):
                        pe.wait_ge(m2_ab, 2 * c + e + 1)
                        pe.wait_ge(m2_re, 2 * c + e + 1)
                        for d in range(2):
                            last = nc.tensor.matmul(bank[2 * s + e][:], wdtT[:, e, d, :], xc[:, d, cols(c)],
                                                    start=(d == 0), stop=(d == 1))
                        last.then_inc(m2_mm, 1)
                    pe.wait_ge(m2_hi, c + 1)
                    pe.wait_ge(m2_r, c + 1)
                    for d in range(2):
                        last = nc.tensor.matmul(bank[4 + s][:], wboT[:, d, :], xc[:, d, cols(c)],
                                                start=(d == 0), stop=(d == 1))
                    last.then_inc(m2_mm, 1)

            pe.wait_ge(m2_st, 2 * NCH)
            with pe.Fori(0, NCH) as c:
                def spread(n):
                    for what, (s_free, need, s_done) in enumerate(
                            ((m3_b, c * 2 * NS + 2 * n + 2, m3_bb), (m3_cs, c * NS + n + 1, m3_cb))):
                        pe.wait_ge(s_free, need)
                        col = what * NS + n
                        nc.tensor.matmul(bank[2 * what + n % 2][:], sel[:, col:col + 1].broadcast_to([P, P]),
                                         BCs[:, cols(c)], start=True, stop=True).then_inc(s_done, 1)

                def sum_states(n):
                    for h in range(2):
                        k = 2 * n + h
                        if n == 0:
                            pe.wait_ge(m3_ya, 2 * c + h + 1)
                        pe.wait_ge(m3_hc, c * 2 * NS + k + 1 + 4)
                        nc.tensor.matmul(bank[4 + h][:], ident[:], hst[:, k % NR, :], start=(n == 0),
                                         stop=(n == NS - 1)).then_inc(m3_ns, 1)

                spread(0)
                spread(1)
                for n in range(2, NS):
                    spread(n)
                    sum_states(n - 2)
                sum_states(NS - 2)
                sum_states(NS - 1)
                pe.wait_ge(m3_y, 2 * c + 2)
                for n in range(CT):
                    for h in range(2):
                        last = nc.tensor.matmul(bank[6][:, n * C:(n + 1) * C], ybuf[:, h, n * P:(n + 1) * P],
                                                wboT[:, 2 + h, :], start=(h == 0), stop=(h == 1))
                last.then_inc(m3_o, 1)

            ffn_tensor(pe, 0)
            pe.wait_ge(st_qz, 3)
            attention_tensor(pe)
            ffn_tensor(pe, 1)


_OUTS = [((8, 256, 128), "float32")]


def _constants():
    import numpy as np

    P, NS, NE, NH, HD = 128, 16, 8, 16, 8
    k = np.arange(P)
    sel = ((k[:, None] % 32 == np.arange(2 * NS)[None, :]) & (k[:, None] < 96)).astype(np.float32)
    mask = np.where(k[None, :] > k[:, None], -1e30, 0.0).astype(np.float32)
    theta = 1.0 / 10000.0 ** (np.arange(0, HD, 2, dtype=np.float32) / HD)
    ang = np.arange(NH, dtype=np.float32)[:, None] * theta[None, :].astype(np.float32)
    scale = np.concatenate([np.full((NH, 1), 1.0 / np.sqrt(HD)), np.ones((NH, 1))])
    rope = np.stack([np.tile(f(ang), (2, 1)) * scale for f in (np.cos, np.sin)]).astype(np.float32)
    return {
        "c_ident": np.eye(P, dtype=np.float32), "c_sel": sel, "c_mask": mask,
        "c_rope": rope, "c_iota": np.arange(NE, dtype=np.float32),
    }


def kernel(**inputs):
    import numpy as _np
    import concourse.bacc as _bacc
    from concourse import mybir as _mybir
    from concourse.bass_utils import run_bass_kernel_spmd as _run

    nc = _bacc.Bacc("TRN2", target_bir_lowering=False, num_devices=1)
    arrays, tensors = {}, {}
    for name, value in {**inputs, **_constants()}.items():
        a = _np.ascontiguousarray(value)
        arrays[f"in_{name}"] = a
        tensors[name] = nc.dram_tensor(f"in_{name}", a.shape, _mybir.dt.from_np(a.dtype), kind="ExternalInput").ap()
    shape, dtype = _OUTS[0]
    out = nc.dram_tensor("out_0", shape, _mybir.dt.from_np(_np.dtype(dtype)), kind="ExternalOutput").ap()
    hybrid_block_kernel(nc, tensors, out)
    r = _run(nc, [arrays], core_ids=[0])
    return r.results[0]["out_0"]
```

```python
from contextlib import ExitStack
import math

import concourse.bass as bass
from concourse import mybir

P = 128
F32 = mybir.dt.float32
BF16 = mybir.dt.bfloat16
U32 = mybir.dt.uint32
ALU = mybir.AluOpType
ACT = mybir.ActivationFunctionType
AX_X = mybir.AxisListType.X


def hybrid_block_kernel(nc, t, out):
    B, S, C = t["L0_attn_a_x"].shape
    T = B * S
    NT = T // P
    NCH, CT = 4, NT // 4
    CW = CT * P
    BPC = CW // S
    DI, NS = t["L0_attn_a_A_log"].shape
    KC = t["L0_attn_a_conv_w"].shape[1]
    NE, _, FI = t["L0_ffn_We1"].shape
    NI = FI // P
    RH = t["L0_ffn_Wr1"].shape[1]
    NH, HD = 16, C // 16
    NG, GH = 4, 4
    QT = S // P
    EPS = 1e-5
    assert C == P and DI == 2 * P and BPC == 2 and QT == 2 and NG * GH == NH

    with ExitStack() as ctx:
        def sb(name, shape, dt=F32):
            return ctx.enter_context(nc.sbuf_tensor(name, shape, dt))

        def sem(name):
            return ctx.enter_context(nc.semaphore(name))

        bank = [ctx.enter_context(nc.psum_tensor(f"bank{i}", [P, 512], F32)) for i in range(8)]

        X = sb("X", [P, NT, C])
        D = sb("D", [P, NT, C])
        U = sb("U", [P, NT, C])
        SQ = sb("SQ", [P, NT * C])
        xT = SQ
        arena = sb("arena", [P, 4 * 2 * T])
        ident = sb("ident", [P, P])
        identb = sb("identb", [P, P], BF16)
        sel = sb("sel", [P, 2 * NS], BF16)
        cmask = sb("cmask", [P, 512], BF16)
        stage = sb("stage", [P, 2, CT, C])
        xnT = sb("xnT", [P, 2, CW])

        st_sum = sb("st_sum", [P, NT])
        st_mean = sb("st_mean", [P, NT])
        st_sd = sb("st_sd", [P, NT])
        st_r = sb("st_r", [P, NT])

        def part(k):
            return arena[:, k * 2 * T:(k + 1) * 2 * T].rearrange("p (h t) -> p h t", h=2)
        xc, zs, dt_, dtx = part(0), part(1), part(2), part(3)
        w_nat = sb("w_nat", [P, 4 * C + 2 * DI + DI + DI + P])
        win_n = w_nat[:, 0:512].rearrange("p (e d) -> p e d", e=4)
        wdt_n = w_nat[:, 512:1024].rearrange("p (e d) -> p e d", e=2)
        wbc_n = w_nat[:, 1024:1280]
        wout_n = w_nat[:, 1280:1536]
        NX = NE + 1
        winT = sb("winT", [P, 4, P])
        wdtT = sb("wdtT", [P, 2, 2, P])
        wboT = sb("wboT", [P, 4, P])
        nw = sb("nw", [P, 1])
        nb = sb("nb", [P, 1])
        cw = sb("cw", [P, 2, KC])
        cb = sb("cb", [P, 2])
        bdt = sb("bdt", [P, 2])
        Dv = sb("Dv", [P, 2])
        Am = sb("Am", [P, 2, NS])
        xpad = sb("xpad", [P, 2, 2, BPC, S + KC - 1])
        conv = sb("conv", [P, 2, 2, CW])
        BCs = sb("BCs", [P, T], BF16)
        bcr = sb("bcr", [P, 2, CW])
        bcm = sb("bcm", [P, 2, CW], BF16)
        NR = 4
        decay = sb("decay", [P, NR, BPC, S])
        xpad_f = xpad[:].rearrange("p s h b t -> p (s h b t)")
        inp = xpad_f[:, 0:NR * CW].rearrange("p (s t) -> p s t", s=NR)
        hst = conv[:].rearrange("p s h t -> p (s h) t")
        Csb = bcr
        ybuf = xnT

        NB, UB = -(-((2 * T + NE * (P - 1)) // P) // 4) * 4, 4
        EW = FI + NI + NI * C + C
        SW = C + 1
        w1 = sb("w1", [P, FI])
        w2 = sb("w2", [P, NI, C])
        bs2 = sb("bs2", [P, C])
        we = sb("we", [P, NE, EW])
        b1n = w_nat[0:NX * NI, 1536:1536 + P]
        b1s = sb("b1s", [P, NI])
        wr1 = sb("wr1", [P, RH])
        wr2 = sb("wr2", [RH, NE])
        br1 = sb("br1", [RH, 1])
        br2 = sb("br2", [P, NE])
        r1 = ybuf[0:RH, :, :]
        tri = sb("tri", [P, P])
        ones = sb("ones", [P, P])
        iota = sb("iota", [P, NB])
        iotaP = sb("iotaP", [P, NT])
        fresh = sb("fresh", [P, NE, NT])
        dest = sb("dest", [P, 2, NT])
        gate = w_nat[:, 0:128].rearrange("p (n e) -> p n e", n=NT)
        gex = w_nat[:, 128:256].rearrange("p (n e) -> p n e", n=NT)
        gmx = sb("gmx", [P, NT])
        gsum = sb("gsum", [P, NT])
        top8 = sb("top8", [P, NT, 8])
        idx8 = sb("idx8", [P, NT, 8], U32)
        idxf = sb("idxf", [P, NT, 2])
        wk = sb("wk", [P, 4, NT])
        pick = w_nat[:, 1216:1472].rearrange("p (q n e) -> p q n e", q=2, n=NT)
        both = w_nat[:, 256:384].rearrange("p (n e) -> p n e", n=NT)
        tot = w_nat[:, 512:640].rearrange("p (e n) -> p e n", e=NE)
        run = w_nat[:, 640:768].rearrange("p (e n) -> p e n", e=NE)
        more = w_nat[:, 768:896].rearrange("p (e n) -> p e n", e=NE)
        nblk = sb("nblk", [P, NE])
        endb = sb("endb", [P, NE])
        begb = sb("begb", [P, NE])
        posn = w_nat[:, 384:512].rearrange("p (n e) -> p n e", n=NT)
        slotf = sb("slotf", [P, 2, NT])
        slot = sb("slot", [P, 2, NT], U32)
        past = w_nat[:, 896:1216].rearrange("p (b e) -> p b e", b=NB)
        ebf = sb("ebf", [P, NB])
        eb = sb("eb", [P, NB], mybir.dt.int32)
        hole = sb("hole", [P, SW])
        pay = arena[:, 8192:8192 + 2 * NT * SW].rearrange("p (q n w) -> p q n w", q=2, n=NT)
        yin = arena[:, 8192:8192 + 2 * NT * C].rearrange("p (q n c) -> p q n c", q=2, n=NT)
        wst = arena[:, 8192:8192 + UB * EW].rearrange("p (s w) -> p s w", s=UB)
        at = 8192 + max(UB * EW, 2 * NT * SW)
        xrow = arena[:, at:at + UB * SW].rearrange("p (s w) -> p s w", s=UB)
        at += UB * SW
        xbT = arena[:, at:at + UB * P].rearrange("p (s w) -> p s w", s=UB)
        assert at + UB * P <= 16384
        hbT = conv[:].rearrange("p s h t -> p (s h t)").rearrange("p (s i t) -> p s i t", s=UB, i=NI)
        hsT = [decay[:].rearrange("p r b t -> p (r b t)").rearrange("p (i t) -> p i t", i=NI),
               xpad_f[:, 0:NI * CW].rearrange("p (i t) -> p i t", i=NI)]
        yrow = bcr[:].rearrange("p s t -> p (s t)")[:, 0:UB * C].rearrange("p (s c) -> p s c", s=UB)
        drow = sb("drow", [P, UB], U32)
        slots = [nc.dram_tensor(f"slots{k}", [NB * P, SW], F32).ap() for k in range(2)]
        results = nc.dram_tensor("results", [2 * T, C], F32).ap()

        wat = sb("wat", [P, 3 * C])
        ra = arena[:, 8192:8320].rearrange("p (h i) -> p h i", h=2 * NH)
        rb = arena[:, 8320:8448].rearrange("p (h i) -> p h i", h=2 * NH)
        wqk = sb("wqk", [P, 2 * NH, 32])
        bat = arena[0:1, 9888:9888 + 2 * C]
        rope = arena[:, 10144:10400].rearrange("p (q h i) -> p q h i", q=2, h=2 * NH)
        bra = arena[0:1, 8448:8576].rearrange("p (h i) -> p h i", h=2 * NH)
        brb = arena[0:1, 8576:8704].rearrange("p (h i) -> p h i", h=2 * NH)
        sel_f = arena[:, 9728:9728 + 2 * NS]
        cmask_f = arena[:, 9760:9760 + P]
        bqk_r = arena[0:1, 8704:9728].rearrange("p (h d) -> p h d", d=32)
        one1 = sb("one1", [1, 1])
        bqk = sb("bqk", [P, 2 * NG])
        bv = sb("bv", [P, C])
        bpj = sb("bpj", [P, C])
        wpj = sb("wpj", [P, C])
        qblk = arena[:, 0:8192].rearrange("p (s g j t) -> p s g j t", s=2, g=NG, j=GH)
        PR = arena[:, 8192:8192 + 3072].rearrange("p (s n) -> p s n", s=2)
        PT = arena[:, 11264:11264 + 3072].rearrange("p (s n) -> p s n", s=2)
        kT = arena[:, 14336:16384].rearrange("p (s g t) -> p s g t", s=2, g=NG)
        va = U[:].rearrange("p n c -> p (n c)").rearrange("p (s q h d) -> p s q h d", s=2, q=QT, h=NH)
        ngm = sb("ngm", [P, 2, QT, GH])
        conv_f = conv[:].rearrange("p s h t -> p (s h t)")
        oT = conv_f[:, 0:2 * S].rearrange("p (s t) -> p s t", s=2)
        rden = sb("rden", [P, 2, QT, GH])
        yat = conv_f[:, 2 * S:4 * S].rearrange("p (s q h d) -> p s q h d", s=2, q=QT, h=NH)
        yT = conv_f[:, 4 * S:6 * S].rearrange("p (s t) -> p s t", s=2)

        ld_x = sem("ld_x")
        ld_a = sem("ld_a")
        ld_f = sem("ld_f")
        ld_b = sem("ld_b")
        n_ld = {"x": 0, "a": 0, "f": 0, "b": 0}
        st_hole = sem("st_hole")
        st_zero = sem("st_zero")
        st_wbc = sem("st_wbc")
        st_tr = sem("st_tr")
        st_cp = sem("st_cp")
        st_const = sem("st_const")
        st_A = sem("st_A")
        st_rope = sem("st_rope")
        st_bq = sem("st_bq")
        st_bqc = sem("st_bqc")
        st_qz = sem("st_qz")
        s_out = sem("s_out")

        def chunk(c, n=CT):
            return bass.ds(c * n, n)

        def cols(c, n=CW):
            return bass.ds(c * n, n)

        def bcast(ap, n):
            return ap.unsqueeze(ap.ndim).broadcast_to(list(ap.shape) + [n])

        act_steps = sem("act_steps")
        pool_steps = sem("pool_steps")

        def apart(engine, steps=act_steps):
            engine.sem_inc(steps, 1)

        LN = {k: {q: sem(f"{k}_{q}") for q in ("m", "c", "q", "v", "s", "r")} for k in ("ln0", "ln1", "lnf0", "lnb", "lnf1")}

        def ln_vector(v, k, src, dst):
            s = LN[k]
            nc.vector.tensor_reduce(st_sum[:], src, AX_X, ALU.add).then_inc(s["m"], 1)
            v.wait_ge(s["m"], 1)
            nc.vector.tensor_scalar(st_mean[:], st_sum[:], 1.0 / C, None, ALU.mult).then_inc(s["m"], 1)
            v.wait_ge(s["m"], 2)
            nc.vector.tensor_tensor(dst, src, bcast(st_mean[:], C), ALU.subtract).then_inc(s["c"], 1)
            v.wait_ge(s["q"], 1)
            nc.vector.tensor_reduce(st_sum[:], SQ[:].rearrange("p (n c) -> p n c", c=C), AX_X,
                                    ALU.add).then_inc(s["v"], 1)
            v.wait_ge(s["s"], 1)
            nc.vector.reciprocal(st_r[:], st_sd[:]).then_inc(s["r"], 1)
            v.wait_ge(s["r"], 1)

        def ln_scalar(a, k, src):
            s = LN[k]
            a.wait_ge(s["c"], 1)
            nc.scalar.activation(SQ[:], src[:].rearrange("p n c -> p (n c)"), ACT.Square).then_inc(s["q"], 1)
            a.wait_ge(s["v"], 1)
            nc.scalar.activation(st_sd[:], st_sum[:], ACT.Sqrt, bias=eps_t[:, 0:1], scale=1.0 / C).then_inc(s["s"], 1)

        eps_t = sb("eps_t", [P, 1])
        one_t = sb("one_t", [P, 1])

        m1_st, m1_tr, m1_xn, m1_xz, m1_xe, m1_ze, m1_cd, m1_cv, m1_xc = (
            sem("m1_" + q) for q in ("st", "tr", "xn", "xz", "xe", "ze", "cd", "cv", "xc"))
        m2_mm, m2_ab, m2_ex, m2_re, m2_hi, m2_r, m2_md, m2_st, m2_ln = (
            sem("m2_" + q) for q in ("mm", "ab", "ex", "re", "hi", "r", "md", "st", "ln"))
        m3_dt, m3_dx, m3_a, m3_bb, m3_cb, m3_cs, m3_b, m3_sc, m3_hc, m3_ns, m3_ya, m3_y, m3_o, m3_x = (
            sem("m3_" + q) for q in ("dt", "dx", "a", "bb", "cb", "cs", "b", "sc", "hc", "ns", "ya", "y", "o", "x"))
        FS = {q: sem(f"f_{q}") for q in (
            "st", "tr", "xt", "r1", "r1s", "lg", "g", "ge", "ga", "mk", "pf", "ix", "eb", "py", "sc",
            "l1", "h", "l2", "x", "ld0", "ld1", "ld2", "ld3", "bt", "bx", "wc", "b1", "bh", "b2", "by", "bd", "so0", "so1", "so2", "so3", "yl", "dn")}
        RUN = dict(st=NCH, tr=NCH, xt=NCH, r1=NCH, r1s=NCH, lg=NCH, g=2 * NT + 26, ge=2, ga=2, mk=1, pf=2, ix=1, eb=1,
                   py=4, sc=16 * 2 * NT, l1=NCH * NI, h=NCH * NI, l2=NCH, x=NCH + 1, ld=16 * NB // UB, bt=NB, bx=NB, wc=NB,
                   b1=NB, bh=NB, b2=NB, by=NB, bd=NB, so=16 * NB // UB, yl=16 * 2 * NCH, dn=2 * NT)
        AS = {q: sem(f"a_{q}") for q in ("st", "tr", "ln", "q", "k", "v", "ve", "s", "m", "se", "t", "te", "o", "oe",
                                         "ot", "rd", "y", "yt", "ye", "p", "x", "xb")}


        def each_block(engine, step):
            with engine.Fori(0, NB // UB - 1) as i:
                for j in range(UB):
                    step(i, j)
            for j in range(UB):
                step(NB // UB - 1, j)

        def exists(i, j):
            return j < UB or not isinstance(i, int)

        def ffn_scalar(a, k, ln):
            f = FS
            ln_scalar(a, ln, D)
            with a.Fori(0, NCH // 2) as i:
                for s in range(2):
                    c = 2 * i + s
                    a.wait_ge(f["tr"], c + 1 + 2 + k * RUN["tr"])
                    apart(a)
                    nc.scalar.activation(xT[:, cols(c)], bank[6 + s][:], ACT.Copy).then_inc(f["xt"], 1)
                    a.wait_ge(f["r1"], c + 1 + k * RUN["r1"])
                    nc.scalar.activation(r1[:, s, :], bank[3 + s][0:RH, :], ACT.Relu,
                                         bias=br1[:, 0:1]).then_inc(f["r1s"], 1)
            a.wait_ge(f["ge"], 1 + k * RUN["ge"])
            nc.scalar.activation(gex[:], gex[:], ACT.Exp).then_inc(f["ga"], 1)
            a.wait_ge(f["ge"], 2 + k * RUN["ge"])
            nc.scalar.activation(wk[:, 1, :], wk[:, 0, :], ACT.Exp, scale=1.0 / 2).then_inc(f["ga"], 1)
            with a.Fori(0, NCH // 2) as i:
                for s in range(2):
                    c = 2 * i + s
                    a.wait_ge(f["l2"], c + 1 + k * RUN["l2"])
                    for b in range(NI):
                        a.wait_ge(f["l1"], c * NI + b + 1 + k * RUN["l1"])
                        nc.scalar.activation(hsT[s][:, b, :], bank[b][:], ACT.Silu,
                                             bias=b1s[:, b:b + 1]).then_inc(f["h"], 1)

            def x_out(i, j):
                a.wait_ge(f["bt"], i * UB + j + 1 + UB + k * RUN["bt"])
                nc.scalar.activation(xbT[:, j % UB, :], bank[j % 2][:, 0:P], ACT.Copy).then_inc(f["bx"], 1)

            def hidden(i, j):
                a.wait_ge(f["wc"], i * UB + j + 1 + k * RUN["wc"])
                a.wait_ge(f["b1"], i * UB + j + 1 + k * RUN["b1"])
                for b in range(NI):
                    last = nc.scalar.activation(hbT[:, j % UB, b, :], bank[2 + j % 2][:, b * P:(b + 1) * P], ACT.Silu,
                                                bias=wst[:, j % UB, FI + b:FI + b + 1])
                last.then_inc(f["bh"], 1)

            def step(i, j):
                if exists(i, j + 2):
                    x_out(i, j + 2)
                if exists(i, j + 1):
                    hidden(i, j + 1)

            x_out(0, 0)
            x_out(0, 1)
            hidden(0, 0)
            each_block(a, step)

        def ffn_pool(p, k):
            f = FS
            p.wait_ge(LN["lnf0" if k == 0 else "lnf1"]["r"], 1)
            for q in range(2):
                nc.gpsimd.tensor_tensor(pay[:, q, :, 0:C], D[:], bcast(st_r[:], C), ALU.mult).then_inc(f["py"], 1)
                nc.gpsimd.tensor_copy(pay[:, q, :, C], dest[:, q, :]).then_inc(f["py"], 1)
            for u in range(UB):
                p.wait_ge(f[f"so{u}"], 16 + k * RUN["so"])
            p.wait_ge(f["py"], 4 + k * RUN["py"])
            p.wait_ge(f["ix"], 1 + k * RUN["ix"])
            for n in range(NT):
                for q in range(2):
                    nc.gpsimd.indirect_dma_start(slots[k], bass.IndirectOffsetOnAxis(ap=slot[:, q, n:n + 1], axis=0),
                                                 pay[:, q, n, :], None).then_inc(f["sc"], 16)
            with p.Fori(0, NB // UB) as i:
                for u in range(UB):
                    n = i * UB + u
                    p.wait_ge(f["by"], n + 1 + UB + k * RUN["by"])
                    apart(p, pool_steps)
                    nc.gpsimd.indirect_dma_start(results, bass.IndirectOffsetOnAxis(ap=drow[:, u:u + 1], axis=0),
                                                 yrow[:, u, :], None, bounds_check=2 * T - 1,
                                                 oob_is_err=False).then_inc(f[f"so{u}"], 16)

        def ffn_sync(sp, k):
            f = FS
            sp.wait_ge(f["sc"], 16 * 2 * NT + k * RUN["sc"])
            with sp.Fori(0, NB // UB) as i:
                for u in range(UB):
                    n = i * UB + u
                    sp.wait_ge(f["bt"], n + 1 + k * RUN["bt"])
                    sp.wait_ge(f["bd"], n + 1 + k * RUN["bd"])
                    sp.dma_start(xrow[:, u, :], slots[k][bass.ds(n * P, P), :]).then_inc(f[f"ld{u}"], 16)
            for u in range(UB):
                sp.wait_ge(f[f"so{u}"], 16 * (NB // UB) + 16 + k * RUN["so"])
            yv = results.rearrange("(q n p) c -> p q n c", q=2, p=P)
            for c in range(NCH):
                for q in range(2):
                    sp.dma_start(yin[:, q, c * CT:(c + 1) * CT, :],
                                 yv[:, q, c * CT:(c + 1) * CT, :]).then_inc(f["yl"], 16)

        def ffn_vector(v, k, ln):
            f = FS
            ln_vector(v, ln, X[:], D[:])
            with v.Fori(0, NCH // 2) as i:
                for s in range(2):
                    c = 2 * i + s
                    v.wait_ge(f["tr"], c + 1 + k * RUN["tr"])
                    nc.vector.tensor_tensor(stage[:, s, :, :], D[:, chunk(c), :], bcast(st_r[:, chunk(c)], C),
                                            ALU.mult).then_inc(f["st"], 1)
            g = [k * RUN["g"]]

            def then(ins):
                ins.then_inc(f["g"], 1)
                g[0] += 1
                v.wait_ge(f["g"], g[0])

            logits = bank[5][:, 0:NT * NE].rearrange("p (n e) -> p n e", e=NE)
            v.wait_ge(f["lg"], NCH + k * RUN["lg"])
            then(nc.vector.tensor_tensor(gate[:], logits, br2[:].unsqueeze(1).broadcast_to([P, NT, NE]), ALU.add))
            then(nc.vector.tensor_reduce(gmx[:], gate[:], AX_X, ALU.max))
            nc.vector.tensor_tensor(gex[:], gate[:], bcast(gmx[:], NE), ALU.subtract).then_inc(f["ge"], 1)
            v.wait_ge(f["ga"], 1 + k * RUN["ga"])
            then(nc.vector.tensor_reduce(gsum[:], gex[:], AX_X, ALU.add))
            then(nc.vector.reciprocal(gmx[:], gsum[:]))
            then(nc.vector.tensor_tensor(gate[:], gex[:], bcast(gmx[:], NE), ALU.mult))
            for n in range(NT):
                nc.vector.max(top8[:, n, :], gate[:, n, :]).then_inc(f["g"], 1)
            g[0] += NT
            for n in range(NT):
                v.wait_ge(f["g"], g[0] - NT + n + 1)
                nc.vector.max_index(idx8[:, n, :], top8[:, n, :], gate[:, n, :]).then_inc(f["g"], 1)
            g[0] += NT
            nc.vector.tensor_tensor(wk[:, 0, :], top8[:, :, 1], top8[:, :, 0], ALU.subtract).then_inc(f["ge"], 1)
            v.wait_ge(f["g"], g[0])
            then(nc.vector.tensor_copy(idxf[:], idx8[:, :, 0:2]))
            for q in range(2):
                nc.vector.tensor_tensor(pick[:, q, :, :], iota[:, 0:NE].unsqueeze(1).broadcast_to([P, NT, NE]),
                                        bcast(idxf[:, :, q], NE), ALU.is_equal).then_inc(f["g"], 1)
            g[0] += 2
            v.wait_ge(f["g"], g[0])
            nc.vector.tensor_tensor(both[:], pick[:, 0, :, :], pick[:, 1, :, :], ALU.add).then_inc(f["mk"], 1)
            v.wait_ge(f["ga"], 2 + k * RUN["ga"])
            then(nc.vector.tensor_scalar(wk[:, 2, :], wk[:, 1, :], 1.0, None, ALU.add))
            then(nc.vector.reciprocal(wk[:, 3, :], wk[:, 2, :]))
            then(nc.vector.tensor_tensor(wk[:, 2, :], wk[:, 3, :], wk[:, 1, :], ALU.mult))
            v.wait_ge(f["pf"], 2 + k * RUN["pf"])
            then(nc.vector.tensor_copy(tot[:], bank[7][:, 0:NT * NE].rearrange("p (n e) -> p e n", e=NE)))
            then(nc.vector.tensor_tensor_scan(run[:].rearrange("p e n -> p (e n)"),
                                              fresh[:].rearrange("p e n -> p (e n)"),
                                              tot[:].rearrange("p e n -> p (e n)"), 0.0, ALU.mult, ALU.add))
            then(nc.vector.tensor_tensor(more[:], run[:, :, NT - 1:NT].broadcast_to([P, NE, NT]),
                                         iotaP[:].unsqueeze(1).broadcast_to([P, NE, NT]), ALU.is_gt))
            then(nc.vector.tensor_reduce(nblk[:], more[:], AX_X, ALU.add))
            then(nc.vector.tensor_tensor_scan(endb[:], ones[:, 0:NE], nblk[:], 0.0, ALU.mult, ALU.add))
            then(nc.vector.tensor_tensor(begb[:], endb[:], nblk[:], ALU.subtract))
            then(nc.vector.tensor_tensor(run[:], run[:], tot[:], ALU.subtract))
            then(nc.vector.scalar_tensor_tensor(out=more[:], in0=bcast(begb[:], NT), scalar=float(P), in1=run[:],
                                                op0=ALU.mult, op1=ALU.add))
            then(nc.vector.tensor_tensor(posn[:], bank[6][:, 0:NT * NE].rearrange("p (n e) -> p n e", e=NE),
                                         more[:].rearrange("p e n -> p n e"), ALU.add))
            for q in range(2):
                nc.vector.tensor_tensor(pick[:, q, :, :], pick[:, q, :, :], posn[:], ALU.mult).then_inc(f["g"], 1)
            g[0] += 2
            v.wait_ge(f["g"], g[0])
            then(nc.vector.tensor_reduce(slotf[:], pick[:], AX_X, ALU.add))
            nc.vector.tensor_copy(slot[:], slotf[:]).then_inc(f["ix"], 1)
            then(nc.vector.tensor_tensor(past[:], endb[:].unsqueeze(1).broadcast_to([P, NB, NE]), bcast(iota[:], NE),
                                         ALU.is_le))
            then(nc.vector.tensor_reduce(ebf[:], past[:], AX_X, ALU.add))
            then(nc.vector.tensor_scalar(ebf[:], ebf[:], NE - 1.0, float(EW), ALU.min, ALU.mult))
            nc.vector.tensor_copy(eb[:], ebf[:]).then_inc(f["eb"], 1)

            for c in range(NCH):
                v.wait_ge(f["l2"], c + 1 + 2 + k * RUN["l2"])
                nc.vector.tensor_tensor(X[:, c * CT:(c + 1) * CT, :], bank[4 + c % 2][:].rearrange("p (n c) -> p n c", c=C),
                                        X[:, c * CT:(c + 1) * CT, :], ALU.add).then_inc(f["x"], 1)
            v.wait_ge(f["x"], NCH + 2 + k * RUN["x"])
            nc.vector.tensor_tensor(X[:], X[:], bs2[:].unsqueeze(1).broadcast_to([P, NT, C]), ALU.add)\
                .then_inc(f["x"], 1)

            flat = we[:].rearrange("p e w -> p (e w)")

            def weights(i, j, first=False):
                if not first:
                    v.wait_ge(f["b2"], i * UB + j - 1 + k * RUN["b2"])
                    v.wait_ge(f["by"], i * UB + j + 1 + k * RUN["by"])
                col = v.value_load(eb[0:1, bass.ds(i * UB + j, 1)] if not isinstance(i, int) else
                                   eb[0:1, i * UB + j:i * UB + j + 1], min_val=0, max_val=(NE - 1) * EW)
                nc.vector.tensor_copy(wst[:, j % UB, :], flat[:, bass.ds(col, EW)]).then_inc(f["wc"], 1)

            def where(i, j):
                it = i + j // UB
                v.wait_ge(f[f"so{j % UB}"], 16 * (it + 1) + k * RUN["so"])
                v.wait_ge(f[f"ld{j % UB}"], 16 * (it + 1) + k * RUN["ld"])
                nc.vector.tensor_copy(drow[:, j % UB:j % UB + 1], xrow[:, j % UB, C:SW]).then_inc(f["bd"], 1)

            def result(i, j):
                v.wait_ge(f["b2"], i * UB + j + 1 + 2 + k * RUN["b2"])
                nc.vector.tensor_tensor(yrow[:, j % UB, :], bank[4 + j % 2][:, 0:C], wst[:, j % UB, EW - C:EW],
                                        ALU.add).then_inc(f["by"], 1)

            def step(i, j):
                if exists(i, j + 1):
                    where(i, j + 1)
                result(i, j)
                if exists(i, j + UB - 1):
                    weights(i, j + UB - 1)

            v.wait_ge(f["eb"], 1 + k * RUN["eb"])
            v.wait_ge(f["sc"], 16 * 2 * NT + k * RUN["sc"])
            for j in range(UB - 1):
                weights(0, j, first=True)
            where(0, 0)
            each_block(v, step)
            v.wait_ge(f["yl"], 16 * 2 * NCH + k * RUN["yl"])
            v.wait_ge(f["x"], NCH + 2 + 1 + k * RUN["x"])
            for q in range(2):
                if q:
                    v.wait_ge(f["dn"], NT + k * RUN["dn"])
                for n in range(NT):
                    nc.vector.scalar_tensor_tensor(out=X[:, n, :], in0=yin[:, q, n, :], scalar=wk[:, 3 - q, n:n + 1],
                                                   in1=X[:, n, :], op0=ALU.mult, op1=ALU.add).then_inc(f["dn"], 1)
            v.wait_ge(f["dn"], 2 * NT + k * RUN["dn"])
            assert g[0] == (k + 1) * RUN["g"]

        def ffn_tensor(pe, k):
            f = FS
            with pe.Fori(0, NCH // 2) as i:
                for s in range(2):
                    c = 2 * i + s
                    pe.wait_ge(f["st"], c + 1 + k * RUN["st"])
                    pe.wait_ge(f["xt"], c + 1 + k * RUN["xt"])
                    for n in range(CT):
                        last = nc.tensor.transpose(bank[6 + s][:, n * P:(n + 1) * P], stage[:, s, n, :], ident[:])
                    last.then_inc(f["tr"], 1)
                    pe.wait_ge(f["xt"], c + 1 + 2 + k * RUN["xt"])
                    nc.tensor.matmul(bank[3 + s][0:RH, :], wr1[:], xT[:, cols(c)], start=True, stop=True)\
                        .then_inc(f["r1"], 1)
                    pe.wait_ge(f["r1s"], c + 1 + k * RUN["r1s"])
                    for n in range(CT):
                        last = nc.tensor.matmul(bank[5][:, bass.ds(c * (CT * NE) + n * NE, NE)],
                                                r1[:, s, n * P:(n + 1) * P], wr2[:], start=True, stop=True)
                    last.then_inc(f["lg"], 1)

            def shared1(c):
                for b in range(NI):
                    pe.wait_ge(f["h"], c * NI + b + 1 + k * RUN["h"])
                    nc.tensor.matmul(bank[b][:], w1[:, b * P:(b + 1) * P], xT[:, c * CW:(c + 1) * CW],
                                     start=True, stop=True).then_inc(f["l1"], 1)

            def shared2(c):
                pe.wait_ge(f["h"], c * NI + NI + NI + k * RUN["h"])
                pe.wait_ge(f["x"], c + 1 + k * RUN["x"])
                for n in range(CT):
                    for b in range(NI):
                        last = nc.tensor.matmul(bank[4 + c % 2][:, n * C:(n + 1) * C],
                                                hsT[c % 2][:, b, n * P:(n + 1) * P], w2[:, b, :],
                                                start=(b == 0), stop=(b == NI - 1))
                last.then_inc(f["l2"], 1)

            pe.wait_ge(f["g"], 1 + k * RUN["g"])
            shared1(0)
            shared1(1)
            shared2(0)
            pe.wait_ge(f["mk"], 1 + k * RUN["mk"])
            flat = both[:].rearrange("p n e -> p (n e)")
            nc.tensor.matmul(bank[6][:, 0:NT * NE], tri[:], flat, start=True, stop=True).then_inc(f["pf"], 1)
            nc.tensor.matmul(bank[7][:, 0:NT * NE], ones[:], flat, start=True, stop=True).then_inc(f["pf"], 1)
            for c in range(2, NCH):
                shared1(c)
                shared2(c - 1)
            shared2(NCH - 1)
            pe.wait_ge(f["h"], NCH * NI + NI + k * RUN["h"])

            def turn(i, j):
                pe.wait_ge(f[f"ld{j % UB}"], 16 * (i + j // UB + 1) + k * RUN["ld"])
                pe.wait_ge(f["bx"], i * UB + j + 1 + k * RUN["bx"])
                nc.tensor.transpose(bank[j % 2][:, 0:P], xrow[:, j % UB, 0:C], ident[:]).then_inc(f["bt"], 1)

            def layer1(i, j):
                n = i * UB + j
                pe.wait_ge(f["wc"], n + 1 + k * RUN["wc"])
                pe.wait_ge(f["bx"], n + 1 + 2 + k * RUN["bx"])
                pe.wait_ge(f["bh"], n + 1 + k * RUN["bh"])
                for b in range(NI):
                    last = nc.tensor.matmul(bank[2 + j % 2][:, b * P:(b + 1) * P], wst[:, j % UB, b * P:(b + 1) * P],
                                            xbT[:, j % UB, :], start=True, stop=True)
                last.then_inc(f["b1"], 1)

            def layer2(i, j):
                n = i * UB + j
                pe.wait_ge(f["bh"], n + 1 + 2 + k * RUN["bh"])
                pe.wait_ge(f["by"], n + 3 + k * RUN["by"])
                for b in range(NI):
                    at = FI + NI + b * C
                    last = nc.tensor.matmul(bank[4 + j % 2][:, 0:C], hbT[:, j % UB, b, :], wst[:, j % UB, at:at + C],
                                            start=(b == 0), stop=(b == NI - 1))
                last.then_inc(f["b2"], 1)

            def step(i, j):
                if exists(i, j + 2):
                    turn(i, j + 2)
                if exists(i, j + 1):
                    layer1(i, j + 1)
                layer2(i, j)

            turn(0, 0)
            turn(0, 1)
            layer1(0, 0)
            each_block(pe, step)

        KU = QU = NG // 2
        SU, TU = KU + 3 * NG, QU + 3 * NG
        HQ = [(0, 0, GH), (1, 0, GH // 2), (1, GH // 2, GH // 2)]

        def s_bank(s, u):
            return bank[(SU * s + u) % 4]

        def t_bank(u):
            return bank[4 + u % 2]

        def probs(s, g, qt):
            kw = (qt + 1) * P
            return PR[:, g % 2, GH * P * qt:GH * P * qt + GH * kw].rearrange("p (j k) -> p j k", k=kw)

        def probsT(g, kt):
            qw = S - kt * P
            at = 0 if kt == 0 else GH * S
            return PT[:, g % 2, at:at + GH * qw].rearrange("p (j q) -> p j q", q=qw)

        def attention_scalar(a):
            f = AS
            ln_scalar(a, "lnb", D)

            def exps(b, s, g):
                a.wait_ge(f["t"], b * 3 * NG + 3 * g + 3)
                for r, (qt, j0, nj) in enumerate(HQ):
                    a.wait_ge(f["m"], b * 3 * NG + 3 * g + r + 1)
                    kw = (qt + 1) * P
                    for j in range(nj):
                        last = nc.scalar.activation(probs(s, g, qt)[:, j0 + j, :],
                                                    s_bank(s, KU + 3 * g + r)[:, j * kw:(j + 1) * kw], ACT.Exp,
                                                    bias=ngm[:, g % 2, qt, j0 + j:j0 + j + 1])
                    last.then_inc(f["se"], 1)

            def o_out(b, s, g):
                a.wait_ge(f["ot"], b * NG + g + 1)
                a.wait_ge(f["o"], b * NG + g + 1 + 2)
                nc.scalar.activation(oT[:, g % 2, :], bank[6][:, 0:S], ACT.Copy).then_inc(f["oe"], 1)

            with a.Fori(0, B // 2) as i:
                for s in range(2):
                    b = 2 * i + s
                    a.wait_ge(f["tr"], b + 1)
                    nc.scalar.activation(xnT[:, s, 0:S], bank[7][:, 0:S], ACT.Copy).then_inc(f["ln"], 1)
                    for u in range(KU):
                        a.wait_ge(f["k"], b * KU + u + 1)
                        for w in range(2):
                            g = 2 * u + w
                            last = nc.scalar.activation(kT[:, s, g, :], s_bank(s, u)[:, w * S:(w + 1) * S],
                                                        ACT.Identity, bias=bqk[:, NG + g:NG + g + 1])
                        last.then_inc(f["se"], 1)
                    exps(b, s, 0)
                    exps(b, s, 1)
                    exps(b, s, 2)
                    o_out(b, s, 0)
                    exps(b, s, 3)
                    for g in range(1, NG):
                        o_out(b, s, g)
                    a.wait_ge(f["yt"], b + 1)
                    nc.scalar.activation(yT[:, s, :], bank[7][:, 0:S], ACT.Copy).then_inc(f["ye"], 1)

        def attention_vector(v):
            f = AS
            ln_vector(v, "lnb", X[:], D[:])

            def maxima(b, s, g):
                v.wait_ge(f["se"], b * SU + 3 * g + 3)
                for r, (qt, j0, nj) in enumerate(HQ):
                    v.wait_ge(f["s"], b * 3 * NG + 3 * g + r + 1)
                    sc = s_bank(s, KU + 3 * g + r)[:].rearrange("p (j k) -> p j k", j=nj)
                    nc.vector.tensor_reduce(ngm[:, g % 2, qt, j0:j0 + nj], sc, AX_X, ALU.max,
                                            negate=True).then_inc(f["m"], 1)

            def pt_out(b, s, g):
                v.wait_ge(f["o"], b * NG + g + 1)
                for r, dst in enumerate((probsT(g, 0)[:, :, 0:P], probsT(g, 0)[:, :, P:S], probsT(g, 1))):
                    v.wait_ge(f["t"], b * 3 * NG + 3 * g + r + 1 + 6)
                    nc.vector.tensor_copy(dst, t_bank(QU + 3 * g + r)[:].rearrange("p (j q) -> p j q", q=P))\
                        .then_inc(f["te"], 1)

            def norm(b, s, g):
                v.wait_ge(f["ot"], b * NG + g + 1 + 2)
                o = bank[7][:, (g % 2) * S:(g % 2 + 1) * S].rearrange("p (qt j d) -> p qt j d", qt=QT, j=GH)
                nc.vector.reciprocal(rden[:, g % 2, :, :], o[:, :, :, HD]).then_inc(f["rd"], 1)
                v.wait_ge(f["rd"], b * NG + g + 1)
                nc.vector.tensor_tensor(yat[:, s, :, GH * g:GH * (g + 1), :], o[:, :, :, 0:HD],
                                        bcast(rden[:, g % 2, :, :], HD), ALU.mult).then_inc(f["y"], 1)

            with v.Fori(0, B // 2) as i:
                for s in range(2):
                    b = 2 * i + s
                    nc.vector.tensor_tensor(stage[:, s, 0:QT, :], D[:, chunk(b, QT), :], bcast(st_r[:, chunk(b, QT)], C),
                                            ALU.mult).then_inc(f["st"], 1)
                for s in range(2):
                    b = 2 * i + s
                    for u in range(QU):
                        v.wait_ge(f["q"], b * QU + u + 1)
                        for j in range(GH):
                            r = slice(32 * j, 32 * j + 32)
                            last = nc.vector.tensor_tensor(
                                qblk[r, s, 2 * u:2 * u + 2, j, :], t_bank(u)[r, :].rearrange("p (w t) -> p w t", w=2),
                                bcast(bqk[r, 2 * u:2 * u + 2], S), ALU.add)
                        last.then_inc(f["te"], 1)
                    v.wait_ge(f["v"], b + 1)
                    nc.vector.tensor_tensor(
                        va[:, s, :, :, 0:HD], bank[6][:, 0:S].rearrange("p (q h d) -> p q h d", q=QT, h=NH),
                        bv[:].rearrange("p (h d) -> p h d", h=NH).unsqueeze(1).broadcast_to([P, QT, NH, HD]),
                        ALU.add).then_inc(f["ve"], 1)
                    maxima(b, s, 0)
                    maxima(b, s, 1)
                    pt_out(b, s, 0)
                    maxima(b, s, 2)
                    pt_out(b, s, 1)
                    maxima(b, s, 3)
                    norm(b, s, 0)
                    pt_out(b, s, 2)
                    norm(b, s, 1)
                    pt_out(b, s, 3)
                    norm(b, s, 2)
                    norm(b, s, 3)
                    v.wait_ge(f["p"], b + 1)
                    xb = X[:, chunk(b, QT), :]
                    nc.vector.tensor_tensor(xb, bank[7][:, S:2 * S].rearrange("p (q c) -> p q c", q=QT), xb,
                                            ALU.add).then_inc(f["x"], 1)
                    v.wait_ge(f["x"], b + 1 + 1)
                    nc.vector.tensor_tensor(xb, xb, bpj[:].unsqueeze(1).broadcast_to([P, QT, C]),
                                            ALU.add).then_inc(f["xb"], 1)
            v.wait_ge(f["xb"], B)

        def attention_tensor(pe):
            f = AS

            def scores(b, s, g):
                for r, (qt, j0, nj) in enumerate(HQ):
                    u = KU + 3 * g + r
                    kw = (qt + 1) * P
                    pe.wait_ge(f["se"], b * SU + u + 1)
                    for j in range(nj):
                        nc.tensor.matmul(s_bank(s, u)[:, j * kw:(j + 1) * kw], qblk[:, s, g, j0 + j, qt * P:(qt + 1) * P],
                                         kT[:, s, g, 0:kw], start=(j == 0), stop=False)
                    diag = s_bank(s, u)[:].rearrange("p (j k) -> p j k", j=nj)[:, :, qt * P:(qt + 1) * P]
                    nc.tensor.matmul(diag, identb[:], cmask[:, 0:nj * P].rearrange("p (j k) -> p j k", j=nj),
                                     start=False, stop=True).then_inc(f["s"], 1)

            def transposes(b, s, g):
                for r, (qt, kt) in enumerate(((0, 0), (1, 0), (1, 1))):
                    if r < 2:
                        pe.wait_ge(f["se"], b * SU + KU + 3 * g + (1, 3)[r] + 4)
                    pe.wait_ge(f["te"], b * TU + QU + 3 * g + r + 1)
                    for j in range(GH):
                        last = nc.tensor.transpose(t_bank(QU + 3 * g + r)[:, j * P:(j + 1) * P],
                                                   probs(s, g, qt)[:, j, kt * P:(kt + 1) * P], ident[:])
                    last.then_inc(f["t"], 1)

            def pv(b, s, g):
                pe.wait_ge(f["te"], b * TU + QU + 3 * g + 3 + 2)
                if g == 0:
                    pe.wait_ge(f["ve"], b + 1)
                pe.wait_ge(f["oe"], b * NG + g + 1)
                for kt in range(QT):
                    for j in range(GH):
                        last = nc.tensor.matmul(bank[6][32 * j:32 * j + 32, kt * P:S], va[:, s, kt, GH * g + j, :],
                                                probsT(g, kt)[:, j, :], start=(kt == 0), stop=(kt == QT - 1),
                                                tile_position=(0, 32 * j), skip_group_check=True)
                last.then_inc(f["o"], 1)

            def o_transposes(b, s, g):
                pe.wait_ge(f["oe"], b * NG + g + 1 + 1)
                if g > 0:
                    pe.wait_ge(f["y"], b * NG + g)
                for qt in range(QT):
                    at = (g % 2) * S + qt * P
                    last = nc.tensor.transpose(bank[7][:, at:at + P], oT[:, g % 2, qt * P:(qt + 1) * P], ident[:])
                last.then_inc(f["ot"], 1)

            with pe.Fori(0, B // 2) as i:
                for s in range(2):
                    b = 2 * i + s
                    pe.wait_ge(f["st"], b + 1)
                    pe.wait_ge(f["x"], b + 1)
                    for q in range(QT):
                        last = nc.tensor.transpose(bank[7][:, q * P:(q + 1) * P], stage[:, s, q, :], ident[:])
                    last.then_inc(f["tr"], 1)
                    pe.wait_ge(f["ln"], b + 1)
                    for u in range(QU):
                        pe.wait_ge(f["te"], b * TU + u + 1)
                        for w in range(2):
                            last = nc.tensor.matmul(t_bank(u)[:, w * S:(w + 1) * S],
                                                    wqk[:, GH * (2 * u + w):GH * (2 * u + w + 1), :],
                                                    xnT[:, s, 0:S], start=True, stop=True)
                        last.then_inc(f["q"], 1)
                    for u in range(KU):
                        pe.wait_ge(f["se"], b * SU + u + 1)
                        for w in range(2):
                            h0 = NH + GH * (2 * u + w)
                            last = nc.tensor.matmul(s_bank(s, u)[:, w * S:(w + 1) * S], wqk[:, h0:h0 + GH, :],
                                                    xnT[:, s, 0:S], start=True, stop=True)
                        last.then_inc(f["k"], 1)
                    pe.wait_ge(f["oe"], b * NG + 1)
                    for q in range(QT):
                        last = nc.tensor.matmul(bank[6][:, q * P:(q + 1) * P], xnT[:, s, q * P:(q + 1) * P],
                                                wat[:, 2 * C:3 * C], start=True, stop=True)
                    last.then_inc(f["v"], 1)
                    pe.wait_ge(f["te"], b * TU + QU + 2)
                    pe.wait_ge(f["se"], b * SU + KU + 4)
                    scores(b, s, 0)
                    scores(b, s, 1)
                    transposes(b, s, 0)
                    scores(b, s, 2)
                    pv(b, s, 0)
                    transposes(b, s, 1)
                    scores(b, s, 3)
                    o_transposes(b, s, 0)
                    pv(b, s, 1)
                    transposes(b, s, 2)
                    o_transposes(b, s, 1)
                    pv(b, s, 2)
                    transposes(b, s, 3)
                    o_transposes(b, s, 2)
                    pv(b, s, 3)
                    o_transposes(b, s, 3)
                    pe.wait_ge(f["y"], b * NG + NG)
                    for q in range(QT):
                        last = nc.tensor.transpose(bank[7][:, q * P:(q + 1) * P],
                                                   yat[:, s, q, :, :].rearrange("p h d -> p (h d)"), ident[:])
                    last.then_inc(f["yt"], 1)
                    pe.wait_ge(f["ye"], b + 1)
                    for q in range(QT):
                        last = nc.tensor.matmul(bank[7][:, S + q * P:S + (q + 1) * P], yT[:, s, q * P:(q + 1) * P],
                                                wpj[:], start=True, stop=True)
                    last.then_inc(f["p"], 1)

        block = ctx.enter_context(nc.Block())

        @block.sync
        def _(sp):
            xv = t["L0_attn_a_x"].rearrange("b (q p) c -> p (b q) c", p=P)
            for c in range(NCH):
                sp.dma_start(X[:, c * CT:(c + 1) * CT, :], xv[:, c * CT:(c + 1) * CT, :]).then_inc(ld_x, 16)

            def load(key, s, dst, src, **how):
                sp.dma_start(dst, src, **how).then_inc(s, 16)
                n_ld[key] += 16

            def rows(v):
                return v.rearrange("(a n) -> a n", a=1)

            def column(dst, v, h=1):
                load("a", ld_a, dst, v.rearrange("(h p) -> p h", h=h), allow_slow_non_contiguous=True)

            load("a", ld_a, ident[:], t["c_ident"])
            load("a", ld_a, win_n, t["L0_attn_a_W_in"].rearrange("(e p) d -> p e d", p=P))
            column(nw[:], t["L0_attn_a_norm_w"])
            column(nb[:], t["L0_attn_a_norm_b"])
            load("a", ld_a, cw[:], t["L0_attn_a_conv_w"].rearrange("(h p) k -> p h k", h=2))
            column(cb[:], t["L0_attn_a_conv_b"], 2)
            load("a", ld_a, wdt_n, t["L0_attn_a_W_dt"].rearrange("(e p) d -> p e d", p=P))
            column(bdt[:], t["L0_attn_a_b_dt"], 2)
            column(Dv[:], t["L0_attn_a_D"], 2)
            load("a", ld_a, Am[:], t["L0_attn_a_A_log"].rearrange("(h p) n -> p h n", h=2))
            load("a", ld_a, wout_n, t["L0_attn_a_W_out"])
            load("a", ld_a, sel_f, t["c_sel"])
            sp.wait_ge(st_wbc, 1)
            for q in range(3):
                load("a", ld_a, wbc_n[32 * q:32 * q + NS, :], t["L0_attn_a_W_B"])
                load("a", ld_a, wbc_n[32 * q + NS:32 * q + 2 * NS, :], t["L0_attn_a_W_C"])

            load("f", ld_f, w1[:], t["L0_ffn_Ws1"])
            load("f", ld_f, w2[:], t["L0_ffn_Ws2"].rearrange("(i p) c -> p i c", p=P))
            load("f", ld_f, bs2[:], t["L0_ffn_bs2"].partition_broadcast(P))
            load("f", ld_f, b1n[0:NI, :], t["L0_ffn_bs1"].rearrange("(i p) -> i p", p=P))
            load("f", ld_f, b1n[NI:NX * NI, :], t["L0_ffn_be1"].rearrange("e (i p) -> (e i) p", p=P))
            load("f", ld_f, we[:, :, 0:FI], t["L0_ffn_We1"].rearrange("e c i -> c e i"))
            for e in range(NE):
                load("f", ld_f, we[:, e, FI + NI:EW - C].rearrange("p (i c) -> p i c", c=C),
                     t["L0_ffn_We2"][e].rearrange("(i p) c -> p i c", p=P))
                load("f", ld_f, we[:, e, EW - C:EW], t["L0_ffn_be2"][e].partition_broadcast(P))
            load("f", ld_f, wr1[:], t["L0_ffn_Wr1"])
            load("f", ld_f, wr2[:], t["L0_ffn_Wr2"])
            load("f", ld_f, br1[:], t["L0_ffn_br1"].rearrange("(p a) -> p a", a=1))
            load("f", ld_f, br2[:], t["L0_ffn_br2"].partition_broadcast(P))
            load("f", ld_f, iota[:], t["c_iota"].partition_broadcast(P))
            load("f", ld_f, iotaP[:], t["c_iotaP"].partition_broadcast(P))
            load("f", ld_f, fresh[:], t["c_fresh"].partition_broadcast(P))
            load("f", ld_f, dest[:], t["c_dest"])
            load("f", ld_f, tri[:], t["c_tri"])

            load("b", ld_b, wat[:], t["L0_attn_b_W_attn"])
            load("b", ld_b, rope, t["c_rope"].partition_broadcast(P))
            load("b", ld_b, bat, rows(t["L0_attn_b_b_attn"])[:, 0:2 * C])
            load("b", ld_b, bv[:], t["L0_attn_b_b_attn"][2 * C:3 * C].partition_broadcast(P))
            load("b", ld_b, bpj[:], t["L0_attn_b_b_proj"].partition_broadcast(P))
            load("b", ld_b, wpj[:], t["L0_attn_b_W_proj"])
            load("b", ld_b, cmask_f, t["c_mask"])

            ffn_sync(sp, 0)
            ffn_sync(sp, 1)
            ov = out.rearrange("b (q p) c -> p (b q) c", p=P)
            for c in range(NCH):
                sp.wait_ge(FS["dn"], NT + (c + 1) * CT + RUN["dn"])
                sp.dma_start(ov[:, c * CT:(c + 1) * CT, :], X[:, c * CT:(c + 1) * CT, :]).then_inc(s_out, 16)
            sp.wait_ge(s_out, 16 * NCH)

        LOADED_A, LOADED_F, LOADED_B = n_ld["a"], n_ld["f"], n_ld["b"]

        @block.gpsimd
        def _(pool):
            pool.sem_inc(m3_hc, 4)
            nc.gpsimd.memset(hole[:, 0:C], 0.0).then_inc(st_hole, 1)
            nc.gpsimd.memset(hole[:, C:SW], float(4 * T)).then_inc(st_hole, 1)
            pool.wait_ge(st_hole, 2)
            half = NB // 2
            for u in range(UB):
                nc.gpsimd.dma_start(slots[u // 2].rearrange("(n p) w -> p n w", p=P)[:, u % 2 * half:(u % 2 + 1) * half, :],
                                    hole[:].unsqueeze(1).broadcast_to([P, half, SW])).then_inc(FS[f"so{u}"], 16)
            nc.gpsimd.memset(wbc_n, 0.0).then_inc(st_wbc, 1)
            nc.gpsimd.memset(eps_t[:], EPS).then_inc(st_zero, 1)
            nc.gpsimd.memset(one_t[:], 1.0).then_inc(st_zero, 1)
            nc.gpsimd.memset(xpad[:], 0.0).then_inc(st_zero, 1)
            nc.gpsimd.memset(decay[:, :, :, 0:1], 0.0).then_inc(st_zero, 1)
            pool.wait_ge(st_wbc, 1)
            nc.gpsimd.memset(wqk[:], 0.0).then_inc(st_zero, 1)
            nc.gpsimd.memset(bqk_r, 0.0).then_inc(st_zero, 1)
            nc.gpsimd.memset(one1[:], 1.0).then_inc(st_zero, 1)
            nc.gpsimd.memset(ones[:], 1.0).then_inc(st_zero, 1)

            pool.wait_ge(ld_a, LOADED_A)
            nc.gpsimd.tensor_copy(identb[:], ident[:]).then_inc(st_const, 1)
            nc.gpsimd.tensor_copy(sel[:], sel_f).then_inc(st_const, 1)
            pool.wait_ge(ld_b, LOADED_B)
            nc.gpsimd.tensor_copy(cmask[:].rearrange("p (j k) -> p j k", k=P),
                                  cmask_f.unsqueeze(1).broadcast_to([P, 512 // P, P])).then_inc(st_const, 1)

            pool.wait_ge(ld_b, LOADED_B)
            n = 0
            for w, wa, wb, o in ((wat[:, 0:2 * C], ra, rb, wqk[:, :, 0:HD]),
                                 (bat, bra, brb, bqk_r[:, :, 0:HD])):
                p = w.shape[0]
                pair = w.rearrange("p (h i two) -> p h i two", h=2 * NH, two=2)
                turned = o.rearrange("p h (i two) -> p h i two", two=2)
                cos, sin = rope[0:p, 0, :, :], rope[0:p, 1, :, :]
                for first, second, op in ((0, 1, ALU.subtract), (1, 0, ALU.add)):
                    nc.gpsimd.tensor_tensor(wa, pair[:, :, :, first], cos, ALU.mult).then_inc(st_rope, 1)
                    nc.gpsimd.tensor_tensor(wb, pair[:, :, :, second], sin, ALU.mult).then_inc(st_rope, 1)
                    n += 2
                    pool.wait_ge(st_rope, n)
                    nc.gpsimd.tensor_tensor(turned[:, :, :, first], wa, wb, op).then_inc(st_rope, 1)
                    n += 1
                    pool.wait_ge(st_rope, n)

            with pool.Fori(0, NCH) as c:
                for n in range(NS):
                    pool.wait_ge(m3_cs, c * NS + n + 1 + 2)
                    for h in range(2):
                        k = 2 * n + h
                        pool.wait_ge(m3_sc, c * 2 * NS + k + 1 + NR)
                        nc.gpsimd.tensor_tensor(hst[:, k % NR, :], hst[:, k % NR, :], Csb[:, n % 2, :],
                                                ALU.mult).then_inc(m3_hc, 1)

            pool.wait_ge(m3_x, 2 * NCH)
            nc.gpsimd.memset(arena[:, 0:8192], 0.0).then_inc(st_qz, 1)
            nc.gpsimd.memset(va, 0.0).then_inc(st_qz, 1)
            pool.wait_ge(st_qz, 2)
            nc.gpsimd.memset(va[:, :, :, :, HD:HD + 1], 1.0).then_inc(st_qz, 1)
            ffn_pool(pool, 0)
            ffn_pool(pool, 1)

        @block.scalar
        def _(act):
            act.sem_inc(m1_xe, 4)
            act.sem_inc(m1_ze, 2)
            act.sem_inc(m1_xc, 4)
            act.sem_inc(m2_ab, 4)
            act.sem_inc(m2_hi, 2)
            act.sem_inc(m3_cs, 2)
            act.sem_inc(FS["xt"], 2)
            act.sem_inc(FS["h"], NI)
            act.sem_inc(FS["bx"], 2)
            act.sem_inc(FS["bh"], 2)
            act.sem_inc(AS["se"], 4)
            act.sem_inc(AS["oe"], 1)
            act.wait_ge(st_zero, 8)
            ln_scalar(act, "ln0", U)
            ln_scalar(act, "ln1", D)
            act.wait_ge(ld_a, LOADED_A)

            with act.Fori(0, NCH // 2) as i:
                for s in range(2):
                    c = 2 * i + s
                    act.wait_ge(m1_tr, c + 1 + 2)
                    nc.scalar.activation(xnT[:, s, :], bank[6 + s][:], ACT.Identity, bias=nb[:, 0:1],
                                         scale=nw[:, 0:1]).then_inc(m1_xn, 1)
                    act.wait_ge(m1_cv, 2 * c + 2)
                    for h in range(2):
                        act.wait_ge(m1_xz, 4 * c + h + 1)
                        nc.scalar.activation(xpad[:, s, h, :, KC - 1:KC - 1 + S],
                                             bank[2 * s + h][:].rearrange("p (b t) -> p b t", b=BPC),
                                             ACT.Copy).then_inc(m1_xe, 1)
                    for h in range(2):
                        act.wait_ge(m1_xz, 4 * c + 2 + h + 1)
                        apart(act)
                        nc.scalar.activation(zs[:, h, cols(c)], bank[4 + h][:], ACT.Silu).then_inc(m1_ze, 1)
                for s in range(2):
                    c = 2 * i + s
                    for h in range(2):
                        act.wait_ge(m1_cv, 2 * c + h + 1 + 4)
                        apart(act)
                        nc.scalar.activation(xc[:, h, cols(c)], conv[:, s, h, :], ACT.Silu).then_inc(m1_xc, 1)

            nc.scalar.activation(Am[:], Am[:], ACT.Exp).then_inc(st_A, 1)

            with act.Fori(0, NCH // 2) as i:
                for s in range(2):
                    c = 2 * i + s
                    for h in range(2):
                        act.wait_ge(m2_mm, 3 * c + h + 1)
                        apart(act)
                        nc.scalar.activation(dt_[:, h, cols(c)], bank[2 * s + h][:], ACT.Abs,
                                             bias=bdt[:, h:h + 1]).then_inc(m2_ab, 1)
                    act.wait_ge(m2_mm, 3 * c + 3)
                    apart(act)
                    nc.scalar.activation(BCs[:, cols(c)], bank[4 + s][:], ACT.Copy).then_inc(m2_hi, 1)
                    for h in range(2):
                        act.wait_ge(m2_ab, 2 * c + h + 1 + 4)
                        apart(act)
                        nc.scalar.activation(dt_[:, h, cols(c)], dt_[:, h, cols(c)], ACT.Exp,
                                             scale=-1.0).then_inc(m2_ex, 1)
            act.wait_ge(m2_ex, 2 * NCH)
            for h in range(2):
                nc.scalar.activation(dt_[:, h, :], dt_[:, h, :], ACT.Ln, bias=one_t[:, 0:1]).then_inc(m2_ln, 1)

            with act.Fori(0, NCH) as c:
                act.wait_ge(st_A, 2)
                for n in range(NS):
                    act.wait_ge(m3_cb, c * NS + n + 1)
                    act.wait_ge(m3_hc, c * 2 * NS + 2 * n + 2)
                    nc.scalar.activation(Csb[:, n % 2, :], bank[2 + n % 2][:], ACT.Copy).then_inc(m3_cs, 1)
                    for h in range(2):
                        k = 2 * n + h
                        act.wait_ge(m3_dt, 2 * c + h + 1)
                        act.wait_ge(m3_sc, c * 2 * NS + k + 1)
                        apart(act)
                        nc.scalar.activation(decay[:, k % NR, :, 1:S],
                                             dt_[:, h, cols(c)].rearrange("p (b t) -> p b t", b=BPC)[:, :, 1:S],
                                             ACT.Exp, scale=Am[:, h, n:n + 1]).then_inc(m3_a, 1)

            ffn_scalar(act, 0, "lnf0")
            attention_scalar(act)
            ffn_scalar(act, 1, "lnf1")

        @block.vector
        def _(v):
            v.sem_inc(m1_cv, 4)
            v.sem_inc(m2_re, 4)
            v.sem_inc(m2_r, 2)
            v.sem_inc(m3_sc, NR)
            v.sem_inc(m3_b, 4)
            v.sem_inc(m3_ya, 2)
            v.sem_inc(FS["x"], 2)
            v.sem_inc(FS["by"], UB)
            v.sem_inc(FS["bd"], UB)
            v.sem_inc(AS["te"], 2)
            v.sem_inc(AS["x"], 1)

            v.wait_ge(ld_x, 16 * NCH)
            ln_vector(v, "ln0", X[:], U[:])
            nc.vector.tensor_tensor(U[:], U[:], bcast(st_r[:], C), ALU.mult).then_inc(LN["ln0"]["r"], 1)
            v.wait_ge(LN["ln0"]["r"], 2)
            ln_vector(v, "ln1", U[:], D[:])

            for n, dst in enumerate((winT[:].rearrange("p a b -> p (a b)"), wdtT[:].rearrange("p a b c -> p (a b c)"),
                                     wboT[:].rearrange("p a b -> p (a b)"))):
                v.wait_ge(st_tr, n + 1)
                nc.vector.tensor_copy(dst, bank[n][:, 0:dst.shape[1]]).then_inc(st_cp, 1)
            v.wait_ge(st_tr, 4)
            nc.vector.tensor_copy(b1s[:], bank[3][:, 0:NI]).then_inc(st_cp, 1)
            nc.vector.tensor_copy(we[:, :, FI:FI + NI], bank[3][:, NI:NX * NI].rearrange("p (e i) -> p e i", i=NI))\
                .then_inc(st_cp, 1)
            v.wait_ge(st_bq, 1)
            nc.vector.tensor_copy(bqk[:], bank[4][:, 0:2 * NG]).then_inc(st_bqc, 1)
            v.wait_ge(ld_a, LOADED_A)

            with v.Fori(0, NCH // 2) as i:
                for s in range(2):
                    c = 2 * i + s
                    v.wait_ge(m1_tr, c + 1)
                    nc.vector.tensor_tensor(stage[:, s, :, :], D[:, chunk(c), :], bcast(st_r[:, chunk(c)], C),
                                            ALU.mult).then_inc(m1_st, 1)
                for s in range(2):
                    c = 2 * i + s
                    for k in range(KC):
                        for h in range(2):
                            src = xpad[:, s, h, :, k:k + S]
                            dst = conv[:, s, h, :].rearrange("p (b t) -> p b t", b=BPC)
                            if k == 0:
                                v.wait_ge(m1_xe, 2 * c + h + 1 + 4)
                                v.wait_ge(m1_xc, 2 * c + h + 1)
                                nc.vector.tensor_scalar(dst, src, cw[:, h, 0:1], cb[:, h:h + 1], ALU.mult,
                                                        ALU.add).then_inc(m1_cd, 1)
                                continue
                            v.wait_ge(m1_cd, c * (2 * KC - 2) + 2 * k + h - 1)
                            last = nc.vector.scalar_tensor_tensor(out=dst, in0=src, scalar=cw[:, h, k:k + 1], in1=dst,
                                                                  op0=ALU.mult, op1=ALU.add)
                            last.then_inc(m1_cd if k < KC - 1 else m1_cv, 1)

            v.wait_ge(st_A, 1)
            nc.vector.tensor_scalar(Am[:], Am[:], -1.0, None, ALU.mult).then_inc(st_A, 1)

            with v.Fori(0, NCH // 2) as i:
                for s in range(2):
                    c = 2 * i + s
                    for h in range(2):
                        v.wait_ge(m2_ab, 2 * c + h + 1 + 4)
                        nc.vector.tensor_scalar(dtx[:, h, cols(c)], bank[2 * s + h][:], bdt[:, h:h + 1], 0.0, ALU.add,
                                                ALU.max).then_inc(m2_re, 1)
                    v.wait_ge(m2_hi, c + 1 + 2)
                    nc.vector.tensor_tensor(bcr[:, s, :], bank[4 + s][:], BCs[:, cols(c)], ALU.subtract)\
                        .then_inc(m2_r, 1)
                    v.wait_ge(m2_r, c + 1 + 2)
                    nc.vector.tensor_copy(bcm[:, s, :], bcr[:, s, :]).then_inc(m2_md, 1)
                    v.wait_ge(m2_md, c + 1)
                    nc.vector.tensor_copy(BCs[32:64, cols(c)], bcm[32:64, s, :]).then_inc(m2_st, 1)
                    nc.vector.tensor_tensor(BCs[64:96, cols(c)], bcr[64:96, s, :], bcm[64:96, s, :],
                                            ALU.subtract).then_inc(m2_st, 1)

            with v.Fori(0, NCH) as c:
                for h in range(2):
                    v.wait_ge(m2_ln, h + 1)
                    nc.vector.tensor_tensor(dt_[:, h, cols(c)], dt_[:, h, cols(c)], dtx[:, h, cols(c)], ALU.add)\
                        .then_inc(m3_dt, 1)
                for h in range(2):
                    v.wait_ge(m3_dt, 2 * c + h + 1)
                    nc.vector.tensor_tensor(dtx[:, h, cols(c)], dt_[:, h, cols(c)], xc[:, h, cols(c)], ALU.mult)\
                        .then_inc(m3_dx, 1)

                def inputs(k):
                    n, h = k // 2, k % 2
                    if k < 2:
                        v.wait_ge(m3_dx, 2 * c + h + 1)
                    v.wait_ge(m3_sc, c * 2 * NS + k + 1)
                    v.wait_ge(m3_bb, c * NS + n + 1)
                    nc.vector.tensor_tensor(inp[:, k % NR, :], bank[n % 2][:], dtx[:, h, cols(c)], ALU.mult)\
                        .then_inc(m3_b, 1)

                inputs(0)
                for k in range(2 * NS):
                    if k + 1 < 2 * NS:
                        inputs(k + 1)
                    v.wait_ge(m3_a, c * 2 * NS + k + 1)
                    v.wait_ge(m3_ns, c * 2 * NS + k + 1)
                    v.wait_ge(m3_b, c * 2 * NS + k + 1 + 4)
                    nc.vector.tensor_tensor_scan(hst[:, k % NR, :], decay[:, k % NR, :, :].rearrange("p b t -> p (b t)"),
                                                 inp[:, k % NR, :], 0.0, ALU.mult, ALU.add).then_inc(m3_sc, 1)
                for h in range(2):
                    v.wait_ge(m3_ns, c * 2 * NS + 2 * NS - 1 + h + NR)
                    nc.vector.scalar_tensor_tensor(out=ybuf[:, h, :], in0=xc[:, h, cols(c)], scalar=Dv[:, h:h + 1],
                                                   in1=bank[4 + h][:], op0=ALU.mult, op1=ALU.add).then_inc(m3_ya, 1)
                for h in range(2):
                    v.wait_ge(m3_ya, 2 * c + h + 1 + 2)
                    nc.vector.tensor_tensor(ybuf[:, h, :], ybuf[:, h, :], zs[:, h, cols(c)], ALU.mult)\
                        .then_inc(m3_y, 1)
                v.wait_ge(m3_o, c + 1)
                nc.vector.tensor_tensor(U[:, chunk(c), :], bank[6][:].rearrange("p (n c) -> p n c", c=C),
                                        U[:, chunk(c), :], ALU.add).then_inc(m3_x, 1)
                v.wait_ge(m3_x, 2 * c + 1)
                nc.vector.tensor_tensor(X[:, chunk(c), :], X[:, chunk(c), :], U[:, chunk(c), :], ALU.add)\
                    .then_inc(m3_x, 1)
            v.wait_ge(m3_x, 2 * NCH)
            ffn_vector(v, 0, "lnf0")
            v.wait_ge(st_qz, 3)
            attention_vector(v)
            ffn_vector(v, 1, "lnf1")

        @block.tensor
        def _(pe):
            pe.sem_inc(m1_tr, 2)
            pe.sem_inc(m3_ns, NR)
            pe.sem_inc(FS["tr"], 2)
            pe.sem_inc(FS["l2"], 2)
            pe.sem_inc(FS["bt"], UB)
            pe.sem_inc(FS["b2"], 2)
            pe.sem_inc(AS["t"], 6)
            pe.sem_inc(AS["o"], 2)
            pe.sem_inc(AS["ot"], 2)

            pe.wait_ge(ld_a, LOADED_A)
            for e in range(4):
                last = nc.tensor.transpose(bank[0][:, e * P:(e + 1) * P], win_n[:, e, :], ident[:])
            last.then_inc(st_tr, 1)
            for e in range(2):
                for d in range(2):
                    last = nc.tensor.transpose(bank[1][:, (2 * e + d) * P:(2 * e + d + 1) * P],
                                               wdt_n[:, e, d * P:(d + 1) * P], ident[:])
            last.then_inc(st_tr, 1)
            for d in range(2):
                nc.tensor.transpose(bank[2][:, d * P:(d + 1) * P], wbc_n[:, d * P:(d + 1) * P], ident[:])
            for d in range(2):
                last = nc.tensor.transpose(bank[2][:, (2 + d) * P:(3 + d) * P], wout_n[:, d * P:(d + 1) * P], ident[:])
            last.then_inc(st_tr, 1)
            pe.wait_ge(ld_f, LOADED_F)
            nc.tensor.transpose(bank[3][:, 0:NX * NI], b1n, ident[0:NX * NI, 0:NX * NI]).then_inc(st_tr, 1)
            pe.wait_ge(st_const, 3)
            pe.wait_ge(st_rope, 12)
            pe.wait_ge(st_zero, 8)
            for g in range(2 * NG):
                last = nc.tensor.matmul(bank[4][:, g:g + 1], bqk_r[:, GH * g:GH * (g + 1), :], one1[:],
                                        start=True, stop=True)
            last.then_inc(st_bq, 1)
            pe.wait_ge(st_cp, 5)
            pe.wait_ge(st_bqc, 1)

            with pe.Fori(0, NCH // 2) as i:
                for s in range(2):
                    c = 2 * i + s
                    pe.wait_ge(m1_st, c + 1)
                    for n in range(CT):
                        last = nc.tensor.transpose(bank[6 + s][:, n * P:(n + 1) * P], stage[:, s, n, :], ident[:])
                    last.then_inc(m1_tr, 1)
                for s in range(2):
                    c = 2 * i + s
                    pe.wait_ge(m1_xn, c + 1)
                    for e in range(4):
                        if e < 2:
                            dst = bank[2 * s + e]
                            pe.wait_ge(m1_xe, 2 * c + e + 1)
                        else:
                            dst = bank[4 + e - 2]
                            pe.wait_ge(m1_ze, 2 * c + e - 2 + 1)
                        nc.tensor.matmul(dst[:], winT[:, e, :], xnT[:, s, :], start=True, stop=True).then_inc(m1_xz, 1)

            pe.wait_ge(m1_xc, 2 * NCH + 4)
            with pe.Fori(0, NCH // 2) as i:
                for s in range(2):
                    c = 2 * i + s
                    for e in range(2):
                        pe.wait_ge(m2_ab, 2 * c + e + 1)
                        pe.wait_ge(m2_re, 2 * c + e + 1)
                        for d in range(2):
                            last = nc.tensor.matmul(bank[2 * s + e][:], wdtT[:, e, d, :], xc[:, d, cols(c)],
                                                    start=(d == 0), stop=(d == 1))
                        last.then_inc(m2_mm, 1)
                    pe.wait_ge(m2_hi, c + 1)
                    pe.wait_ge(m2_r, c + 1)
                    for d in range(2):
                        last = nc.tensor.matmul(bank[4 + s][:], wboT[:, d, :], xc[:, d, cols(c)],
                                                start=(d == 0), stop=(d == 1))
                    last.then_inc(m2_mm, 1)

            pe.wait_ge(m2_st, 2 * NCH)
            with pe.Fori(0, NCH) as c:
                def spread(n):
                    for what, (s_free, need, s_done) in enumerate(
                            ((m3_b, c * 2 * NS + 2 * n + 2, m3_bb), (m3_cs, c * NS + n + 1, m3_cb))):
                        pe.wait_ge(s_free, need)
                        col = what * NS + n
                        nc.tensor.matmul(bank[2 * what + n % 2][:], sel[:, col:col + 1].broadcast_to([P, P]),
                                         BCs[:, cols(c)], start=True, stop=True).then_inc(s_done, 1)

                def sum_states(n):
                    for h in range(2):
                        k = 2 * n + h
                        if n == 0:
                            pe.wait_ge(m3_ya, 2 * c + h + 1)
                        pe.wait_ge(m3_hc, c * 2 * NS + k + 1 + 4)
                        nc.tensor.matmul(bank[4 + h][:], ident[:], hst[:, k % NR, :], start=(n == 0),
                                         stop=(n == NS - 1)).then_inc(m3_ns, 1)

                spread(0)
                spread(1)
                for n in range(2, NS):
                    spread(n)
                    sum_states(n - 2)
                sum_states(NS - 2)
                sum_states(NS - 1)
                pe.wait_ge(m3_y, 2 * c + 2)
                for n in range(CT):
                    for h in range(2):
                        last = nc.tensor.matmul(bank[6][:, n * C:(n + 1) * C], ybuf[:, h, n * P:(n + 1) * P],
                                                wboT[:, 2 + h, :], start=(h == 0), stop=(h == 1))
                last.then_inc(m3_o, 1)

            ffn_tensor(pe, 0)
            pe.wait_ge(st_qz, 3)
            attention_tensor(pe)
            ffn_tensor(pe, 1)


_OUTS = [((8, 256, 128), "float32")]


def _constants():
    import numpy as np

    P, NS, NE, NH, HD = 128, 16, 8, 16, 8
    k = np.arange(P)
    sel = ((k[:, None] % 32 == np.arange(2 * NS)[None, :]) & (k[:, None] < 96)).astype(np.float32)
    mask = np.where(k[None, :] > k[:, None], -1e30, 0.0).astype(np.float32)
    theta = 1.0 / 10000.0 ** (np.arange(0, HD, 2, dtype=np.float32) / HD)
    ang = np.arange(NH, dtype=np.float32)[:, None] * theta[None, :].astype(np.float32)
    scale = np.concatenate([np.full((NH, 1), 1.0 / np.sqrt(HD)), np.ones((NH, 1))])
    rope = np.stack([np.tile(f(ang), (2, 1)) * scale for f in (np.cos, np.sin)]).astype(np.float32)
    return {
        "c_ident": np.eye(P, dtype=np.float32), "c_sel": sel, "c_mask": mask,
        "c_rope": rope, "c_iota": np.arange(40, dtype=np.float32),
        "c_iotaP": P * np.arange(16, dtype=np.float32),
        "c_fresh": np.tile((np.arange(16) > 0).astype(np.float32), (NE, 1)),
        "c_dest": (k[:, None, None] + P * np.arange(32).reshape(2, 16)[None]).astype(np.float32),
        "c_tri": (k[:, None] < k[None, :]).astype(np.float32),
    }


def kernel(**inputs):
    import numpy as _np
    import concourse.bacc as _bacc
    from concourse import mybir as _mybir
    from concourse.bass_utils import run_bass_kernel_spmd as _run

    nc = _bacc.Bacc("TRN2", target_bir_lowering=False, num_devices=1)
    arrays, tensors = {}, {}
    for name, value in {**inputs, **_constants()}.items():
        a = _np.ascontiguousarray(value)
        arrays[f"in_{name}"] = a
        tensors[name] = nc.dram_tensor(f"in_{name}", a.shape, _mybir.dt.from_np(a.dtype), kind="ExternalInput").ap()
    shape, dtype = _OUTS[0]
    out = nc.dram_tensor("out_0", shape, _mybir.dt.from_np(_np.dtype(dtype)), kind="ExternalOutput").ap()
    hybrid_block_kernel(nc, tensors, out)
    r = _run(nc, [arrays], core_ids=[0])
    return r.results[0]["out_0"]
```

```python
from contextlib import ExitStack
import math

import concourse.bass as bass
from concourse import mybir

P = 128
F32 = mybir.dt.float32
BF16 = mybir.dt.bfloat16
U32 = mybir.dt.uint32
ALU = mybir.AluOpType
ACT = mybir.ActivationFunctionType
AX_X = mybir.AxisListType.X


def hybrid_block_kernel(nc, t, out):
    B, S, C = t["L0_attn_a_x"].shape
    T = B * S
    NT = T // P
    NCH, CT = 4, NT // 4
    CW = CT * P
    BPC = CW // S
    DI, NS = t["L0_attn_a_A_log"].shape
    KC = t["L0_attn_a_conv_w"].shape[1]
    NE, _, FI = t["L0_ffn_We1"].shape
    NI = FI // P
    RH = t["L0_ffn_Wr1"].shape[1]
    NH, HD = 16, C // 16
    NG, GH = 4, 4
    QT = S // P
    EPS = 1e-5
    assert C == P and DI == 2 * P and BPC == 2 and QT == 2 and NG * GH == NH

    with ExitStack() as ctx:
        def sb(name, shape, dt=F32):
            return ctx.enter_context(nc.sbuf_tensor(name, shape, dt))

        def sem(name):
            return ctx.enter_context(nc.semaphore(name))

        bank = [ctx.enter_context(nc.psum_tensor(f"bank{i}", [P, 512], F32)) for i in range(8)]

        X = sb("X", [P, NT, C])
        D = sb("D", [P, NT, C])
        U = sb("U", [P, NT, C])
        SQ = sb("SQ", [P, NT * C])
        xT = SQ
        arena = sb("arena", [P, 4 * 2 * T])
        ident = sb("ident", [P, P])
        identb = sb("identb", [P, P], BF16)
        sel = sb("sel", [P, 2 * NS], BF16)
        cmask = sb("cmask", [P, 512], BF16)
        stage = sb("stage", [P, 2, CT, C])
        xnT = sb("xnT", [P, 2, CW])

        st_sum = sb("st_sum", [P, NT])
        st_neg = sb("st_neg", [P, NT])
        act_junk = sb("act_junk", [P, 1])
        st_ssq = sb("st_ssq", [P, NT])
        st_sd = sb("st_sd", [P, NT])
        st_r = sb("st_r", [P, NT])

        def part(k):
            return arena[:, k * 2 * T:(k + 1) * 2 * T].rearrange("p (h t) -> p h t", h=2)
        xc, zs, dt_, dtx = part(0), part(1), part(2), part(3)
        w_nat = sb("w_nat", [P, 4 * C + 2 * DI + DI + DI + P])
        win_n = w_nat[:, 0:512].rearrange("p (e d) -> p e d", e=4)
        wdt_n = w_nat[:, 512:1024].rearrange("p (e d) -> p e d", e=2)
        wbc_n = w_nat[:, 1024:1280]
        wout_n = w_nat[:, 1280:1536]
        NX = NE + 1
        winT = sb("winT", [P, 4, P])
        wdtT = sb("wdtT", [P, 2, 2, P])
        wboT = sb("wboT", [P, 4, P])
        nw = sb("nw", [P, 1])
        nb = sb("nb", [P, 1])
        cw = sb("cw", [P, 2, KC])
        cb = sb("cb", [P, 2])
        bdt = sb("bdt", [P, 2])
        Dv = sb("Dv", [P, 2])
        Am = sb("Am", [P, 2, NS])
        xpad = sb("xpad", [P, 2, 2, BPC, S + KC - 1])
        conv = sb("conv", [P, 2, 2, CW])
        BCs = sb("BCs", [P, T], BF16)
        bcr = sb("bcr", [P, 2, CW])
        bcm = sb("bcm", [P, 2, CW], BF16)
        NR = 4
        decay = sb("decay", [P, NR, BPC, S])
        xpad_f = xpad[:].rearrange("p s h b t -> p (s h b t)")
        inp = xpad_f[:, 0:NR * CW].rearrange("p (s t) -> p s t", s=NR)
        hst = conv[:].rearrange("p s h t -> p (s h) t")
        Csb = bcr
        ybuf = xnT

        NB, UB = -(-((2 * T + NE * (P - 1)) // P) // 8) * 8, 8
        WR = 4
        EW = FI + NI + NI * C + C
        w1 = sb("w1", [P, FI])
        w2 = sb("w2", [P, NI, C])
        bs2 = sb("bs2", [P, C])
        we = sb("we", [P, NE, EW])
        b1n = w_nat[0:NX * NI, 1536:1536 + P]
        b1s = sb("b1s", [P, NI])
        wr1 = sb("wr1", [P, RH])
        wr2 = sb("wr2", [RH, NE])
        br1 = sb("br1", [RH, 1])
        br2 = sb("br2", [P, NE])
        r1 = ybuf[0:RH, :, :]
        tri = sb("tri", [P, P])
        ones = sb("ones", [P, P])
        iota = sb("iota", [P, NB])
        starts = sb("starts", [P, NB + 1])
        lanes = sb("lanes", [P, P])
        iotaP = sb("iotaP", [P, NT])
        fresh = sb("fresh", [P, NE, NT])
        dest = sb("dest", [P, 2 * NT])
        gate = w_nat[:, 0:128].rearrange("p (n e) -> p n e", n=NT)
        gex = w_nat[:, 128:256].rearrange("p (n e) -> p n e", n=NT)
        gmx = sb("gmx", [P, NT])
        gsum = sb("gsum", [P, NT])
        top8 = sb("top8", [P, NT, 8])
        idx8 = sb("idx8", [P, NT, 8], U32)
        idxf = sb("idxf", [P, NT, 2])
        wk = sb("wk", [P, 4, NT])
        pick = w_nat[:, 1216:1472].rearrange("p (q n e) -> p q n e", q=2, n=NT)
        both = w_nat[:, 256:384].rearrange("p (n e) -> p n e", n=NT)
        tot = w_nat[:, 512:640].rearrange("p (e n) -> p e n", e=NE)
        run = w_nat[:, 640:768].rearrange("p (e n) -> p e n", e=NE)
        more = w_nat[:, 768:896].rearrange("p (e n) -> p e n", e=NE)
        nblk = sb("nblk", [P, NE])
        endb = sb("endb", [P, NE])
        begb = sb("begb", [P, NE])
        posn = w_nat[:, 384:512].rearrange("p (n e) -> p n e", n=NT)
        slotf = sb("slotf", [P, 2, NT])
        blk = sb("blk", [P, 2 * NT])
        lane = sb("lane", [P, 2 * NT])
        past = w_nat[:, 896:1216].rearrange("p (b e) -> p b e", b=NB)
        ebf = sb("ebf", [P, NB])
        eb = sb("eb", [P, NB], mybir.dt.int32)
        who = sb("who", [P, 3, NB])
        yin = arena[:, 8192:8192 + 2 * NT * C].rearrange("p (q n c) -> p q n c", q=2, n=NT)
        lane1 = arena[:, 8192:8192 + 2 * NT * P].rearrange("p (n j) -> p n j", j=P)
        at = 8192 + 2 * NT * P
        reach = arena[:, at:at + 2 * NT * (NB + 1)].rearrange("p (n b) -> p n b", b=NB + 1)
        at += 2 * NT * (NB + 1)
        blk1 = arena[:, at:at + 2 * NT * NB].rearrange("p (n b) -> p n b", b=NB)
        at += 2 * NT * NB
        assert at <= 16384
        wst = [arena[:, 8192 + u * EW:8192 + (u + 1) * EW] for u in range(WR)]
        at = 8192 + WR * EW
        xrow = arena[:, at:at + UB * C].rearrange("p (s w) -> p s w", s=UB)
        at += UB * C
        xbT = arena[:, at:at + WR * P].rearrange("p (s w) -> p s w", s=WR)
        assert at + WR * P <= 16384
        hbT = conv[:].rearrange("p s h t -> p (s h t)").rearrange("p (s i t) -> p s i t", s=WR, i=NI)
        hsT = [decay[:].rearrange("p r b t -> p (r b t)").rearrange("p (i t) -> p i t", i=NI),
               xpad_f[:, 0:NI * CW].rearrange("p (i t) -> p i t", i=NI)]
        yrow = bcr[:].rearrange("p s t -> p (s t)")[:, 0:UB * C].rearrange("p (s c) -> p s c", s=UB)
        trow = sb("trow", [P, UB], U32)
        drow = sb("drow", [P, UB], U32)
        rows_x = [nc.dram_tensor(f"rows_x{k}", [T, C], F32).ap() for k in range(2)]
        results = nc.dram_tensor("results", [2 * T, C], F32).ap()

        wat = sb("wat", [P, 3 * C])
        ra = arena[:, 8192:8320].rearrange("p (h i) -> p h i", h=2 * NH)
        rb = arena[:, 8320:8448].rearrange("p (h i) -> p h i", h=2 * NH)
        wqk = sb("wqk", [P, 2 * NH, 32])
        bat = arena[0:1, 9888:9888 + 2 * C]
        rope = arena[:, 10144:10400].rearrange("p (q h i) -> p q h i", q=2, h=2 * NH)
        bra = arena[0:1, 8448:8576].rearrange("p (h i) -> p h i", h=2 * NH)
        brb = arena[0:1, 8576:8704].rearrange("p (h i) -> p h i", h=2 * NH)
        sel_f = arena[:, 9728:9728 + 2 * NS]
        cmask_f = arena[:, 9760:9760 + P]
        bqk_r = arena[0:1, 8704:9728].rearrange("p (h d) -> p h d", d=32)
        one1 = sb("one1", [1, 1])
        bqk = sb("bqk", [P, 2 * NG])
        bv = sb("bv", [P, C])
        bpj = sb("bpj", [P, C])
        wpj = sb("wpj", [P, C])
        qblk = arena[:, 0:8192].rearrange("p (s g j t) -> p s g j t", s=2, g=NG, j=GH)
        PR = arena[:, 8192:8192 + 3072].rearrange("p (s n) -> p s n", s=2)
        PT = arena[:, 11264:11264 + 3072].rearrange("p (s n) -> p s n", s=2)
        kT = arena[:, 14336:16384].rearrange("p (s g t) -> p s g t", s=2, g=NG)
        va = U[:].rearrange("p n c -> p (n c)")
        va = va.rearrange("p (s q h d) -> p s q h d", s=2, q=QT, h=NH)
        ngm = sb("ngm", [P, 2, QT, GH])
        conv_f = conv[:].rearrange("p s h t -> p (s h t)")
        oT = conv_f[:, 0:2 * S].rearrange("p (s t) -> p s t", s=2)
        rden = sb("rden", [P, 2, QT, GH])
        yat = conv_f[:, 2 * S:4 * S].rearrange("p (s q h d) -> p s q h d", s=2, q=QT, h=NH)
        yT = conv_f[:, 4 * S:6 * S].rearrange("p (s t) -> p s t", s=2)

        ld_x = sem("ld_x")
        ld_a = sem("ld_a")
        ld_f = sem("ld_f")
        ld_b = sem("ld_b")
        n_ld = {"x": 0, "a": 0, "f": 0, "b": 0}
        st_zero = sem("st_zero")
        st_wbc = sem("st_wbc")
        st_tr = sem("st_tr")
        st_cp = sem("st_cp")
        st_const = sem("st_const")
        st_A = sem("st_A")
        st_rope = sem("st_rope")
        st_bq = sem("st_bq")
        st_bqc = sem("st_bqc")
        st_qz = sem("st_qz")
        out_done = sem("out_done")

        def chunk(c, n=CT):
            return bass.ds(c * n, n)

        def cols(c, n=CW):
            return bass.ds(c * n, n)

        def bcast(ap, n):
            return ap.unsqueeze(ap.ndim).broadcast_to(list(ap.shape) + [n])

        act_steps = sem("act_steps")
        pool_steps = sem("pool_steps")
        dve_steps = sem("dve_steps")

        def apart(engine, steps=act_steps):
            engine.sem_inc(steps, 1)

        LN = {k: {q: sem(f"{k}_{q}") for q in ("m", "n", "v", "s", "r")} for k in ("ln0", "ln1", "lnf0", "lnb", "lnf1")}

        LA = 3 * NT // 4

        def ln_sum(k, src, c):
            nc.vector.tensor_reduce(st_sum[:, c * CT:(c + 1) * CT], src[:, c * CT:(c + 1) * CT, :], AX_X,
                                    ALU.add).then_inc(LN[k]["m"], 1)

        def ln_mean(v, k, c):
            v.wait_ge(LN[k]["m"], c + 1)
            nc.vector.tensor_scalar(st_neg[:, c * CT:(c + 1) * CT], st_sum[:, c * CT:(c + 1) * CT], -1.0 / C, None,
                                    ALU.mult).then_inc(LN[k]["n"], 1)

        def ln_vector(v, k, src, summed=False):
            s = LN[k]
            if not summed:
                ln_sum(k, src, 0)
                for c in range(1, NCH):
                    ln_sum(k, src, c)
                    ln_mean(v, k, c - 1)
                ln_mean(v, k, NCH - 1)
            v.wait_ge(s["n"], NCH)
            own = slice(LA, NT)
            nc.vector.tensor_tensor(D[:, own, :], src[:, own, :], bcast(st_neg[:, own], C), ALU.add).then_inc(s["m"], 1)
            v.wait_ge(s["m"], NCH + 1)
            squares = SQ[:, LA * C:].rearrange("p (n c) -> p n c", c=C)
            nc.vector.tensor_tensor(squares, D[:, own, :], D[:, own, :], ALU.mult).then_inc(s["m"], 1)
            v.wait_ge(s["m"], NCH + 2)
            nc.vector.tensor_reduce(st_ssq[:, own], squares, AX_X, ALU.add).then_inc(s["m"], 1)
            nc.vector.tensor_tensor(D[:, 0:LA, :], src[:, 0:LA, :], bcast(st_neg[:, 0:LA], C), ALU.add)
            v.wait_ge(s["s"], 1)
            nc.vector.reciprocal(st_r[:], st_sd[:]).then_inc(s["r"], 1)
            v.wait_ge(s["r"], 1)

        def ln_apply(dst, c, done):
            nc.vector.tensor_tensor(dst[:, c * CT:(c + 1) * CT, :], D[:, c * CT:(c + 1) * CT, :],
                                    bcast(st_r[:, c * CT:(c + 1) * CT], C), ALU.mult).then_inc(done, 1)

        def ln_scalar(a, k, src):
            s = LN[k]
            nc.scalar.activation(act_junk[:], one_t[:], ACT.Sqrt)
            for n in range(LA):
                if n % CT == 0:
                    a.wait_ge(s["n"], n // CT + 1)
                nc.scalar.activation(SQ[:, n * C:(n + 1) * C], src[:, n, :], ACT.Square, bias=st_neg[:, n:n + 1],
                                     accum_out=st_ssq[:, n:n + 1]).then_inc(s["v"], 1)
            a.wait_ge(s["v"], LA)
            a.wait_ge(s["m"], NCH + 3)
            nc.scalar.activation(st_sd[:], st_ssq[:], ACT.Sqrt, bias=eps_t[:, 0:1], scale=1.0 / C).then_inc(s["s"], 1)

        eps_t = sb("eps_t", [P, 1])
        one_t = sb("one_t", [P, 1])

        m1_st, m1_tr, m1_xn, m1_xz, m1_xe, m1_ze, m1_cd, m1_cv, m1_xc = (
            sem("m1_" + q) for q in ("st", "tr", "xn", "xz", "xe", "ze", "cd", "cv", "xc"))
        m2_mm, m2_ab, m2_ex, m2_re, m2_hi, m2_r, m2_md, m2_st, m2_ln = (
            sem("m2_" + q) for q in ("mm", "ab", "ex", "re", "hi", "r", "md", "st", "ln"))
        m2_dt, m2_dx = (sem("m2_" + q) for q in ("dt", "dx"))
        m3_a, m3_bb, m3_cb, m3_cs, m3_b, m3_sc, m3_hc, m3_ns, m3_ya, m3_y, m3_o, m3_x = (
            sem("m3_" + q) for q in ("a", "bb", "cb", "cs", "b", "sc", "hc", "ns", "ya", "y", "o", "x"))
        FS = {q: sem(f"f_{q}") for q in (
            "st", "tr", "xt", "r1", "r1s", "lg", "g", "ge", "ga", "mk", "pf", "nx", "bk", "lo", "ic", "wh", "eb", "xw",
            "ft", "l1", "h", "l2", "x", "bt", "bx", "wc", "b1", "bh", "b2", "by", "dn",
            *(f"ld{u}" for u in range(UB)), *(f"so{u}" for u in range(UB)), *(f"yl{c}" for c in range(NCH)))}
        RUN = dict(st=NCH, tr=NCH, xt=NCH, r1=NCH, r1s=NCH, lg=NCH, g=2 * NT + 32, ge=2, ga=2, mk=1, pf=2,
                   nx=2 + 2 * NT - 2 * NT // 8, bk=2, lo=2 * NT // 8, ic=1, wh=1, eb=1, xw=16 * NCH, ft=NB,
                   l1=NCH * NI, h=NCH * NI, l2=NCH, x=NCH + 1, ld=16 * NB // UB, yl=32, bt=NB, bx=NB, wc=NB,
                   b1=NB, bh=NB, b2=NB, by=NB, so=16 * NB // UB, dn=2 * NT)
        AS = {q: sem(f"a_{q}") for q in ("st", "tr", "q", "k", "v", "s", "m", "sa", "sv", "t", "ta", "tv", "o", "oe",
                                         "ot", "rd", "y", "yt", "p", "xb")}


        def each_block(engine, step):
            with engine.Fori(0, NB // UB - 1) as i:
                for j in range(UB):
                    step(i, j)
            for j in range(UB):
                step(NB // UB - 1, j)

        def exists(i, j):
            return j < UB or not isinstance(i, int)

        XB, RB = (0, 1, 6, 7), (2, 3, 4, 2)

        def ffn_scalar(a, k, ln):
            f = FS
            ln_scalar(a, ln, X)
            for c in range(NCH):
                a.wait_ge(f["tr"], c + 1 + k * RUN["tr"])
                nc.scalar.activation(xT[:, cols(c)], bank[XB[c]][:], ACT.Copy).then_inc(f["xt"], 1)
            a.wait_ge(f["ge"], 1 + k * RUN["ge"])
            nc.scalar.activation(gex[:], gex[:], ACT.Exp).then_inc(f["ga"], 1)
            a.wait_ge(f["ge"], 2 + k * RUN["ge"])
            nc.scalar.activation(wk[:, 1, :], wk[:, 0, :], ACT.Exp, scale=1.0 / 2).then_inc(f["ga"], 1)
            with a.Fori(0, NCH // 2) as i:
                for s in range(2):
                    c = 2 * i + s
                    a.wait_ge(f["l2"], c + 1 + k * RUN["l2"])
                    for b in range(NI):
                        a.wait_ge(f["l1"], c * NI + b + 1 + k * RUN["l1"])
                        nc.scalar.activation(hsT[s][:, b, :], bank[b][:], ACT.Silu,
                                             bias=b1s[:, b:b + 1]).then_inc(f["h"], 1)

            def x_out(i, j):
                a.wait_ge(f["bt"], i * UB + j + 1 + UB + k * RUN["bt"])
                nc.scalar.activation(xbT[:, j % WR, :], bank[j % 2][:, 0:P], ACT.Copy).then_inc(f["bx"], 1)

            def hidden(i, j):
                a.wait_ge(f["wc"], i * UB + j + 1 + k * RUN["wc"])
                a.wait_ge(f["b1"], i * UB + j + 1 + k * RUN["b1"])
                for b in range(NI):
                    last = nc.scalar.activation(hbT[:, j % WR, b, :], bank[2 + j % 2][:, b * P:(b + 1) * P], ACT.Silu,
                                                bias=wst[j % WR][:, FI + b:FI + b + 1])
                last.then_inc(f["bh"], 1)

            def step(i, j):
                if exists(i, j + 2):
                    x_out(i, j + 2)
                if exists(i, j + 1):
                    hidden(i, j + 1)

            x_out(0, 0)
            x_out(0, 1)
            hidden(0, 0)
            each_block(a, step)

        def ffn_pool(p, k):
            f = FS

            def gather(i, j, first=False):
                it = i + j // UB
                if not first:
                    p.wait_ge(f["bt"], i * UB + j + 1 + k * RUN["bt"])
                p.wait_ge(f["ft"], i * UB + j + 1 + k * RUN["ft"])
                apart(p, pool_steps)
                nc.gpsimd.indirect_dma_start(xrow[:, j % UB, :], None, rows_x[k],
                                             bass.IndirectOffsetOnAxis(ap=trow[:, j % UB:j % UB + 1], axis=0))\
                    .then_inc(f[f"ld{j % UB}"], 16)

            def step(i, j):
                if exists(i, j + UB):
                    gather(i, j + UB)
                p.wait_ge(f["by"], i * UB + j + 1 + UB + k * RUN["by"])
                apart(p, pool_steps)
                nc.gpsimd.indirect_dma_start(results, bass.IndirectOffsetOnAxis(ap=drow[:, j:j + 1], axis=0),
                                             yrow[:, j, :], None, bounds_check=2 * T - 1,
                                             oob_is_err=False).then_inc(f[f"so{j}"], 16)

            p.wait_ge(f["xw"], (k + 1) * RUN["xw"])
            for j in range(UB):
                gather(0, j, first=True)
            each_block(p, step)

        def ffn_sync(sp, k):
            f = FS
            xv = rows_x[k].rearrange("(n p) c -> p n c", p=P)
            for c in range(NCH):
                sp.wait_ge(f["st"], c + 1 + k * RUN["st"])
                sp.dma_start(xv[:, c * CT:(c + 1) * CT, :], D[:, c * CT:(c + 1) * CT, :]).then_inc(f["xw"], 16)
            for u in range(UB):
                sp.wait_ge(f[f"so{u}"], 16 * (NB // UB) + 16 + k * RUN["so"])
            yv = results.rearrange("(q n p) c -> p q n c", q=2, p=P)
            for c in range(NCH):
                for q in range(2):
                    sp.dma_start(yin[:, q, c * CT:(c + 1) * CT, :],
                                 yv[:, q, c * CT:(c + 1) * CT, :]).then_inc(f[f"yl{c}"], 16)

        def ffn_vector(v, k, ln):
            f = FS
            ln_vector(v, ln, X)
            for c in range(NCH):
                ln_apply(D, c, f["st"])
            for c in range(NCH):
                v.wait_ge(f["r1"], c + 1 + k * RUN["r1"])
                if c >= 2:
                    v.wait_ge(f["lg"], c - 1 + k * RUN["lg"])
                nc.vector.tensor_scalar(r1[:, c % 2, :], bank[RB[c]][0:RH, :], br1[:, 0:1], 0.0, ALU.add,
                                        ALU.max).then_inc(f["r1s"], 1)
            g = [k * RUN["g"]]

            def then(ins):
                ins.then_inc(f["g"], 1)
                g[0] += 1
                v.wait_ge(f["g"], g[0])

            logits = bank[5][:, 0:NT * NE].rearrange("p (n e) -> p n e", e=NE)
            v.wait_ge(f["lg"], NCH + k * RUN["lg"])
            then(nc.vector.tensor_tensor(gate[:], logits, br2[:].unsqueeze(1).broadcast_to([P, NT, NE]), ALU.add))
            then(nc.vector.tensor_reduce(gmx[:], gate[:], AX_X, ALU.max))
            nc.vector.tensor_tensor(gex[:], gate[:], bcast(gmx[:], NE), ALU.subtract).then_inc(f["ge"], 1)
            v.wait_ge(f["ga"], 1 + k * RUN["ga"])
            then(nc.vector.tensor_reduce(gsum[:], gex[:], AX_X, ALU.add))
            then(nc.vector.reciprocal(gmx[:], gsum[:]))
            then(nc.vector.tensor_tensor(gate[:], gex[:], bcast(gmx[:], NE), ALU.mult))
            for n in range(NT):
                nc.vector.max(top8[:, n, :], gate[:, n, :]).then_inc(f["g"], 1)
            g[0] += NT
            for n in range(NT):
                v.wait_ge(f["g"], g[0] - NT + n + 1)
                nc.vector.max_index(idx8[:, n, :], top8[:, n, :], gate[:, n, :]).then_inc(f["g"], 1)
            g[0] += NT
            nc.vector.tensor_tensor(wk[:, 0, :], top8[:, :, 1], top8[:, :, 0], ALU.subtract).then_inc(f["ge"], 1)
            v.wait_ge(f["g"], g[0])
            then(nc.vector.tensor_copy(idxf[:], idx8[:, :, 0:2]))
            for q in range(2):
                nc.vector.tensor_tensor(pick[:, q, :, :], iota[:, 0:NE].unsqueeze(1).broadcast_to([P, NT, NE]),
                                        bcast(idxf[:, :, q], NE), ALU.is_equal).then_inc(f["g"], 1)
            g[0] += 2
            v.wait_ge(f["g"], g[0])
            nc.vector.tensor_tensor(both[:], pick[:, 0, :, :], pick[:, 1, :, :], ALU.add).then_inc(f["mk"], 1)
            v.wait_ge(f["ga"], 2 + k * RUN["ga"])
            then(nc.vector.tensor_scalar(wk[:, 2, :], wk[:, 1, :], 1.0, None, ALU.add))
            then(nc.vector.reciprocal(wk[:, 3, :], wk[:, 2, :]))
            then(nc.vector.tensor_tensor(wk[:, 2, :], wk[:, 3, :], wk[:, 1, :], ALU.mult))
            v.wait_ge(f["pf"], 2 + k * RUN["pf"])
            then(nc.vector.tensor_copy(tot[:], bank[7][:, 0:NT * NE].rearrange("p (n e) -> p e n", e=NE)))
            then(nc.vector.tensor_tensor_scan(run[:].rearrange("p e n -> p (e n)"),
                                              fresh[:].rearrange("p e n -> p (e n)"),
                                              tot[:].rearrange("p e n -> p (e n)"), 0.0, ALU.mult, ALU.add))
            then(nc.vector.tensor_tensor(more[:], run[:, :, NT - 1:NT].broadcast_to([P, NE, NT]),
                                         iotaP[:].unsqueeze(1).broadcast_to([P, NE, NT]), ALU.is_gt))
            then(nc.vector.tensor_reduce(nblk[:], more[:], AX_X, ALU.add))
            then(nc.vector.tensor_tensor_scan(endb[:], ones[:, 0:NE], nblk[:], 0.0, ALU.mult, ALU.add))
            then(nc.vector.tensor_tensor(begb[:], endb[:], nblk[:], ALU.subtract))
            then(nc.vector.tensor_tensor(run[:], run[:], tot[:], ALU.subtract))
            then(nc.vector.scalar_tensor_tensor(out=more[:], in0=bcast(begb[:], NT), scalar=float(P), in1=run[:],
                                                op0=ALU.mult, op1=ALU.add))
            then(nc.vector.tensor_tensor(posn[:], bank[6][:, 0:NT * NE].rearrange("p (n e) -> p n e", e=NE),
                                         more[:].rearrange("p e n -> p n e"), ALU.add))
            for q in range(2):
                nc.vector.tensor_tensor(pick[:, q, :, :], pick[:, q, :, :], posn[:], ALU.mult).then_inc(f["g"], 1)
            g[0] += 2
            v.wait_ge(f["g"], g[0])
            then(nc.vector.tensor_reduce(slotf[:], pick[:], AX_X, ALU.add))
            at = slotf[:].rearrange("p q n -> p (q n)")
            then(nc.vector.tensor_tensor(reach, bcast(at, NB + 1), starts[:].unsqueeze(1).broadcast_to([P, 2 * NT, NB + 1]),
                                         ALU.is_ge))
            nc.vector.tensor_reduce(blk[:], reach, AX_X, ALU.add).then_inc(f["bk"], 1)
            nc.vector.tensor_tensor(blk1, reach[:, :, 0:NB], reach[:, :, 1:NB + 1], ALU.subtract).then_inc(f["nx"], 1)
            v.wait_ge(f["bk"], 1 + k * RUN["bk"])
            nc.vector.scalar_tensor_tensor(out=lane[:], in0=blk[:], scalar=-float(P), in1=at, op0=ALU.mult,
                                           op1=ALU.add).then_inc(f["bk"], 1)
            v.wait_ge(f["nx"], 1 + k * RUN["nx"])
            nc.vector.tensor_tensor(blk1, blk1, bcast(dest[:], NB), ALU.mult).then_inc(f["nx"], 1)
            v.wait_ge(f["bk"], 2 + k * RUN["bk"])
            for n in range(2 * NT):
                last = nc.vector.tensor_scalar(lane1[:, n, :], lanes[:], lane[:, n:n + 1], None, ALU.is_equal)
                last.then_inc(*((f["lo"], 1) if n % 8 == 7 else (f["nx"], 1)))
            then(nc.vector.tensor_tensor(past[:], endb[:].unsqueeze(1).broadcast_to([P, NB, NE]), bcast(iota[:], NE),
                                         ALU.is_le))
            then(nc.vector.tensor_reduce(ebf[:], past[:], AX_X, ALU.add))
            then(nc.vector.tensor_scalar(ebf[:], ebf[:], NE - 1.0, float(EW), ALU.min, ALU.mult))
            nc.vector.tensor_copy(eb[:], ebf[:]).then_inc(f["eb"], 1)
            v.wait_ge(f["ic"], 1 + k * RUN["ic"])
            then(nc.vector.tensor_scalar(who[:, 2, :], bank[7][:, 0:NB], 0.0, float(4 * T), ALU.is_equal, ALU.mult))
            then(nc.vector.tensor_tensor(who[:, 2, :], bank[7][:, 0:NB], who[:, 2, :], ALU.add))
            then(nc.vector.tensor_scalar(who[:, 0, :], who[:, 2, :], 1.0, None, ALU.subtract))
            then(nc.vector.tensor_scalar(who[:, 1, :], who[:, 0, :], float(T), -float(T), ALU.is_ge, ALU.mult))
            then(nc.vector.tensor_tensor(who[:, 1, :], who[:, 1, :], who[:, 0, :], ALU.add))
            nc.vector.tensor_scalar(who[:, 1, :], who[:, 1, :], float(T - 1), None, ALU.min).then_inc(f["wh"], 1)

            flat = we[:].rearrange("p e w -> p (e w)")

            def weights(i, j, first=False):
                if not first:
                    v.wait_ge(f["b2"], i * UB + j - 1 + k * RUN["b2"])
                    v.wait_ge(f["by"], i * UB + j + 1 + UB - WR + k * RUN["by"])
                col = v.value_load(eb[0:1, bass.ds(i * UB + j, 1)] if not isinstance(i, int) else
                                   eb[0:1, i * UB + j:i * UB + j + 1], min_val=0, max_val=(NE - 1) * EW)
                nc.vector.tensor_copy(wst[j % WR], flat[:, bass.ds(col, EW)]).then_inc(f["wc"], 1)

            def fetch(i, j, first=False):
                if not first:
                    v.wait_ge(f[f"ld{j % UB}"], 16 * (i + j // UB) + k * RUN["ld"])
                n = i * UB + j
                src = who[:, 1, n:n + 1] if isinstance(n, int) else who[:, 1, bass.ds(n, 1)]
                nc.vector.tensor_copy(trow[:, j % UB:j % UB + 1], src).then_inc(f["ft"], 1)

            def where(i, j):
                v.wait_ge(f[f"so{j % UB}"], 16 * (i + j // UB + 1) + k * RUN["so"])
                apart(v, dve_steps)
                n = i * UB + j
                src = who[:, 0, n:n + 1] if isinstance(n, int) else who[:, 0, bass.ds(n, 1)]
                nc.vector.tensor_copy(drow[:, j % UB:j % UB + 1], src)

            def result(i, j):
                v.wait_ge(f["b2"], i * UB + j + 1 + 2 + k * RUN["b2"])
                nc.vector.tensor_tensor(yrow[:, j % UB, :], bank[4 + j % 2][:, 0:C], wst[j % WR][:, EW - C:EW],
                                        ALU.add).then_inc(f["by"], 1)

            def step(i, j):
                if exists(i, j + UB):
                    fetch(i, j + UB)
                if exists(i, j + 1):
                    where(i, j + 1)
                result(i, j)
                if exists(i, j + WR - 1):
                    weights(i, j + WR - 1)

            v.wait_ge(f["wh"], 1 + k * RUN["wh"])
            for j in range(UB):
                fetch(0, j, first=True)
            v.wait_ge(f["eb"], 1 + k * RUN["eb"])
            for j in range(WR - 1):
                weights(0, j, first=True)
            where(0, 0)

            for c in range(NCH):
                v.wait_ge(f["l2"], c + 1 + 2 + k * RUN["l2"])
                nc.vector.tensor_tensor(X[:, c * CT:(c + 1) * CT, :], bank[4 + c % 2][:].rearrange("p (n c) -> p n c", c=C),
                                        X[:, c * CT:(c + 1) * CT, :], ALU.add).then_inc(f["x"], 1)
            v.wait_ge(f["x"], NCH + 2 + k * RUN["x"])
            nc.vector.tensor_tensor(X[:], X[:], bs2[:].unsqueeze(1).broadcast_to([P, NT, C]), ALU.add)\
                .then_inc(f["x"], 1)

            each_block(v, step)
            v.wait_ge(f["x"], NCH + 2 + 1 + k * RUN["x"])
            for c in range(NCH):
                v.wait_ge(f[f"yl{c}"], (k + 1) * RUN["yl"])
                for q in range(2):
                    for n in range(c * CT, (c + 1) * CT):
                        if q:
                            v.wait_ge(f["dn"], n + c * CT + 1 + k * RUN["dn"])
                        if k == 0 and c and not q and n == c * CT + 1:
                            ln_mean(v, "lnb", c - 1)
                        nc.vector.scalar_tensor_tensor(out=X[:, n, :], in0=yin[:, q, n, :], scalar=wk[:, 3 - q, n:n + 1],
                                                       in1=X[:, n, :], op0=ALU.mult, op1=ALU.add).then_inc(f["dn"], 1)
                if k == 0:
                    v.wait_ge(f["dn"], 2 * (c + 1) * CT)
                    ln_sum("lnb", X, c)
            if k == 0:
                ln_mean(v, "lnb", NCH - 1)
            v.wait_ge(f["dn"], 2 * NT + k * RUN["dn"])
            assert g[0] == (k + 1) * RUN["g"]

        def ffn_tensor(pe, k):
            f = FS
            for c in range(NCH):
                pe.wait_ge(f["st"], c + 1 + k * RUN["st"])
                for n in range(CT):
                    last = nc.tensor.transpose(bank[XB[c]][:, n * P:(n + 1) * P], D[:, c * CT + n, :], ident[:])
                last.then_inc(f["tr"], 1)

            def hidden_router(c):
                pe.wait_ge(f["xt"], c + 1 + k * RUN["xt"])
                if c == 3:
                    pe.wait_ge(f["r1s"], 1 + k * RUN["r1s"])
                nc.tensor.matmul(bank[RB[c]][0:RH, :], wr1[:], xT[:, c * CW:(c + 1) * CW], start=True, stop=True)\
                    .then_inc(f["r1"], 1)

            def logits(c):
                pe.wait_ge(f["r1s"], c + 1 + k * RUN["r1s"])
                for n in range(CT):
                    at = (c * CT + n) * NE
                    last = nc.tensor.matmul(bank[5][:, at:at + NE], r1[:, c % 2, n * P:(n + 1) * P], wr2[:],
                                            start=True, stop=True)
                last.then_inc(f["lg"], 1)

            hidden_router(0)
            hidden_router(1)
            for c in range(2, NCH):
                logits(c - 2)
                hidden_router(c)
            logits(NCH - 2)
            logits(NCH - 1)

            def shared1(c):
                for b in range(NI):
                    pe.wait_ge(f["h"], c * NI + b + 1 + k * RUN["h"])
                    nc.tensor.matmul(bank[b][:], w1[:, b * P:(b + 1) * P], xT[:, c * CW:(c + 1) * CW],
                                     start=True, stop=True).then_inc(f["l1"], 1)

            def shared2(c):
                pe.wait_ge(f["h"], c * NI + NI + NI + k * RUN["h"])
                pe.wait_ge(f["x"], c + 1 + k * RUN["x"])
                for n in range(CT):
                    for b in range(NI):
                        last = nc.tensor.matmul(bank[4 + c % 2][:, n * C:(n + 1) * C],
                                                hsT[c % 2][:, b, n * P:(n + 1) * P], w2[:, b, :],
                                                start=(b == 0), stop=(b == NI - 1))
                last.then_inc(f["l2"], 1)

            shared1(0)
            pe.wait_ge(f["mk"], 1 + k * RUN["mk"])
            flat = both[:].rearrange("p n e -> p (n e)")
            nc.tensor.matmul(bank[6][:, 0:NT * NE], tri[:], flat, start=True, stop=True).then_inc(f["pf"], 1)
            nc.tensor.matmul(bank[7][:, 0:NT * NE], ones[:], flat, start=True, stop=True).then_inc(f["pf"], 1)
            shared1(1)
            shared2(0)
            shared1(2)
            shared2(1)
            for n in range(2 * NT):
                if n == 0:
                    pe.wait_ge(f["nx"], 2 + k * RUN["nx"])
                if n % 8 == 0:
                    pe.wait_ge(f["lo"], n // 8 + 1 + k * RUN["lo"])
                last = nc.tensor.matmul(bank[7][:, 0:NB], lane1[:, n, :], blk1[:, n, :], start=(n == 0),
                                        stop=(n == 2 * NT - 1))
            last.then_inc(f["ic"], 1)
            shared1(3)
            shared2(2)
            shared2(3)
            pe.wait_ge(f["h"], NCH * NI + NI + k * RUN["h"])

            def turn(i, j):
                pe.wait_ge(f[f"ld{j % UB}"], 16 * (i + j // UB + 1) + k * RUN["ld"])
                pe.wait_ge(f["bx"], i * UB + j + 1 + k * RUN["bx"])
                nc.tensor.transpose(bank[j % 2][:, 0:P], xrow[:, j % UB, 0:C], ident[:]).then_inc(f["bt"], 1)

            def layer1(i, j):
                n = i * UB + j
                pe.wait_ge(f["wc"], n + 1 + k * RUN["wc"])
                pe.wait_ge(f["bx"], n + 1 + 2 + k * RUN["bx"])
                pe.wait_ge(f["bh"], n + 1 + k * RUN["bh"])
                for b in range(NI):
                    last = nc.tensor.matmul(bank[2 + j % 2][:, b * P:(b + 1) * P], wst[j % WR][:, b * P:(b + 1) * P],
                                            xbT[:, j % WR, :], start=True, stop=True)
                last.then_inc(f["b1"], 1)

            def layer2(i, j):
                n = i * UB + j
                pe.wait_ge(f["bh"], n + 1 + 2 + k * RUN["bh"])
                pe.wait_ge(f["by"], n - 1 + UB + k * RUN["by"])
                for b in range(NI):
                    at = FI + NI + b * C
                    last = nc.tensor.matmul(bank[4 + j % 2][:, 0:C], hbT[:, j % WR, b, :], wst[j % WR][:, at:at + C],
                                            start=(b == 0), stop=(b == NI - 1))
                last.then_inc(f["b2"], 1)

            def step(i, j):
                if exists(i, j + 2):
                    turn(i, j + 2)
                if exists(i, j + 1):
                    layer1(i, j + 1)
                layer2(i, j)

            turn(0, 0)
            turn(0, 1)
            layer1(0, 0)
            pe.wait_ge(f["x"], NCH + 2 + k * RUN["x"])
            each_block(pe, step)

        SQ0, SK0 = 6, 8
        TX, TV, TY, TP = 3, 7, 14, 15
        HQ = [(0, 0, GH), (1, 0, GH // 2), (1, GH // 2, GH // 2)]

        def s_unit(g, r):
            return (0, 3 * (g - 2) + r) if g >= 2 else (-1, 10 + 3 * g + r)

        def t_unit(g, r):
            return (0, 4, 8, 11)[g] + r

        def owners(units, dve):
            n, outs = {"v": 0, "a": 0}, []
            for u in range(units):
                who = "v" if u in dve else "a"
                n[who] += 1
                outs.append((who, n[who]))
            return outs, n

        S_OUT, S_N = owners(16, (SQ0,))
        T_OUT, T_N = owners(16, (0, 1, 4, 5, TV, 8, 9, 11, 12, TP))
        CREDIT = {"sa": S_N["a"] - 9, "ta": T_N["a"] - 1, "tv": T_N["v"] - 1}

        def s_out(b, u):
            who, n = S_OUT[u]
            return AS["s" + who], (b + 1) * S_N[who] + n

        def t_out(b, u):
            who, n = T_OUT[u]
            return AS["t" + who], (b + 1) * T_N[who] + n

        def s_free(b, u):
            return s_out(b, u - 4) if u >= 4 else s_out(b - 1, u + 12)

        def t_free(b, u):
            return t_out(b, u - 2) if u >= 2 else t_out(b - 1, u + 14)

        def exps_done(b, g):
            step, u = s_unit(g, 2)
            return s_out(b + step, u)

        def each_batch(engine, step):
            with engine.Fori(0, B // 2 - 1) as i:
                for s in range(2):
                    step(2 * i + s, s, True)
            step(B - 2, 0, True)
            step(B - 1, 1, False)

        def probs(s, g, qt):
            kw = (qt + 1) * P
            return PR[:, g % 2, GH * P * qt:GH * P * qt + GH * kw].rearrange("p (j k) -> p j k", k=kw)

        def probsT(g, kt):
            qw = S - kt * P
            at = 0 if kt == 0 else GH * S
            return PT[:, g % 2, at:at + GH * qw].rearrange("p (j q) -> p j q", q=qw)

        def pt_part(g, r):
            return (probsT(g, 0)[:, :, 0:P], probsT(g, 0)[:, :, P:S], probsT(g, 1))[r]

        def attention_scalar(a):
            f = AS
            ln_scalar(a, "lnb", X)

            def exps(b, g):
                a.wait_ge(f["t"], b * 3 * NG + 3 * g + 3)
                for r, (qt, j0, nj) in enumerate(HQ):
                    a.wait_ge(f["m"], b * 3 * NG + 3 * g + r + 1)
                    kw = (qt + 1) * P
                    for j in range(nj):
                        last = nc.scalar.activation(probs(0, g, qt)[:, j0 + j, :],
                                                    bank[s_unit(g, r)[1] % 4][:, j * kw:(j + 1) * kw], ACT.Exp,
                                                    bias=ngm[:, g % 2, qt, j0 + j:j0 + j + 1])
                    last.then_inc(f["sa"], 1)

            def pt_out(b, g):
                a.wait_ge(f["o"], b * NG + g + 1)
                a.wait_ge(f["t"], b * 3 * NG + 3 * g + 3 + 6)
                nc.scalar.activation(pt_part(g, 2), bank[4 + t_unit(g, 2) % 2][:].rearrange("p (j q) -> p j q", q=P),
                                     ACT.Copy).then_inc(f["ta"], 1)

            def o_out(b, g):
                a.wait_ge(f["ot"], b * NG + g + 1)
                a.wait_ge(f["o"], b * NG + g + 1 + 2)
                nc.scalar.activation(oT[:, g % 2, :], bank[6][:, 0:S], ACT.Copy).then_inc(f["oe"], 1)

            def x_out(b, s):
                a.wait_ge(f["tr"], b + 1)
                nc.scalar.activation(xnT[:, s, 0:S], bank[4 + TX % 2][:, 0:S], ACT.Copy).then_inc(f["ta"], 1)

            def q_out(b, s):
                a.wait_ge(f["q"], b * (NG // 2) + 2)
                for j in range(GH):
                    r = slice(32 * j, 32 * j + 32)
                    for w in range(2):
                        g = 2 + w
                        last = nc.scalar.activation(qblk[r, s, g, j, :], bank[(SQ0 + 1) % 4][r, w * S:(w + 1) * S],
                                                    ACT.Identity, bias=bqk[r, g:g + 1])
                last.then_inc(f["sa"], 1)

            def k_out(b, s):
                for u in range(NG // 2):
                    a.wait_ge(f["k"], b * (NG // 2) + u + 1)
                    for w in range(2):
                        g = 2 * u + w
                        last = nc.scalar.activation(kT[:, s, g, :], bank[(SK0 + u) % 4][:, w * S:(w + 1) * S],
                                                    ACT.Identity, bias=bqk[:, NG + g:NG + g + 1])
                    last.then_inc(f["sa"], 1)

            def step(b, s, more):
                exps(b, 1)
                pt_out(b, 0)
                if more:
                    x_out(b + 1, 1 - s)
                else:
                    a.wait_ge(*t_out(b, TX - 1))
                    a.sem_inc(f["ta"], 1)
                exps(b, 2)
                o_out(b, 0)
                pt_out(b, 1)
                exps(b, 3)
                o_out(b, 1)
                pt_out(b, 2)
                if more:
                    q_out(b + 1, 1 - s)
                o_out(b, 2)
                if more:
                    k_out(b + 1, 1 - s)
                pt_out(b, 3)
                o_out(b, 3)
                if more:
                    exps(b + 1, 0)
                a.wait_ge(f["yt"], b + 1)
                nc.scalar.activation(yT[:, s, :], bank[4 + TY % 2][:, 0:S], ACT.Copy).then_inc(f["ta"], 1)

            x_out(0, 0)
            q_out(0, 0)
            k_out(0, 0)
            exps(0, 0)
            each_batch(a, step)

        def attention_vector(v):
            f = AS
            ln_vector(v, "lnb", X, summed=True)

            def rows_out(b, s):
                nc.vector.tensor_tensor(stage[:, s, 0:QT, :], D[:, chunk(b, QT), :], bcast(st_r[:, chunk(b, QT)], C),
                                        ALU.mult).then_inc(f["st"], 1)

            def maxima(b, g):
                step, u = s_unit(g, 2)
                v.wait_ge(*exps_done(b if g >= 2 else b - 1, (g - 2) % NG))
                for r, (qt, j0, nj) in enumerate(HQ):
                    v.wait_ge(f["s"], b * 3 * NG + 3 * g + r + 1)
                    sc = bank[s_unit(g, r)[1] % 4][:].rearrange("p (j k) -> p j k", j=nj)
                    nc.vector.tensor_reduce(ngm[:, g % 2, qt, j0:j0 + nj], sc, AX_X, ALU.max,
                                            negate=True).then_inc(f["m"], 1)

            def pt_out(b, g):
                v.wait_ge(f["o"], b * NG + g + 1)
                for r in range(2):
                    v.wait_ge(f["t"], b * 3 * NG + 3 * g + r + 1 + 6)
                    nc.vector.tensor_copy(pt_part(g, r),
                                          bank[4 + t_unit(g, r) % 2][:].rearrange("p (j q) -> p j q", q=P))\
                        .then_inc(f["tv"], 1)

            def q_out(b, s):
                v.wait_ge(f["q"], b * (NG // 2) + 1)
                for j in range(GH):
                    r = slice(32 * j, 32 * j + 32)
                    last = nc.vector.tensor_tensor(
                        qblk[r, s, 0:2, j, :], bank[SQ0 % 4][r, :].rearrange("p (w t) -> p w t", w=2),
                        bcast(bqk[r, 0:2], S), ALU.add)
                last.then_inc(f["sv"], 1)

            def v_out(b, s):
                v.wait_ge(f["v"], b + 1)
                nc.vector.tensor_tensor(
                    va[:, s, :, :, 0:HD], bank[4 + TV % 2][:, 0:S].rearrange("p (q h d) -> p q h d", q=QT, h=NH),
                    bv[:].rearrange("p (h d) -> p h d", h=NH).unsqueeze(1).broadcast_to([P, QT, NH, HD]),
                    ALU.add).then_inc(f["tv"], 1)

            def norm(b, s, g):
                v.wait_ge(f["ot"], b * NG + g + 1 + 2)
                o = bank[7][:, (g % 2) * S:(g % 2 + 1) * S].rearrange("p (qt j d) -> p qt j d", qt=QT, j=GH)
                nc.vector.reciprocal(rden[:, g % 2, :, :], o[:, :, :, HD]).then_inc(f["rd"], 1)
                v.wait_ge(f["rd"], b * NG + g + 1)
                nc.vector.tensor_tensor(yat[:, s, :, GH * g:GH * (g + 1), :], o[:, :, :, 0:HD],
                                        bcast(rden[:, g % 2, :, :], HD), ALU.mult).then_inc(f["y"], 1)

            def step(b, s, more):
                pt_out(b, 0)
                maxima(b, 2)
                pt_out(b, 1)
                maxima(b, 3)
                norm(b, s, 0)
                if more:
                    v_out(b + 1, 1 - s)
                else:
                    v.wait_ge(*t_out(b, 5))
                    v.sem_inc(f["tv"], 1)
                pt_out(b, 2)
                if more:
                    q_out(b + 1, 1 - s)
                norm(b, s, 1)
                pt_out(b, 3)
                if more and not (isinstance(b, int) and b + 2 >= B):
                    rows_out(b + 2, s)
                norm(b, s, 2)
                if more:
                    maxima(b + 1, 0)
                norm(b, s, 3)
                if more:
                    maxima(b + 1, 1)
                v.wait_ge(f["p"], b + 1)
                if isinstance(b, int) or s == 0:
                    v.wait_ge(f["xb"], 1)
                xb = X[:, chunk(b, QT), :]
                nc.vector.tensor_tensor(xb, bank[4 + TP % 2][:, 0:S].rearrange("p (q c) -> p q c", q=QT), xb,
                                        ALU.add).then_inc(f["tv"], 1)

            rows_out(0, 0)
            rows_out(1, 1)
            nc.vector.tensor_tensor(X[:], X[:], bpj[:].unsqueeze(1).broadcast_to([P, NT, C]), ALU.add)\
                .then_inc(f["xb"], 1)
            q_out(0, 0)
            v_out(0, 0)
            maxima(0, 0)
            maxima(0, 1)
            each_batch(v, step)
            v.wait_ge(*t_out(B - 1, TP))

        def attention_tensor(pe):
            f = AS

            def scores(b, s, g, parts=(0, 1, 2)):
                for r in parts:
                    qt, j0, nj = HQ[r]
                    step, u = s_unit(g, r)
                    kw = (qt + 1) * P
                    if g == 0 and r == 0:
                        pe.wait_ge(*s_out(b - 1, SQ0))
                        pe.wait_ge(*s_out(b - 1, SK0 + 1))
                    pe.wait_ge(*s_free(b + step, u))
                    for j in range(nj):
                        nc.tensor.matmul(bank[u % 4][:, j * kw:(j + 1) * kw], qblk[:, s, g, j0 + j, qt * P:(qt + 1) * P],
                                         kT[:, s, g, 0:kw], start=(j == 0), stop=False)
                    diag = bank[u % 4][:].rearrange("p (j k) -> p j k", j=nj)[:, :, qt * P:(qt + 1) * P]
                    nc.tensor.matmul(diag, identb[:], cmask[:, 0:nj * P].rearrange("p (j k) -> p j k", j=nj),
                                     start=False, stop=True).then_inc(f["s"], 1)

            def transposes(b, s, g):
                for r, (qt, kt) in enumerate(((0, 0), (1, 0), (1, 1))):
                    if r < 2:
                        step, u = s_unit(g, (0, 2)[r])
                        pe.wait_ge(*s_out(b + step, u))
                    pe.wait_ge(*t_free(b, t_unit(g, r)))
                    for j in range(GH):
                        last = nc.tensor.transpose(bank[4 + t_unit(g, r) % 2][:, j * P:(j + 1) * P],
                                                   probs(s, g, qt)[:, j, kt * P:(kt + 1) * P], ident[:])
                    last.then_inc(f["t"], 1)

            def pv(b, s, g):
                pe.wait_ge(*t_out(b, t_unit(g, 1)))
                pe.wait_ge(*t_out(b, t_unit(g, 2)))
                pe.wait_ge(f["oe"], b * NG + g + 1)
                for kt in range(QT):
                    for j in range(GH):
                        last = nc.tensor.matmul(bank[6][32 * j:32 * j + 32, kt * P:S], va[:, s, kt, GH * g + j, :],
                                                probsT(g, kt)[:, j, :], start=(kt == 0), stop=(kt == QT - 1),
                                                tile_position=(0, 32 * j), skip_group_check=True)
                last.then_inc(f["o"], 1)

            def o_transposes(b, s, g):
                pe.wait_ge(f["oe"], b * NG + g + 1 + 1)
                pe.wait_ge(f["y"], b * NG + g + 1)
                for qt in range(QT):
                    at = (g % 2) * S + qt * P
                    last = nc.tensor.transpose(bank[7][:, at:at + P], oT[:, g % 2, qt * P:(qt + 1) * P], ident[:])
                last.then_inc(f["ot"], 1)

            def x_transposes(b, s, first=False):
                pe.wait_ge(f["st"], b + 1)
                if not first:
                    pe.wait_ge(*t_free(b - 1, TX))
                for q in range(QT):
                    last = nc.tensor.transpose(bank[4 + TX % 2][:, q * P:(q + 1) * P], stage[:, s, q, :], ident[:])
                last.then_inc(f["tr"], 1)

            def project(b, s, u0, what, first_head, first=False):
                for u in range(NG // 2):
                    if not first:
                        pe.wait_ge(*s_free(b - 1, u0 + u))
                    for w in range(2):
                        h0 = first_head + GH * (2 * u + w)
                        last = nc.tensor.matmul(bank[(u0 + u) % 4][:, w * S:(w + 1) * S], wqk[:, h0:h0 + GH, :],
                                                xnT[:, s, 0:S], start=True, stop=True)
                    last.then_inc(what, 1)

            def values(b, s, first=False):
                pe.wait_ge(f["ta"], T_N["a"] if first else t_out(b - 1, TX)[1])
                if not first:
                    pe.wait_ge(*t_free(b - 1, TV))
                for q in range(QT):
                    last = nc.tensor.matmul(bank[4 + TV % 2][:, q * P:(q + 1) * P], xnT[:, s, q * P:(q + 1) * P],
                                            wat[:, 2 * C:3 * C], start=True, stop=True)
                last.then_inc(f["v"], 1)

            def step(b, s, more):
                transposes(b, s, 0)
                scores(b, s, 2)
                if more:
                    x_transposes(b + 1, 1 - s)
                pv(b, s, 0)
                transposes(b, s, 1)
                scores(b, s, 3)
                o_transposes(b, s, 0)
                pv(b, s, 1)
                if more:
                    values(b + 1, 1 - s)
                transposes(b, s, 2)
                if more:
                    project(b + 1, 1 - s, SQ0, f["q"], 0)
                o_transposes(b, s, 1)
                pv(b, s, 2)
                if more:
                    project(b + 1, 1 - s, SK0, f["k"], NH)
                transposes(b, s, 3)
                o_transposes(b, s, 2)
                pv(b, s, 3)
                if more:
                    scores(b + 1, 1 - s, 0)
                o_transposes(b, s, 3)
                if more:
                    scores(b + 1, 1 - s, 1, (0,))
                pe.wait_ge(f["y"], b * NG + NG + 1)
                pe.wait_ge(*t_free(b, TY))
                for q in range(QT):
                    last = nc.tensor.transpose(bank[4 + TY % 2][:, q * P:(q + 1) * P],
                                               yat[:, s, q, :, :].rearrange("p h d -> p (h d)"), ident[:])
                last.then_inc(f["yt"], 1)
                if more:
                    scores(b + 1, 1 - s, 1, (1, 2))
                pe.wait_ge(*t_free(b, TP))
                pe.wait_ge(*t_out(b, TY))
                for q in range(QT):
                    last = nc.tensor.matmul(bank[4 + TP % 2][:, q * P:(q + 1) * P], yT[:, s, q * P:(q + 1) * P],
                                            wpj[:], start=True, stop=True)
                last.then_inc(f["p"], 1)

            x_transposes(0, 0, first=True)
            values(0, 0, first=True)
            project(0, 0, SQ0, f["q"], 0, first=True)
            project(0, 0, SK0, f["k"], NH, first=True)
            scores(0, 0, 0)
            scores(0, 0, 1)
            each_batch(pe, step)

        block = ctx.enter_context(nc.Block())

        @block.sync
        def _(sp):
            xv = t["L0_attn_a_x"].rearrange("b (q p) c -> p (b q) c", p=P)
            for c in range(NCH):
                sp.dma_start(X[:, c * CT:(c + 1) * CT, :], xv[:, c * CT:(c + 1) * CT, :]).then_inc(ld_x, 16)

            def load(key, s, dst, src, **how):
                sp.dma_start(dst, src, **how).then_inc(s, 16)
                n_ld[key] += 16

            def rows(v):
                return v.rearrange("(a n) -> a n", a=1)

            def column(dst, v, h=1):
                load("a", ld_a, dst, v.rearrange("(h p) -> p h", h=h), allow_slow_non_contiguous=True)

            load("a", ld_a, ident[:], t["c_ident"])
            load("a", ld_a, win_n, t["L0_attn_a_W_in"].rearrange("(e p) d -> p e d", p=P))
            column(nw[:], t["L0_attn_a_norm_w"])
            column(nb[:], t["L0_attn_a_norm_b"])
            load("a", ld_a, cw[:], t["L0_attn_a_conv_w"].rearrange("(h p) k -> p h k", h=2))
            column(cb[:], t["L0_attn_a_conv_b"], 2)
            load("a", ld_a, wdt_n, t["L0_attn_a_W_dt"].rearrange("(e p) d -> p e d", p=P))
            column(bdt[:], t["L0_attn_a_b_dt"], 2)
            column(Dv[:], t["L0_attn_a_D"], 2)
            load("a", ld_a, Am[:], t["L0_attn_a_A_log"].rearrange("(h p) n -> p h n", h=2))
            load("a", ld_a, wout_n, t["L0_attn_a_W_out"])
            load("a", ld_a, sel_f, t["c_sel"])
            sp.wait_ge(st_wbc, 1)
            for q in range(3):
                load("a", ld_a, wbc_n[32 * q:32 * q + NS, :], t["L0_attn_a_W_B"])
                load("a", ld_a, wbc_n[32 * q + NS:32 * q + 2 * NS, :], t["L0_attn_a_W_C"])

            load("b", ld_b, wat[:], t["L0_attn_b_W_attn"])
            load("b", ld_b, rope, t["c_rope"].partition_broadcast(P))
            load("b", ld_b, bat, rows(t["L0_attn_b_b_attn"])[:, 0:2 * C])
            load("b", ld_b, bv[:], t["L0_attn_b_b_attn"][2 * C:3 * C].partition_broadcast(P))
            load("b", ld_b, bpj[:], t["L0_attn_b_b_proj"].partition_broadcast(P))
            load("b", ld_b, wpj[:], t["L0_attn_b_W_proj"])
            load("b", ld_b, cmask_f, t["c_mask"])

            load("f", ld_f, w1[:], t["L0_ffn_Ws1"])
            load("f", ld_f, w2[:], t["L0_ffn_Ws2"].rearrange("(i p) c -> p i c", p=P))
            load("f", ld_f, bs2[:], t["L0_ffn_bs2"].partition_broadcast(P))
            load("f", ld_f, b1n[0:NI, :], t["L0_ffn_bs1"].rearrange("(i p) -> i p", p=P))
            load("f", ld_f, b1n[NI:NX * NI, :], t["L0_ffn_be1"].rearrange("e (i p) -> (e i) p", p=P))
            load("f", ld_f, we[:, :, 0:FI], t["L0_ffn_We1"].rearrange("e c i -> c e i"))
            for e in range(NE):
                load("f", ld_f, we[:, e, FI + NI:EW - C].rearrange("p (i c) -> p i c", c=C),
                     t["L0_ffn_We2"][e].rearrange("(i p) c -> p i c", p=P))
                load("f", ld_f, we[:, e, EW - C:EW], t["L0_ffn_be2"][e].partition_broadcast(P))
            load("f", ld_f, wr1[:], t["L0_ffn_Wr1"])
            load("f", ld_f, wr2[:], t["L0_ffn_Wr2"])
            load("f", ld_f, br1[:], t["L0_ffn_br1"].rearrange("(p a) -> p a", a=1))

            ffn_sync(sp, 0)
            ffn_sync(sp, 1)
            ov = out.rearrange("b (q p) c -> p (b q) c", p=P)
            for c in range(NCH):
                sp.wait_ge(FS["dn"], 2 * (c + 1) * CT + RUN["dn"])
                sp.dma_start(ov[:, c * CT:(c + 1) * CT, :], X[:, c * CT:(c + 1) * CT, :]).then_inc(out_done, 16)
            sp.wait_ge(out_done, 16 * NCH)

        LOADED_A, LOADED_F, LOADED_B = n_ld["a"], n_ld["f"], n_ld["b"]

        @block.gpsimd
        def _(pool):
            pool.sem_inc(m3_hc, 4)
            nc.gpsimd.memset(eps_t[:], EPS).then_inc(st_zero, 1)
            nc.gpsimd.memset(one_t[:], 1.0).then_inc(st_zero, 1)
            nc.gpsimd.memset(wbc_n, 0.0).then_inc(st_wbc, 1)
            nc.gpsimd.memset(xpad[:], 0.0).then_inc(st_zero, 1)
            nc.gpsimd.memset(decay[:, :, :, 0:1], 0.0).then_inc(st_zero, 1)
            pool.wait_ge(st_wbc, 1)
            nc.gpsimd.memset(wqk[:], 0.0).then_inc(st_zero, 1)
            nc.gpsimd.memset(bqk_r, 0.0).then_inc(st_zero, 1)
            nc.gpsimd.memset(one1[:], 1.0).then_inc(st_zero, 1)
            nc.gpsimd.memset(ones[:], 1.0).then_inc(st_zero, 1)
            for u, (dst, name) in enumerate(((tri, "c_tri"), (dest, "c_dest"), (starts, "c_starts"), (lanes, "c_lanes"),
                                          (iota, "c_iota"), (iotaP, "c_iotaP"), (fresh, "c_fresh"), (br2, "L0_ffn_br2"))):
                src = t[name] if name in ("c_tri", "c_dest") else t[name].partition_broadcast(P)
                nc.gpsimd.dma_start(dst[:], src).then_inc(FS[f"so{u}"], 16)

            pool.wait_ge(ld_a, LOADED_A)
            nc.gpsimd.tensor_copy(identb[:], ident[:]).then_inc(st_const, 1)
            nc.gpsimd.tensor_copy(sel[:], sel_f).then_inc(st_const, 1)
            pool.wait_ge(ld_b, LOADED_B)
            nc.gpsimd.tensor_copy(cmask[:].rearrange("p (j k) -> p j k", k=P),
                                  cmask_f.unsqueeze(1).broadcast_to([P, 512 // P, P])).then_inc(st_const, 1)

            pool.wait_ge(ld_b, LOADED_B)
            n = 0
            for w, wa, wb, o in ((wat[:, 0:2 * C], ra, rb, wqk[:, :, 0:HD]),
                                 (bat, bra, brb, bqk_r[:, :, 0:HD])):
                p = w.shape[0]
                pair = w.rearrange("p (h i two) -> p h i two", h=2 * NH, two=2)
                turned = o.rearrange("p h (i two) -> p h i two", two=2)
                cos, sin = rope[0:p, 0, :, :], rope[0:p, 1, :, :]
                for first, second, op in ((0, 1, ALU.subtract), (1, 0, ALU.add)):
                    nc.gpsimd.tensor_tensor(wa, pair[:, :, :, first], cos, ALU.mult).then_inc(st_rope, 1)
                    nc.gpsimd.tensor_tensor(wb, pair[:, :, :, second], sin, ALU.mult).then_inc(st_rope, 1)
                    n += 2
                    pool.wait_ge(st_rope, n)
                    nc.gpsimd.tensor_tensor(turned[:, :, :, first], wa, wb, op).then_inc(st_rope, 1)
                    n += 1
                    pool.wait_ge(st_rope, n)

            with pool.Fori(0, NCH) as c:
                for h in range(2):
                    pool.wait_ge(m2_ln, 2 * c + h + 1)
                    nc.gpsimd.tensor_tensor(dt_[:, h, cols(c)], dt_[:, h, cols(c)], dtx[:, h, cols(c)], ALU.add)\
                        .then_inc(m2_dt, 1)
                for h in range(2):
                    pool.wait_ge(m2_dt, 2 * c + h + 1)
                    nc.gpsimd.tensor_tensor(dtx[:, h, cols(c)], dt_[:, h, cols(c)], xc[:, h, cols(c)], ALU.mult)\
                        .then_inc(m2_dx, 1)
            with pool.Fori(0, NCH) as c:
                for n in range(NS):
                    pool.wait_ge(m3_cs, c * NS + n + 1 + 2)
                    for h in range(2):
                        k = 2 * n + h
                        pool.wait_ge(m3_sc, c * 2 * NS + k + 1 + NR)
                        nc.gpsimd.tensor_tensor(hst[:, k % NR, :], hst[:, k % NR, :], Csb[:, n % 2, :],
                                                ALU.mult).then_inc(m3_hc, 1)

            pool.wait_ge(m3_x, 2 * NCH)
            nc.gpsimd.memset(arena[:, 0:8192], 0.0).then_inc(st_qz, 1)
            nc.gpsimd.memset(va, 0.0).then_inc(st_qz, 1)
            pool.wait_ge(st_qz, 2)
            nc.gpsimd.memset(va[:, :, :, :, HD:HD + 1], 1.0).then_inc(st_qz, 1)
            ffn_pool(pool, 0)
            ffn_pool(pool, 1)

        @block.scalar
        def _(act):
            act.sem_inc(m1_xe, 4)
            act.sem_inc(m1_ze, 2)
            act.sem_inc(m1_xc, 4)
            act.sem_inc(m2_hi, 2)
            act.sem_inc(m3_cs, 2)
            act.sem_inc(FS["h"], NI)
            act.sem_inc(FS["bx"], 2)
            act.sem_inc(FS["bh"], 2)
            act.sem_inc(AS["sa"], CREDIT["sa"])
            act.sem_inc(AS["ta"], CREDIT["ta"])
            act.sem_inc(AS["oe"], 1)
            act.wait_ge(st_zero, 2)
            ln_scalar(act, "ln0", X)
            ln_scalar(act, "ln1", U)
            act.wait_ge(st_zero, 8)
            act.wait_ge(ld_a, LOADED_A)

            for c in range(NCH):
                act.wait_ge(m1_tr, c + 1)
                nc.scalar.activation(xT[:, cols(c)], bank[XB[c]][:], ACT.Identity, bias=nb[:, 0:1],
                                     scale=nw[:, 0:1]).then_inc(m1_xn, 1)
            with act.Fori(0, NCH // 2) as i:
                for s in range(2):
                    c = 2 * i + s
                    act.wait_ge(m1_cv, 2 * c + 2)
                    for h in range(2):
                        act.wait_ge(m1_xz, 4 * c + h + 1)
                        nc.scalar.activation(xpad[:, s, h, :, KC - 1:KC - 1 + S],
                                             bank[2 * s + h][:].rearrange("p (b t) -> p b t", b=BPC),
                                             ACT.Copy).then_inc(m1_xe, 1)
                    for h in range(2):
                        act.wait_ge(m1_xz, 4 * c + 2 + h + 1)
                        apart(act)
                        nc.scalar.activation(zs[:, h, cols(c)], bank[4 + h][:], ACT.Silu).then_inc(m1_ze, 1)
                for s in range(2):
                    c = 2 * i + s
                    for h in range(2):
                        act.wait_ge(m1_cv, 2 * c + h + 1 + 4)
                        apart(act)
                        nc.scalar.activation(xc[:, h, cols(c)], conv[:, s, h, :], ACT.Silu).then_inc(m1_xc, 1)

            with act.Fori(0, NCH // 2) as i:
                for s in range(2):
                    c = 2 * i + s
                    act.wait_ge(m2_mm, 3 * c + 3)
                    apart(act)
                    nc.scalar.activation(BCs[:, cols(c)], bank[4 + s][:], ACT.Copy).then_inc(m2_hi, 1)
                for s in range(2):
                    c = 2 * i + s
                    for h in range(2):
                        act.wait_ge(m2_ab, 2 * c + h + 1 + 4)
                        apart(act)
                        nc.scalar.activation(dt_[:, h, cols(c)], dt_[:, h, cols(c)], ACT.Exp,
                                             bias=bdt[:, h:h + 1]).then_inc(m2_ex, 1)
                for s in range(2):
                    c = 2 * i + s
                    for h in range(2):
                        act.wait_ge(m2_ex, 2 * c + h + 1)
                        apart(act)
                        nc.scalar.activation(dt_[:, h, cols(c)], dt_[:, h, cols(c)], ACT.Ln,
                                             bias=one_t[:, 0:1]).then_inc(m2_ln, 1)

            nc.scalar.activation(Am[:], Am[:], ACT.Exp).then_inc(st_A, 1)

            with act.Fori(0, NCH) as c:
                act.wait_ge(st_A, 2)
                for n in range(NS):
                    act.wait_ge(m3_cb, c * NS + n + 1)
                    act.wait_ge(m3_hc, c * 2 * NS + 2 * n + 2)
                    nc.scalar.activation(Csb[:, n % 2, :], bank[2 + n % 2][:], ACT.Copy).then_inc(m3_cs, 1)
                    for h in range(2):
                        k = 2 * n + h
                        if n == 0:
                            act.wait_ge(m2_dt, 2 * c + h + 1)
                        act.wait_ge(m3_sc, c * 2 * NS + k + 1)
                        apart(act)
                        nc.scalar.activation(decay[:, k % NR, :, 1:S],
                                             dt_[:, h, cols(c)].rearrange("p (b t) -> p b t", b=BPC)[:, :, 1:S],
                                             ACT.Exp, scale=Am[:, h, n:n + 1]).then_inc(m3_a, 1)

            ffn_scalar(act, 0, "lnf0")
            attention_scalar(act)
            ffn_scalar(act, 1, "lnf1")

        @block.vector
        def _(v):
            v.sem_inc(m1_cv, 4)
            v.sem_inc(m2_re, 4)
            v.sem_inc(m2_ab, 4)
            v.sem_inc(m2_r, 2)
            v.sem_inc(m3_sc, NR)
            v.sem_inc(m3_b, 4)
            v.sem_inc(m3_ya, 2)
            v.sem_inc(FS["x"], 2)
            v.sem_inc(FS["by"], UB)
            v.sem_inc(AS["tv"], CREDIT["tv"])
            v.sem_inc(AS["y"], 1)

            v.wait_ge(ld_x, 16 * NCH)
            ln_vector(v, "ln0", X)
            for c in range(NCH):
                ln_apply(U, c, LN["ln0"]["r"])
            v.wait_ge(LN["ln0"]["r"], 1 + NCH)
            ln_vector(v, "ln1", U)

            for n, dst in enumerate((winT[:].rearrange("p a b -> p (a b)"), wdtT[:].rearrange("p a b c -> p (a b c)"),
                                     wboT[:].rearrange("p a b -> p (a b)"))):
                v.wait_ge(st_tr, n + 1)
                nc.vector.tensor_copy(dst, bank[n][:, 0:dst.shape[1]]).then_inc(st_cp, 1)
            v.wait_ge(ld_a, LOADED_A)

            for c in range(NCH):
                ln_apply(D, c, m1_st)
            v.wait_ge(st_bq, 1)
            nc.vector.tensor_copy(bqk[:], bank[4][:, 0:2 * NG]).then_inc(st_bqc, 1)
            with v.Fori(0, NCH // 2) as i:
                for s in range(2):
                    c = 2 * i + s
                    for k in range(KC):
                        for h in range(2):
                            src = xpad[:, s, h, :, k:k + S]
                            dst = conv[:, s, h, :].rearrange("p (b t) -> p b t", b=BPC)
                            if k == 0:
                                v.wait_ge(m1_xe, 2 * c + h + 1 + 4)
                                v.wait_ge(m1_xc, 2 * c + h + 1)
                                nc.vector.tensor_scalar(dst, src, cw[:, h, 0:1], cb[:, h:h + 1], ALU.mult,
                                                        ALU.add).then_inc(m1_cd, 1)
                                continue
                            v.wait_ge(m1_cd, c * (2 * KC - 2) + 2 * k + h - 1)
                            last = nc.vector.scalar_tensor_tensor(out=dst, in0=src, scalar=cw[:, h, k:k + 1], in1=dst,
                                                                  op0=ALU.mult, op1=ALU.add)
                            last.then_inc(m1_cd if k < KC - 1 else m1_cv, 1)

            v.wait_ge(st_tr, 4)
            nc.vector.tensor_copy(b1s[:], bank[7][:, 0:NI]).then_inc(st_cp, 1)
            nc.vector.tensor_copy(we[:, :, FI:FI + NI], bank[7][:, NI:NX * NI].rearrange("p (e i) -> p e i", i=NI))\
                .then_inc(st_cp, 1)


            with v.Fori(0, NCH // 2) as i:
                for s in range(2):
                    c = 2 * i + s
                    for h in range(2):
                        v.wait_ge(m2_mm, 3 * c + h + 1)
                        nc.vector.tensor_scalar(dtx[:, h, cols(c)], bank[2 * s + h][:], bdt[:, h:h + 1], 0.0, ALU.add,
                                                ALU.max).then_inc(m2_re, 1)
                    for h in range(2):
                        v.wait_ge(m2_re, 2 * c + h + 1 + 4)
                        nc.vector.scalar_tensor_tensor(out=dt_[:, h, cols(c)], in0=dtx[:, h, cols(c)], scalar=-2.0,
                                                       in1=bank[2 * s + h][:], op0=ALU.mult, op1=ALU.add)\
                            .then_inc(m2_ab, 1)
                for s in range(2):
                    c = 2 * i + s
                    v.wait_ge(m2_hi, c + 1 + 2)
                    nc.vector.tensor_tensor(bcr[:, s, :], bank[4 + s][:], BCs[:, cols(c)], ALU.subtract)\
                        .then_inc(m2_r, 1)
                    v.wait_ge(m2_r, c + 1 + 2)
                    nc.vector.tensor_copy(bcm[:, s, :], bcr[:, s, :]).then_inc(m2_md, 1)
                    v.wait_ge(m2_md, c + 1)
                    nc.vector.tensor_copy(BCs[32:64, cols(c)], bcm[32:64, s, :]).then_inc(m2_st, 1)
                    nc.vector.tensor_tensor(BCs[64:96, cols(c)], bcr[64:96, s, :], bcm[64:96, s, :],
                                            ALU.subtract).then_inc(m2_st, 1)

            def inputs(c, k):
                n, h = k // 2, k % 2
                if k < 2:
                    v.wait_ge(m2_dx, 2 * c + h + 1)
                v.wait_ge(m3_sc, c * 2 * NS + k + 1)
                v.wait_ge(m3_bb, c * NS + n + 1)
                nc.vector.tensor_tensor(inp[:, k % NR, :], bank[n % 2][:], dtx[:, h, cols(c)], ALU.mult)\
                    .then_inc(m3_b, 1)

            def scan(c, k, last=False):
                if k + 1 < 2 * NS:
                    inputs(c, k + 1)
                elif not last:
                    inputs(c + 1, 0)
                v.wait_ge(m3_a, c * 2 * NS + k + 1)
                v.wait_ge(m3_ns, c * 2 * NS + k + 1)
                v.wait_ge(m3_b, c * 2 * NS + k + 1 + 4)
                nc.vector.tensor_tensor_scan(hst[:, k % NR, :], decay[:, k % NR, :, :].rearrange("p b t -> p (b t)"),
                                             inp[:, k % NR, :], 0.0, ALU.mult, ALU.add).then_inc(m3_sc, 1)

            def gate_y(c):
                for h in range(2):
                    v.wait_ge(m3_ns, c * 2 * NS + 2 * NS - 1 + h + NR)
                    nc.vector.scalar_tensor_tensor(out=ybuf[:, h, :], in0=xc[:, h, cols(c)], scalar=Dv[:, h:h + 1],
                                                   in1=bank[4 + h][:], op0=ALU.mult, op1=ALU.add).then_inc(m3_ya, 1)
                for h in range(2):
                    v.wait_ge(m3_ya, 2 * c + h + 1 + 2)
                    nc.vector.tensor_tensor(ybuf[:, h, :], ybuf[:, h, :], zs[:, h, cols(c)], ALU.mult)\
                        .then_inc(m3_y, 1)

            def residual(c):
                v.wait_ge(m3_o, c + 1)
                nc.vector.tensor_tensor(U[:, chunk(c), :], bank[6][:].rearrange("p (n c) -> p n c", c=C),
                                        U[:, chunk(c), :], ALU.add).then_inc(m3_x, 1)
                v.wait_ge(m3_x, 2 * c + 1)
                nc.vector.tensor_tensor(X[:, chunk(c), :], X[:, chunk(c), :], U[:, chunk(c), :], ALU.add)\
                    .then_inc(m3_x, 1)

            v.wait_ge(st_A, 1)
            nc.vector.tensor_scalar(Am[:], Am[:], -1.0, None, ALU.mult).then_inc(st_A, 1)
            TURN = 8
            inputs(0, 0)
            for k in range(TURN):
                scan(0, k)
            with v.Fori(0, NCH - 1) as c:
                for k in range(TURN, 2 * NS):
                    scan(c, k)
                for k in range(TURN):
                    scan(c + 1, k)
                    if k == 2:
                        gate_y(c)
                    if k == TURN - 1:
                        residual(c)
            for k in range(TURN, 2 * NS):
                scan(NCH - 1, k, last=k == 2 * NS - 1)
            gate_y(NCH - 1)
            residual(NCH - 1)
            v.wait_ge(m3_x, 2 * NCH)
            for u in range(UB):
                v.wait_ge(FS[f"so{u}"], 16)
            ffn_vector(v, 0, "lnf0")
            v.wait_ge(st_qz, 3)
            attention_vector(v)
            ffn_vector(v, 1, "lnf1")

        @block.tensor
        def _(pe):
            pe.sem_inc(m3_ns, NR)
            pe.sem_inc(FS["l2"], 2)
            pe.sem_inc(FS["bt"], UB)
            pe.sem_inc(FS["b2"], 2)
            pe.sem_inc(AS["t"], 6)
            pe.sem_inc(AS["o"], 2)
            pe.sem_inc(AS["ot"], 2)

            pe.wait_ge(ld_a, LOADED_A)
            for e in range(4):
                last = nc.tensor.transpose(bank[0][:, e * P:(e + 1) * P], win_n[:, e, :], ident[:])
            last.then_inc(st_tr, 1)
            for e in range(2):
                for d in range(2):
                    last = nc.tensor.transpose(bank[1][:, (2 * e + d) * P:(2 * e + d + 1) * P],
                                               wdt_n[:, e, d * P:(d + 1) * P], ident[:])
            last.then_inc(st_tr, 1)
            for d in range(2):
                nc.tensor.transpose(bank[2][:, d * P:(d + 1) * P], wbc_n[:, d * P:(d + 1) * P], ident[:])
            for d in range(2):
                last = nc.tensor.transpose(bank[2][:, (2 + d) * P:(3 + d) * P], wout_n[:, d * P:(d + 1) * P], ident[:])
            last.then_inc(st_tr, 1)
            pe.wait_ge(st_cp, 3)
            pe.wait_ge(st_zero, 8)

            for c in range(NCH):
                pe.wait_ge(m1_st, c + 1)
                for n in range(CT):
                    last = nc.tensor.transpose(bank[XB[c]][:, n * P:(n + 1) * P], D[:, c * CT + n, :], ident[:])
                last.then_inc(m1_tr, 1)
            pe.wait_ge(st_const, 3)
            pe.wait_ge(st_rope, 12)
            for g in range(2 * NG):
                last = nc.tensor.matmul(bank[4][:, g:g + 1], bqk_r[:, GH * g:GH * (g + 1), :], one1[:],
                                        start=True, stop=True)
            last.then_inc(st_bq, 1)
            pe.wait_ge(st_bqc, 1)
            pe.wait_ge(m1_xn, NCH)
            with pe.Fori(0, NCH // 2) as i:
                for s in range(2):
                    c = 2 * i + s
                    for e in range(4):
                        if e < 2:
                            dst = bank[2 * s + e]
                            pe.wait_ge(m1_xe, 2 * c + e + 1)
                        else:
                            dst = bank[4 + e - 2]
                            pe.wait_ge(m1_ze, 2 * c + e - 2 + 1)
                        nc.tensor.matmul(dst[:], winT[:, e, :], xT[:, cols(c)], start=True, stop=True).then_inc(m1_xz, 1)

            pe.wait_ge(ld_f, LOADED_F)
            nc.tensor.transpose(bank[7][:, 0:NX * NI], b1n, ident[0:NX * NI, 0:NX * NI]).then_inc(st_tr, 1)
            with pe.Fori(0, NCH // 2) as i:
                for s in range(2):
                    c = 2 * i + s
                    pe.wait_ge(m1_xc, 2 * c + 2 + 4)
                    pe.wait_ge(m1_xe, 2 * (NCH - 1 + s) + 4)
                    for e in range(2):
                        pe.wait_ge(m2_ab, 2 * c + e + 1)
                        for d in range(2):
                            last = nc.tensor.matmul(bank[2 * s + e][:], wdtT[:, e, d, :], xc[:, d, cols(c)],
                                                    start=(d == 0), stop=(d == 1))
                        last.then_inc(m2_mm, 1)
                    pe.wait_ge(m1_ze, 2 * NCH + 2)
                    pe.wait_ge(m2_hi, c + 1)
                    pe.wait_ge(m2_r, c + 1)
                    for d in range(2):
                        last = nc.tensor.matmul(bank[4 + s][:], wboT[:, d, :], xc[:, d, cols(c)],
                                                start=(d == 0), stop=(d == 1))
                    last.then_inc(m2_mm, 1)

            pe.wait_ge(m2_st, 2 * NCH)
            def spread(c, n):
                for what, (s_free, need, s_done) in enumerate(
                        ((m3_b, c * 2 * NS + 2 * n + 2, m3_bb), (m3_cs, c * NS + n + 1, m3_cb))):
                    pe.wait_ge(s_free, need)
                    col = what * NS + n
                    nc.tensor.matmul(bank[2 * what + n % 2][:], sel[:, col:col + 1].broadcast_to([P, P]),
                                     BCs[:, cols(c)], start=True, stop=True).then_inc(s_done, 1)

            def sum_state(c, n, last=False):
                if n + 2 < NS:
                    spread(c, n + 2)
                elif not last:
                    spread(c + 1, n + 2 - NS)
                for h in range(2):
                    k = 2 * n + h
                    if n == 0:
                        pe.wait_ge(m3_ya, 2 * c + h + 1)
                    pe.wait_ge(m3_hc, c * 2 * NS + k + 1 + 4)
                    nc.tensor.matmul(bank[4 + h][:], ident[:], hst[:, k % NR, :], start=(n == 0),
                                     stop=(n == NS - 1)).then_inc(m3_ns, 1)

            def project_y(c):
                pe.wait_ge(m3_y, 2 * c + 2)
                for n in range(CT):
                    for h in range(2):
                        last = nc.tensor.matmul(bank[6][:, n * C:(n + 1) * C], ybuf[:, h, n * P:(n + 1) * P],
                                                wboT[:, 2 + h, :], start=(h == 0), stop=(h == 1))
                last.then_inc(m3_o, 1)

            spread(0, 0)
            spread(0, 1)
            sum_state(0, 0)
            with pe.Fori(0, NCH - 1) as c:
                for n in range(1, NS):
                    sum_state(c, n)
                sum_state(c + 1, 0)
                project_y(c)
            for n in range(1, NS):
                sum_state(NCH - 1, n, last=n >= NS - 2)
            project_y(NCH - 1)

            pe.wait_ge(FS["so0"], 16)
            ffn_tensor(pe, 0)
            pe.wait_ge(st_qz, 3)
            attention_tensor(pe)
            ffn_tensor(pe, 1)


_OUTS = [((8, 256, 128), "float32")]


def _constants():
    import numpy as np

    P, NS, NE, NH, HD = 128, 16, 8, 16, 8
    k = np.arange(P)
    sel = ((k[:, None] % 32 == np.arange(2 * NS)[None, :]) & (k[:, None] < 96)).astype(np.float32)
    mask = np.where(k[None, :] > k[:, None], -1e30, 0.0).astype(np.float32)
    theta = 1.0 / 10000.0 ** (np.arange(0, HD, 2, dtype=np.float32) / HD)
    ang = np.arange(NH, dtype=np.float32)[:, None] * theta[None, :].astype(np.float32)
    scale = np.concatenate([np.full((NH, 1), 1.0 / np.sqrt(HD)), np.ones((NH, 1))])
    rope = np.stack([np.tile(f(ang), (2, 1)) * scale for f in (np.cos, np.sin)]).astype(np.float32)
    return {
        "c_ident": np.eye(P, dtype=np.float32), "c_sel": sel, "c_mask": mask,
        "c_rope": rope, "c_iota": np.arange(40, dtype=np.float32),
        "c_iotaP": P * np.arange(16, dtype=np.float32),
        "c_fresh": np.tile((np.arange(16) > 0).astype(np.float32), (NE, 1)),
        "c_dest": (1 + k[:, None] + P * np.arange(32)[None]).astype(np.float32),
        "c_starts": P * np.arange(41, dtype=np.float32),
        "c_lanes": np.arange(-P, 0, dtype=np.float32),
        "c_tri": (k[:, None] < k[None, :]).astype(np.float32),
    }


def kernel(**inputs):
    import numpy as _np
    import concourse.bacc as _bacc
    from concourse import mybir as _mybir
    from concourse.bass_utils import run_bass_kernel_spmd as _run

    nc = _bacc.Bacc("TRN2", target_bir_lowering=False, num_devices=1)
    arrays, tensors = {}, {}
    for name, value in {**inputs, **_constants()}.items():
        a = _np.ascontiguousarray(value)
        arrays[f"in_{name}"] = a
        tensors[name] = nc.dram_tensor(f"in_{name}", a.shape, _mybir.dt.from_np(a.dtype), kind="ExternalInput").ap()
    shape, dtype = _OUTS[0]
    out = nc.dram_tensor("out_0", shape, _mybir.dt.from_np(_np.dtype(dtype)), kind="ExternalOutput").ap()
    hybrid_block_kernel(nc, tensors, out)
    r = _run(nc, [arrays], core_ids=[0])
    return r.results[0]["out_0"]
```
